# Optimizing a Trainium2 kernel written in Bass

```python
import numpy as np
import jax
import jax.numpy as jnp

def _softmax(x, axis=-1):
    return jax.nn.softmax(x, axis=axis)

def _gelu(x):
    return jax.nn.gelu(x, approximate=True)

def _silu(x):
    return jax.nn.silu(x)

def _sigmoid(x):
    return jax.nn.sigmoid(x)

def _layernorm(x, axis=-1, eps=1e-05):
    m = jnp.mean(x, axis=axis, keepdims=True)
    v = jnp.var(x, axis=axis, keepdims=True)
    return (x - m) / jnp.sqrt(v + eps)

def _scatter_add(tgt, idx, src, axis=0):
    return tgt.at[idx].add(src)

def _segment_sum(src, seg, n):
    return jax.ops.segment_sum(src, seg, n)
kernel_name = 'mk_seq_preln_d2_jaxref_r8_55b5d8'

def setup_inputs(seed: int=0):
    np.random.seed(seed)
    _w = jnp.asarray

    def _L0_attn_setup():
        import jax, jax.numpy as jnp
        import numpy as np
        N_HEADS = 16
        HEAD_DIM = 64
        ROPE_THETA = 10000.0
        EPS = 1e-06

        def _rmsnorm(x, w):
            rms = jnp.sqrt(jnp.mean(jnp.square(x), axis=-1, keepdims=True) + EPS)
            return x / rms * w

        def _rope(x, cos, sin):
            x1, x2 = jnp.split(x, 2, axis=-1)
            return jnp.concatenate([x1 * cos - x2 * sin, x1 * sin + x2 * cos], axis=-1)
        key = jax.random.key(seed)
        ks = jax.random.split(key, 3)
        B, T, C = (2, 256, 128)
        x = jax.random.normal(ks[0], (B, T, C), dtype=jnp.float32)
        wqkv = jax.random.normal(ks[1], (3 * N_HEADS * HEAD_DIM, C), dtype=jnp.float32) * C ** (-0.5)
        wo = jax.random.normal(ks[2], (C, N_HEADS * HEAD_DIM), dtype=jnp.float32) * (N_HEADS * HEAD_DIM) ** (-0.5)
        q_norm_w = jnp.ones((HEAD_DIM,), dtype=jnp.float32)
        k_norm_w = jnp.ones((HEAD_DIM,), dtype=jnp.float32)
        return {'x': x, 'wqkv': wqkv, 'wo': wo, 'q_norm_w': q_norm_w, 'k_norm_w': k_norm_w}
    _L0_attn_in = _L0_attn_setup()

    def _L0_ffn_setup():
        import jax, jax.numpy as jnp
        import numpy as np
        DIM = 128
        DEPTH = 2
        HEADS = 8
        DIM_HEAD = 64
        WINDOW = 64
        INNER = HEADS * DIM_HEAD
        HID = int(DIM * 4 * 2 / 3)
        B, N = (2, 1024)
        QK_SCALE = 8.0

        def shift_token(t):
            t1, t2 = jnp.split(t, 2, axis=-1)
            t2 = jnp.pad(t2, ((0, 0), (1, 0), (0, 0)))[:, :-1]
            return jnp.concatenate([t1, t2], axis=-1)

        def l2norm(t):
            return t / jnp.clip(jnp.linalg.norm(t, axis=-1, keepdims=True), 1e-12)

        def rotate_half(x):
            x1, x2 = jnp.split(x, 2, axis=-1)
            return jnp.concatenate([-x2, x1], axis=-1)

        def rotary_xpos(q, k):
            n = q.shape[-2]
            half_idx = jnp.arange(0, DIM_HEAD, 2, dtype=jnp.float32)
            inv_freq = 1.0 / 10000.0 ** (half_idx / DIM_HEAD)
            t = jnp.arange(n, dtype=jnp.float32)
            freqs = t[:, None] * inv_freq[None, :]
            freqs = jnp.concatenate([freqs, freqs], axis=-1)
            base = (half_idx + 0.4 * DIM_HEAD) / (1.4 * DIM_HEAD)
            power = (t - n // 2) / float(WINDOW // 2)
            scale = base[None, :] ** power[:, None]
            scale = jnp.concatenate([scale, scale], axis=-1)
            cos, sin = (jnp.cos(freqs), jnp.sin(freqs))
            q = q * cos * scale + rotate_half(q) * sin * scale
            k = k * cos / scale + rotate_half(k) * sin / scale
            return (q, k)

        def local_attention(q, k, v):
            b, h, n, d = q.shape
            w = n // WINDOW
            bq = q.reshape(b, h, w, WINDOW, d) * QK_SCALE
            bk = k.reshape(b, h, w, WINDOW, d)
            bv = v.reshape(b, h, w, WINDOW, d)

            def look_around(t):
                p = jnp.pad(t, ((0, 0), (0, 0), (1, 0), (0, 0), (0, 0)))
                return jnp.concatenate([p[:, :, :w], p[:, :, 1:]], axis=3)
            bk, bv = (look_around(bk), look_around(bv))
            bt = jnp.arange(n).reshape(w, WINDOW)
            btp = jnp.pad(bt, ((1, 0), (0, 0)), constant_values=-1)
            btk = jnp.concatenate([btp[:w], btp[1:]], axis=1)
            sim = jnp.einsum('bhwid,bhwjd->bhwij', bq, bk)
            i = bt[:, :, None]
            j = btk[:, None, :]
            mask = (i < j) | (i > j + WINDOW) | (j == -1)
            sim = jnp.where(mask, -jnp.finfo(sim.dtype).max, sim)
            attn = jax.nn.softmax(sim, axis=-1)
            out = jnp.einsum('bhwij,bhwjd->bhwid', attn, bv)
            return out.reshape(b, h, n, d)

        def _layer(x, wqkv, qs, ksc, wo, lg, lb, w1, b1, w2, b2):
            b, n, _ = x.shape
            h = shift_token(x)
            qkv = h @ wqkv
            q, k, v = jnp.split(qkv, 3, axis=-1)
            to_heads = lambda t: t.reshape(b, n, HEADS, DIM_HEAD).transpose(0, 2, 1, 3)
            q, k, v = (to_heads(q), to_heads(k), to_heads(v))
            q = l2norm(q) * qs
            k = l2norm(k) * ksc
            q, k = rotary_xpos(q, k)
            o = local_attention(q, k, v)
            o = o.transpose(0, 2, 1, 3).reshape(b, n, INNER)
            x = x + o @ wo
            h = shift_token(x)
            mu = h.mean(-1, keepdims=True)
            var = h.var(-1, keepdims=True)
            h = (h - mu) / jnp.sqrt(var + 1e-05) * lg + lb
            h = h @ w1 + b1
            a, g = jnp.split(h, 2, axis=-1)
            h = a * jax.nn.gelu(g, approximate=False)
            x = x + h @ w2 + b2
            return x
        key = jax.random.key(seed)
        ks = jax.random.split(key, 6)
        return {'x': jax.random.normal(ks[0], (B, N, DIM), jnp.float32), 'wqkv': jax.random.normal(ks[1], (DEPTH, DIM, 3 * INNER), jnp.float32) * 0.02, 'q_scale': jnp.ones((DEPTH, DIM_HEAD), jnp.float32), 'k_scale': jnp.ones((DEPTH, DIM_HEAD), jnp.float32), 'wo': jax.random.normal(ks[2], (DEPTH, INNER, DIM), jnp.float32) * 0.02, 'ln_g': jnp.ones((DEPTH, DIM), jnp.float32), 'ln_b': jnp.zeros((DEPTH, DIM), jnp.float32), 'w1': jax.random.normal(ks[3], (DEPTH, DIM, 2 * HID), jnp.float32) * 0.02, 'b1': jnp.zeros((DEPTH, 2 * HID), jnp.float32), 'w2': jax.random.normal(ks[4], (DEPTH, HID, DIM), jnp.float32) * 0.02, 'b2': jnp.zeros((DEPTH, DIM), jnp.float32)}
    _L0_ffn_in = _L0_ffn_setup()

    def _L1_attn_setup():
        import jax, jax.numpy as jnp
        import numpy as np
        D_MODEL, H, DK, DV = (128, 16, 64, 64)
        key = jax.random.key(seed)
        ks = jax.random.split(key, 9)
        s = lambda fan_in: 1.0 / np.sqrt(fan_in)
        return {'x': jax.random.normal(ks[0], (2, 256, D_MODEL), dtype=jnp.float32), 'Wq': jax.random.uniform(ks[1], (D_MODEL, H * DK), jnp.float32, -s(D_MODEL), s(D_MODEL)), 'bq': jax.random.uniform(ks[2], (H * DK,), jnp.float32, -s(D_MODEL), s(D_MODEL)), 'Wk': jax.random.uniform(ks[3], (D_MODEL, DK), jnp.float32, -s(D_MODEL), s(D_MODEL)), 'bk': jax.random.uniform(ks[4], (DK,), jnp.float32, -s(D_MODEL), s(D_MODEL)), 'Wv': jax.random.uniform(ks[5], (D_MODEL, DV), jnp.float32, -s(D_MODEL), s(D_MODEL)), 'bv': jax.random.uniform(ks[6], (DV,), jnp.float32, -s(D_MODEL), s(D_MODEL)), 'Wo': jax.random.uniform(ks[7], (H * DV, D_MODEL), jnp.float32, -s(H * DV), s(H * DV)), 'bo': jax.random.uniform(ks[8], (D_MODEL,), jnp.float32, -s(H * DV), s(H * DV))}
    _L1_attn_in = _L1_attn_setup()

    def _L1_ffn_setup():
        import jax, jax.numpy as jnp
        import numpy as np
        D_MODEL = 128
        D_FF = 512
        NUM_EXPERTS = 8
        TOP_K = 2
        B, S = (4, 512)
        key = jax.random.key(seed)
        ks = jax.random.split(key, 7)
        s_dm = 1.0 / np.sqrt(D_MODEL)
        s_ff = 1.0 / np.sqrt(D_FF)
        return {'x': jax.random.normal(ks[0], (B, S, D_MODEL), jnp.float32), 'router_w': jax.random.normal(ks[1], (D_MODEL, NUM_EXPERTS), jnp.float32) * s_dm, 'router_b': jnp.zeros((NUM_EXPERTS,), jnp.float32), 'w1': jax.random.normal(ks[2], (NUM_EXPERTS, D_MODEL, D_FF), jnp.float32) * s_dm, 'b1': jnp.zeros((NUM_EXPERTS, D_FF), jnp.float32), 'w2': jax.random.normal(ks[3], (NUM_EXPERTS, D_FF, D_MODEL), jnp.float32) * s_ff, 'b2': jnp.zeros((NUM_EXPERTS, D_MODEL), jnp.float32)}
    _L1_ffn_in = _L1_ffn_setup()
    _d = {'L0_attn_x': _L0_attn_in['x'], 'L0_attn_wqkv': _L0_attn_in['wqkv'], 'L0_attn_wo': _L0_attn_in['wo'], 'L0_attn_q_norm_w': _L0_attn_in['q_norm_w'], 'L0_attn_k_norm_w': _L0_attn_in['k_norm_w'], 'L0_ffn_wqkv': _L0_ffn_in['wqkv'], 'L0_ffn_q_scale': _L0_ffn_in['q_scale'], 'L0_ffn_k_scale': _L0_ffn_in['k_scale'], 'L0_ffn_wo': _L0_ffn_in['wo'], 'L0_ffn_ln_g': _L0_ffn_in['ln_g'], 'L0_ffn_ln_b': _L0_ffn_in['ln_b'], 'L0_ffn_w1': _L0_ffn_in['w1'], 'L0_ffn_b1': _L0_ffn_in['b1'], 'L0_ffn_w2': _L0_ffn_in['w2'], 'L0_ffn_b2': _L0_ffn_in['b2'], 'L1_attn_Wq': _L1_attn_in['Wq'], 'L1_attn_bq': _L1_attn_in['bq'], 'L1_attn_Wk': _L1_attn_in['Wk'], 'L1_attn_bk': _L1_attn_in['bk'], 'L1_attn_Wv': _L1_attn_in['Wv'], 'L1_attn_bv': _L1_attn_in['bv'], 'L1_attn_Wo': _L1_attn_in['Wo'], 'L1_attn_bo': _L1_attn_in['bo'], 'L1_ffn_router_w': _L1_ffn_in['router_w'], 'L1_ffn_router_b': _L1_ffn_in['router_b'], 'L1_ffn_w1': _L1_ffn_in['w1'], 'L1_ffn_b1': _L1_ffn_in['b1'], 'L1_ffn_w2': _L1_ffn_in['w2'], 'L1_ffn_b2': _L1_ffn_in['b2']}
    _x0 = _d['L0_attn_x']
    _d['L0_attn_x'] = jax.random.normal(jax.random.fold_in(jax.random.key(seed), 1), (1, 2048, 128), dtype=_x0.dtype)
    del _x0
    return _d

def reference(L0_attn_x, L0_attn_wqkv, L0_attn_wo, L0_attn_q_norm_w, L0_attn_k_norm_w, L0_ffn_wqkv, L0_ffn_q_scale, L0_ffn_k_scale, L0_ffn_wo, L0_ffn_ln_g, L0_ffn_ln_b, L0_ffn_w1, L0_ffn_b1, L0_ffn_w2, L0_ffn_b2, L1_attn_Wq, L1_attn_bq, L1_attn_Wk, L1_attn_bk, L1_attn_Wv, L1_attn_bv, L1_attn_Wo, L1_attn_bo, L1_ffn_router_w, L1_ffn_router_b, L1_ffn_w1, L1_ffn_b1, L1_ffn_w2, L1_ffn_b2):

    def _L0_attn_ref(x, wqkv, wo, q_norm_w, k_norm_w):
        import jax, jax.numpy as jnp
        import numpy as np
        N_HEADS = 16
        HEAD_DIM = 64
        ROPE_THETA = 10000.0
        EPS = 1e-06

        def _rmsnorm(x, w):
            rms = jnp.sqrt(jnp.mean(jnp.square(x), axis=-1, keepdims=True) + EPS)
            return x / rms * w

        def _rope(x, cos, sin):
            x1, x2 = jnp.split(x, 2, axis=-1)
            return jnp.concatenate([x1 * cos - x2 * sin, x1 * sin + x2 * cos], axis=-1)
        B, T, C = x.shape
        H, D = (N_HEADS, HEAD_DIM)
        qkv = jnp.einsum('btc,oc->bto', x, wqkv)
        q, k, v = jnp.split(qkv, 3, axis=-1)

        def to_heads(t):
            return t.reshape(B, T, H, D).transpose(0, 2, 1, 3)
        q, k, v = (to_heads(q), to_heads(k), to_heads(v))
        q = _rmsnorm(q, q_norm_w)
        k = _rmsnorm(k, k_norm_w)
        inv_freq = 1.0 / ROPE_THETA ** (jnp.arange(0, D, 2, dtype=jnp.float32) / D)
        freqs = jnp.arange(T, dtype=jnp.float32)[:, None] * inv_freq
        cos, sin = (jnp.cos(freqs), jnp.sin(freqs))
        q = _rope(q, cos, sin)
        k = _rope(k, cos, sin)
        scale = D ** (-0.5)
        attn = jnp.einsum('bhtd,bhsd->bhts', q, k) * scale
        causal = jnp.tril(jnp.ones((T, T), dtype=bool))
        attn = jnp.where(causal, attn, -jnp.inf)
        attn = jax.nn.softmax(attn.astype(jnp.float32), axis=-1).astype(q.dtype)
        out = jnp.einsum('bhts,bhsd->bhtd', attn, v)
        out = out.transpose(0, 2, 1, 3).reshape(B, T, H * D)
        return jnp.einsum('bte,ce->btc', out, wo)

    def _L0_ffn_ref(x, wqkv, q_scale, k_scale, wo, ln_g, ln_b, w1, b1, w2, b2):
        import jax, jax.numpy as jnp
        import numpy as np
        DIM = 128
        DEPTH = 2
        HEADS = 8
        DIM_HEAD = 64
        WINDOW = 64
        INNER = HEADS * DIM_HEAD
        HID = int(DIM * 4 * 2 / 3)
        B, N = (2, 1024)
        QK_SCALE = 8.0

        def shift_token(t):
            t1, t2 = jnp.split(t, 2, axis=-1)
            t2 = jnp.pad(t2, ((0, 0), (1, 0), (0, 0)))[:, :-1]
            return jnp.concatenate([t1, t2], axis=-1)

        def l2norm(t):
            return t / jnp.clip(jnp.linalg.norm(t, axis=-1, keepdims=True), 1e-12)

        def rotate_half(x):
            x1, x2 = jnp.split(x, 2, axis=-1)
            return jnp.concatenate([-x2, x1], axis=-1)

        def rotary_xpos(q, k):
            n = q.shape[-2]
            half_idx = jnp.arange(0, DIM_HEAD, 2, dtype=jnp.float32)
            inv_freq = 1.0 / 10000.0 ** (half_idx / DIM_HEAD)
            t = jnp.arange(n, dtype=jnp.float32)
            freqs = t[:, None] * inv_freq[None, :]
            freqs = jnp.concatenate([freqs, freqs], axis=-1)
            base = (half_idx + 0.4 * DIM_HEAD) / (1.4 * DIM_HEAD)
            power = (t - n // 2) / float(WINDOW // 2)
            scale = base[None, :] ** power[:, None]
            scale = jnp.concatenate([scale, scale], axis=-1)
            cos, sin = (jnp.cos(freqs), jnp.sin(freqs))
            q = q * cos * scale + rotate_half(q) * sin * scale
            k = k * cos / scale + rotate_half(k) * sin / scale
            return (q, k)

        def local_attention(q, k, v):
            b, h, n, d = q.shape
            w = n // WINDOW
            bq = q.reshape(b, h, w, WINDOW, d) * QK_SCALE
            bk = k.reshape(b, h, w, WINDOW, d)
            bv = v.reshape(b, h, w, WINDOW, d)

            def look_around(t):
                p = jnp.pad(t, ((0, 0), (0, 0), (1, 0), (0, 0), (0, 0)))
                return jnp.concatenate([p[:, :, :w], p[:, :, 1:]], axis=3)
            bk, bv = (look_around(bk), look_around(bv))
            bt = jnp.arange(n).reshape(w, WINDOW)
            btp = jnp.pad(bt, ((1, 0), (0, 0)), constant_values=-1)
            btk = jnp.concatenate([btp[:w], btp[1:]], axis=1)
            sim = jnp.einsum('bhwid,bhwjd->bhwij', bq, bk)
            i = bt[:, :, None]
            j = btk[:, None, :]
            mask = (i < j) | (i > j + WINDOW) | (j == -1)
            sim = jnp.where(mask, -jnp.finfo(sim.dtype).max, sim)
            attn = jax.nn.softmax(sim, axis=-1)
            out = jnp.einsum('bhwij,bhwjd->bhwid', attn, bv)
            return out.reshape(b, h, n, d)

        def _layer(x, wqkv, qs, ksc, wo, lg, lb, w1, b1, w2, b2):
            b, n, _ = x.shape
            h = shift_token(x)
            qkv = h @ wqkv
            q, k, v = jnp.split(qkv, 3, axis=-1)
            to_heads = lambda t: t.reshape(b, n, HEADS, DIM_HEAD).transpose(0, 2, 1, 3)
            q, k, v = (to_heads(q), to_heads(k), to_heads(v))
            q = l2norm(q) * qs
            k = l2norm(k) * ksc
            q, k = rotary_xpos(q, k)
            o = local_attention(q, k, v)
            o = o.transpose(0, 2, 1, 3).reshape(b, n, INNER)
            x = x + o @ wo
            h = shift_token(x)
            mu = h.mean(-1, keepdims=True)
            var = h.var(-1, keepdims=True)
            h = (h - mu) / jnp.sqrt(var + 1e-05) * lg + lb
            h = h @ w1 + b1
            a, g = jnp.split(h, 2, axis=-1)
            h = a * jax.nn.gelu(g, approximate=False)
            x = x + h @ w2 + b2
            return x
        for l in range(DEPTH):
            x = _layer(x, wqkv[l], q_scale[l], k_scale[l], wo[l], ln_g[l], ln_b[l], w1[l], b1[l], w2[l], b2[l])
        return x

    def _L1_attn_ref(x, Wq, bq, Wk, bk, Wv, bv, Wo, bo):
        import jax, jax.numpy as jnp
        import numpy as np
        D_MODEL, H, DK, DV = (128, 16, 64, 64)
        B, S, _ = x.shape
        q = (x @ Wq + bq).reshape(B, S, H, DK)
        k = x @ Wk + bk
        v = x @ Wv + bv
        scores = jnp.einsum('bshd,btd->bhst', q, k) / np.sqrt(DK).astype(x.dtype)
        w = jax.nn.softmax(scores, axis=-1)
        out = jnp.einsum('bhst,btd->bshd', w, v).reshape(B, S, H * DV)
        return out @ Wo + bo

    def _L1_ffn_ref(x, router_w, router_b, w1, b1, w2, b2):
        import jax, jax.numpy as jnp
        import numpy as np
        D_MODEL = 128
        D_FF = 512
        NUM_EXPERTS = 8
        TOP_K = 2
        B, S = (4, 512)
        Bx, Sx, D = x.shape
        xf = x.reshape(-1, D)
        logits = xf @ router_w + router_b
        top_w, sel = jax.lax.top_k(logits, TOP_K)
        gates = jax.nn.softmax(top_w, axis=-1)

        def body(i, acc):
            h = jax.nn.gelu(xf @ w1[i] + b1[i], approximate=False)
            out_i = h @ w2[i] + b2[i]
            gate_i = jnp.sum(gates * (sel == i), axis=-1, keepdims=True)
            return acc + out_i * gate_i
        out = jax.lax.fori_loop(0, NUM_EXPERTS, body, jnp.zeros_like(xf))
        return out.reshape(Bx, Sx, D)
    x = L0_attn_x
    x = x + _L0_attn_ref(_layernorm(x, axis=-1), L0_attn_wqkv, L0_attn_wo, L0_attn_q_norm_w, L0_attn_k_norm_w)
    x = x + _L0_ffn_ref(_layernorm(x, axis=-1), L0_ffn_wqkv, L0_ffn_q_scale, L0_ffn_k_scale, L0_ffn_wo, L0_ffn_ln_g, L0_ffn_ln_b, L0_ffn_w1, L0_ffn_b1, L0_ffn_w2, L0_ffn_b2)
    x = x + _L1_attn_ref(_layernorm(x, axis=-1), L1_attn_Wq, L1_attn_bq, L1_attn_Wk, L1_attn_bk, L1_attn_Wv, L1_attn_bv, L1_attn_Wo, L1_attn_bo)
    x = x + _L1_ffn_ref(_layernorm(x, axis=-1), L1_ffn_router_w, L1_ffn_router_b, L1_ffn_w1, L1_ffn_b1, L1_ffn_w2, L1_ffn_b2)
    return x

_drawn_inputs = setup_inputs


def setup_inputs(seed=0):
    import zlib

    import numpy as np

    out = dict(_drawn_inputs(seed))
    spreads = {'L0_attn_q_norm_w': (1.0, 0.2),
     'L0_attn_k_norm_w': (1.0, 0.2),
     'L0_ffn_q_scale': (1.0, 0.6),
     'L0_ffn_k_scale': (1.0, 0.6),
     'L0_ffn_ln_g': (1.0, 0.6),
     'L0_ffn_ln_b': (0.0, 0.8),
     'L0_ffn_b1': (0.0, 0.587),
     'L0_ffn_b2': (0.0, 0.1),
     'L1_ffn_router_b': (0.0, 0.1),
     'L1_ffn_b1': (0.0, 0.32),
     'L1_ffn_b2': (0.0, 0.291)}
    factors = {'L0_ffn_w1': 2.992,
     'L0_ffn_w2': 3.376,
     'L1_attn_Wq': 4.447,
     'L1_attn_bq': 8.0,
     'L1_attn_Wk': 4.115,
     'L1_attn_bk': 64.0,
     'L1_attn_bo': 3.468,
     'L1_attn_bv': 2.985}
    for name, (base, spread) in spreads.items():
        noise = np.random.default_rng([zlib.crc32(name.encode()), seed]).standard_normal(out[name].shape)
        drawn = base * np.exp(spread * noise) if base else spread * noise
        out[name] = jnp.asarray(drawn.astype(out[name].dtype))
    for name, factor in factors.items():
        out[name] = (out[name] * factor).astype(out[name].dtype)
    return out
```

```python
from contextlib import ExitStack

import concourse.bass as bass
from concourse import mybir
import numpy as np

F32 = mybir.dt.float32
F16 = mybir.dt.float16
BF16 = mybir.dt.bfloat16
U32 = mybir.dt.uint32
ACT = mybir.ActivationFunctionType
ALU = mybir.AluOpType
AX_X = mybir.AxisListType.X

P = 128
T = 2048
NT = T // P
C = 128
HEADS = 16
HD = 64
QG = 4
GROUPS = NT // QG
CHUNK = 4
LN_EPS = 1e-5
RMS_EPS = 1e-6

TURN_BANK = 4
OUT_BANK = 6
MAKE_BANK = 7


class HeadPlan:

    def __init__(self, causal):
        self.causal = causal
        self.blocks = []
        for j in range(NT):
            for s in range(2):
                kts = [k for k in range(j + 1 if causal else NT) if k % 2 == s]
                if kts:
                    self.blocks.append((j, s, kts))
        self.nb = len(self.blocks)
        self.fills = []
        self.before = []
        count, f = [0, 0], 0
        for _, _, kts in self.blocks:
            self.before.append(tuple(count))
            mine = []
            for c in range(0, len(kts), CHUNK):
                mine.append((f % 2, count[f % 2], kts[c:c + CHUNK], c))
                count[f % 2] += 1
                f += 1
            self.fills.append(mine)
        self.before.append(tuple(count))
        self.per_head = tuple(count)
        self.last = [max(b for b in range(self.nb) if self.blocks[b][0] // QG == g) for g in range(GROUPS)]

    def due(self, k):
        found = []
        for g in range(-1, GROUPS):
            since = k - (-1 if g < 0 else self.last[g])
            if 1 <= since <= 8:
                found.append((g, since))
        return found

    def value_pieces(self, g):
        n = QG * (g % GROUPS + 1) if self.causal else NT
        order = [x for k in range(0, n, 2) for x in ((0, k), (1, k + 1))]
        m = (len(order) // 2 + 3) // 4 * 2
        return [order[i * m:(i + 1) * m] for i in range(4)]


def make_identity(pool, tile, zeroed, done):
    pool.memset(tile[:], 0.0).then_inc(zeroed, 1)
    pool.wait_ge(zeroed, 1)
    pool.affine_select(out=tile[:], in_=tile[:], compare_op=ALU.not_equal, fill=1.0, base=0,
                       pattern=[[-1, P]], channel_multiplier=1).then_inc(done, 1)


class Sems:

    def __init__(self, nc, ctx, stage):
        self.nc, self.stage, self.held = nc, stage, []
        ctx.callback(self.free)

    def __call__(self, name):
        self.held.append(self.nc.alloc_semaphore(name=f"{self.stage}_{name}"))
        return self.held[-1]

    def free(self):
        self.nc.clear_and_free_semaphores(self.held)
        self.nc.all_engine_barrier()


def layernorm_stage(nc, ps, x, xn, xnT, ident, stage, shift_rows=None):
    CH = 4
    with ExitStack() as ctx:
        sem = Sems(nc, ctx, stage)
        stats = ctx.enter_context(nc.sbuf_tensor(f"{stage}_stats", [P, NT, 6], F32))
        mv = ctx.enter_context(nc.sbuf_tensor(f"{stage}_mv", [P, NT, 2], F32))
        veps = ctx.enter_context(nc.sbuf_tensor(f"{stage}_veps", [P, NT], F32))
        rstd = ctx.enter_context(nc.sbuf_tensor(f"{stage}_rstd", [P, NT], F32))
        minus_half = ctx.enter_context(nc.sbuf_tensor(f"{stage}_mh", [P, 1], F32))
        stats_done, mv_done, veps_done = sem("stats_done"), sem("mv_done"), sem("veps_done")
        rstd_done, const_done, xn_done = sem("rstd_done"), sem("const_done"), sem("xn_done")
        turned, emptied = sem("turned"), sem("emptied")
        block = ctx.enter_context(nc.Block())

        @block.vector
        def _(dve):
            for t in range(NT):
                nc.vector.bn_stats(stats[:, t, :], x[:, t, :]).then_inc(stats_done, 1)
            for t in range(NT):
                dve.wait_ge(stats_done, t + 1)
                nc.vector.bn_aggr(mv[:, t, :], stats[:, t, :]).then_inc(mv_done, 1)
            for t in range(NT):
                if t % CH == 0:
                    dve.wait_ge(rstd_done, t // CH + 1)
                    dve.wait_ge(mv_done, NT)
                nc.vector.tensor_scalar(xn[:, t, :], x[:, t, :], mv[:, t, 0:1], rstd[:, t:t + 1],
                                        ALU.subtract, ALU.mult).then_inc(xn_done, 1)

        @block.gpsimd
        def _(pool):
            pool.memset(minus_half[:], -0.5).then_inc(const_done, 1)
            pool.wait_ge(const_done, 1)
            for k in range(NT // CH):
                pool.wait_ge(mv_done, CH * k + CH)
                pool.tensor_scalar(veps[:, CH * k:CH * k + CH], mv[:, CH * k:CH * k + CH, 1], LN_EPS, 0.0,
                                   ALU.add, ALU.add).then_inc(veps_done, 1)
                pool.wait_ge(veps_done, k + 1)
                pool.tensor_tensor(rstd[:, CH * k:CH * k + CH], veps[:, CH * k:CH * k + CH],
                                   minus_half[:].to_broadcast([P, CH]), ALU.pow).then_inc(rstd_done, 1)

        @block.tensor
        def _(pe):
            for k in range(NT // CH):
                pe.wait_ge(xn_done, CH * k + CH)
                for i in range(CH):
                    mm = nc.tensor.transpose(ps[:, k, i * P:(i + 1) * P], xn[:, CH * k + i, :], ident[:])
                mm.then_inc(turned, 1)

        @block.scalar
        def _(act):
            for k in range(NT // CH):
                act.wait_ge(turned, k + 1)
                nc.scalar.activation(xnT[:, k * CH * P:(k + 1) * CH * P], ps[:, k, :], ACT.Copy)\
                    .then_inc(emptied, 1)
            act.wait_ge(emptied, NT // CH)


def attention_stage(nc, plan, stage, ps, x, xnT, const, make):
    causal = plan.causal
    NB = plan.nb
    blocks = plan.blocks
    ident, identb, ident16, mask = const["ident"], const["identb"], const["ident16"], const["mask"]
    WoT = make["WoT"]
    FILLS = 14 if causal else 4
    FIRST_PROJ = 4
    SQUARE_STEP, SUM_STEP, TWIST_STEP, FIRST_TURN = 12, 14, 20, 23
    PROJ_GAP = 1 if causal else 4

    with ExitStack() as ctx:
        sem = Sems(nc, ctx, stage)

        def sb(name, shape, dt):
            return ctx.enter_context(nc.sbuf_tensor(f"{stage}_{name}", shape, dt))

        probs = sb("probs", [P, 2, CHUNK * 2 * P], F32)
        pT = sb("pT", [P, 2, NT, QG * P], F32)
        o_sb = sb("o_sb", [P, QG * P], F32)
        wo_h = [sb(f"wo_h{i}", [P, C], F32) for i in range(2)]
        negm = sb("negm", [P, 2, QG, 2], F32)
        sums = sb("sums", [P, 2, QG, 2], F32)
        joint = sb("joint", [P, QG], F32)
        diff = sb("diff", [P, QG, 2], F32)
        alpha = sb("alpha", [P, QG, 2], F32)
        part = sb("part", [P, QG, 2], F32)
        den = sb("den", [P, QG], F32)
        rden = sb("rden", [P, QG], F32)
        wgt = sb("wgt", [P, QG, 2], F32)
        nought = sb("nought", [P, 8], F32)
        q = [sb(f"q{i}", [P, T], F16) for i in range(2)]
        if causal:
            kA = [sb(f"kA{i}", [P, T], F16) for i in range(2)]
            kB = [sb(f"kB{i}", [P, T], F16) for i in range(2)]
            raw = [sb(f"raw{i}", [P, 3, NT, HD], F32) for i in range(2)]
            V = [raw[i][:, 2] for i in range(2)]
            sq = sb("sq", [P, 2, NT, HD], F32)
            rot = sb("rot", [P, 2, NT, HD], F32)
            ss = sb("ss", [P, 2 * NT], F32)
            rms = sb("rms", [P, 2 * NT], F32)
            rinv = sb("rinv", [P, 2 * NT], F32)
            halves = sb("halves", [P, NT, 5 * HD], F16)
            minus_half = const["minus_half"]
        else:
            kA, kB, V = [make["kA"]] * 2, [make["kB"]] * 2, [make["V"]] * 2
            wq_h = [sb(f"wq_h{i}", [P, 2, HD], F32) for i in range(2)]
            bq_h = [sb(f"bq_h{i}", [P, 1], F32) for i in range(2)]
            qf = sb("qf", [P, 512], F32)

        cleared = sem("cleared")
        scores_ready = sem("scores_ready")
        negm_ready = sem("negm_ready")
        probs_ready = sem("probs_ready")
        turned = [sem("turned0"), sem("turned1")]
        emptied = [sem("emptied0"), sem("emptied1")]
        values_ready = sem("values_ready")
        o_ready = sem("o_ready")
        y_ready = sem("y_ready")
        y_added = sem("y_added")
        joint_ready, diff_ready, alpha_ready = sem("joint_ready"), sem("diff_ready"), sem("alpha_ready")
        part_ready, den_ready, rden_ready, wgt_ready = (sem(n) for n in ("part_ready", "den_ready", "rden_ready", "wgt_ready"))
        made = sem("made")
        made_out = sem("made_out")
        wo_staged = sem("wo_staged")
        if causal:
            sq_ready, ss_ready, rms_ready = sem("sq_ready"), sem("ss_ready"), sem("rms_ready")
            roped, rinv_ready = sem("roped"), sem("rinv_ready")
            scaled, hi_ready, halves_ready = sem("scaled"), sem("hi_ready"), sem("halves_ready")
        else:
            wq_staged, bq_staged = sem("wq_staged"), sem("bq_staged")
            q_hi, q_ready = sem("q_hi"), sem("q_ready")

        def B(i, p, c):
            return i * (2 * NB) + (p * NB + c)

        def G(i, p, g):
            return i * (2 * GROUPS) + (p * GROUPS + g + 1)

        def F(bank, i, p, n):
            return i * (2 * plan.per_head[bank]) + (p * plan.per_head[bank] + n)

        def H(i, p, per, c):
            return i * (2 * per) + (p * per + c)

        def k_tiles(t, kts):
            return t[:].rearrange("p (k n) -> p k n", n=P)[:, kts[0]:kts[-1] + 1:2, :]

        block = ctx.enter_context(nc.Block())

        @block.tensor
        def _(pe):
            def scores(i, p, b):
                slot = (p * NB + b) % 2
                own = p if b < NB else 1 - p
                j, s, kts = blocks[b % NB]
                for c in range(0, len(kts), CHUNK):
                    some = kts[c:c + CHUNK]
                    out = ps[:, 2 * slot + c // CHUNK, 0:len(some) * P]
                    diagonal = causal and j in some
                    qt = q[own][:, j * P:(j + 1) * P]
                    nc.tensor.matmul(out, qt, k_tiles(kA[own], some), start=True, stop=False)
                    mm = nc.tensor.matmul(out, qt, k_tiles(kB[own], some), start=False, stop=not diagonal)
                    if diagonal:
                        at = some.index(j) * P
                        mm = nc.tensor.matmul(out[:, at:at + P], identb[:], mask[:], start=False, stop=True)
                mm.then_inc(scores_ready, 1)

            def turn(i, p, b):
                slot = (p * NB + b) % 2
                for bank, n, kts, off in plan.fills[b]:
                    pe.wait_ge(emptied[bank], F(bank, i, p, n + 1))
                    for m in range(len(kts)):
                        mm = nc.tensor.transpose(ps[:, TURN_BANK + bank, m * P:(m + 1) * P],
                                                 probs[:, slot, (off + m) * P:(off + m + 1) * P], ident[:])
                    mm.then_inc(turned[bank], 1)

            def values(i, p, g, piece):
                own = p if g >= 0 else 1 - p
                slot = (g + 1) % 2
                if piece == 0:
                    pe.wait_ge(y_added, G(i, p, g) * 2 + 2)
                    done = plan.before[plan.last[g] + 1] if g >= 0 else (0, 0)
                    for bank in range(2):
                        pe.wait_ge(emptied[bank], F(bank, i, p, done[bank] + 1))
                pieces = plan.value_pieces(g)
                seen = [(h, k) for pc in pieces[:piece] for h, k in pc]
                left = [(h, k) for pc in pieces[piece + 1:] for h, k in pc]
                for n, (half, k) in enumerate(pieces[piece]):
                    first = max(0, k - QG * (g % GROUPS)) if causal else 0
                    mm = nc.tensor.matmul(
                        ps[half * HD:(half + 1) * HD, OUT_BANK, first * P:QG * P],
                        V[own][:, k, :], pT[:, slot, k, first * P:QG * P],
                        start=not any(h == half for h, _ in seen + pieces[piece][:n]),
                        stop=not any(h == half for h, _ in pieces[piece][n + 1:] + left))
                if not left:
                    if pieces[piece]:
                        mm.then_inc(values_ready, 1)

            def project(i, p, g, half):
                own = p if g >= 0 else 1 - p
                if half == 0:
                    pe.wait_ge(o_ready, G(i, p, g) + 1)
                    pe.wait_ge(wo_staged, H(i, p, 1, 1 if g >= 0 else 0) + 1)
                else:
                    pe.wait_ge(y_added, G(i, p, g) * 2 + 3)
                rows = slice(half * HD, (half + 1) * HD)
                for jj in range(QG):
                    if causal and g == 0 and jj == 0 and half == 1:
                        continue
                    mm = nc.tensor.matmul(ps[:, OUT_BANK, jj * P:(jj + 1) * P], o_sb[rows, jj * P:(jj + 1) * P],
                                          wo_h[own][rows, :], start=True, stop=True)
                mm.then_inc(y_ready, 1)

            def trail(i, p, k):
                for g, since in plan.due(k):
                    if since <= 4:
                        values(i, p, g, since - 1)
                    if since == 5:
                        project(i, p, g, 0)
                    if since == 6:
                        project(i, p, g, 1)

            def make_fill(i, p, f):
                pe.wait_ge(made_out, H(i, p, FILLS, f) + 1)
                if causal and f < 8:
                    for a in range(2):
                        t = 2 * f + a
                        mm = nc.tensor.matmul(ps[:, MAKE_BANK, a * 256:a * 256 + 3 * HD],
                                              xnT[:, t * P:(t + 1) * P],
                                              make["WT"][:, :, i * 2 + p, :], start=True, stop=True)
                elif causal:
                    if f == 8:
                        pe.wait_ge(halves_ready, H(i, p, 1, 1))
                    what, half = (f - 8) % 3, (f - 8) // 3
                    off = (0, 2 * HD, 3 * HD)[what]
                    bank16 = ps[:, MAKE_BANK, :].bitcast(F16)
                    for m in range(8):
                        mm = nc.tensor.transpose(bank16[:, m * P:(m + 1) * P],
                                                 halves[:, 8 * half + m, off:off + P], ident16[:])
                else:
                    if f == 0:
                        pe.wait_ge(wq_staged, H(i, p, 1, 1) * 2)
                    mm = nc.tensor.matmul(ps[:, MAKE_BANK, :], wq_h[p][:].rearrange("p a e -> p (a e)"),
                                          xnT[:, f * 512:(f + 1) * 512], start=True, stop=True)
                mm.then_inc(made, 1)

            def fills_due(k):
                if causal:
                    return [k - FIRST_PROJ] if 0 <= k - FIRST_PROJ < 8 else \
                        [k - FIRST_TURN + 8] if 0 <= k - FIRST_TURN < 6 else []
                return [(k - FIRST_PROJ) // PROJ_GAP] if (k - FIRST_PROJ) % PROJ_GAP == 0 and 0 <= k - FIRST_PROJ < 4 * PROJ_GAP else []

            def operands_ready(i, p):
                if causal:
                    pe.wait_ge(made_out, H(i, p, FILLS, FILLS) + 1)
                else:
                    pe.wait_ge(q_ready, H(i, p, FILLS, FILLS))

            pe.wait_ge(cleared, 1)
            for bank in range(2):
                nc.tensor.transpose(ps[:, TURN_BANK + bank, 0:P], ident[:], ident[:]).then_inc(turned[bank], 1)
            for f in range(FILLS):
                make_fill(0, 0, f)
            operands_ready(0, 0)
            scores(0, 0, 0)
            scores(0, 0, 1)
            with pe.Fori(0, HEADS // 2) as i:
                for p in range(2):
                    for k in range(NB):
                        pe.wait_ge(probs_ready, B(i, p, k) + 2)
                        if k == NB - 2:
                            operands_ready(*((i, 1) if p == 0 else (i + 1, 0)))
                        scores(i, p, k + 2)
                        turn(i, p, k)
                        trail(i, p, k)
                        for f in fills_due(k):
                            make_fill(*((i, 1) if p == 0 else (i + 1, 0)), f)
            for k in range(6):
                for g, since in plan.due(k):
                    if g < 0:
                        if since <= 4:
                            values(HEADS // 2, 0, -1, since - 1)
                        elif since <= 6:
                            project(HEADS // 2, 0, -1, since - 5)

        @block.vector
        def _(dve):
            def maximum(i, p, b):
                slot = (p * NB + b) % 2
                j, s, kts = blocks[b % NB]
                g, jj = j // QG, j % QG
                if causal and j == 0:
                    nc.vector.memset(negm[:, 1, 0, 1:2], 1e30)
                dve.wait_ge(scores_ready, B(i, p, b) + 1)
                nc.vector.tensor_reduce(negm[:, (g + 1) % 2, jj, s:s + 1],
                                        ps[:, 2 * slot:2 * slot + 2, :].rearrange("p a n -> p (a n)")[:, 0:len(kts) * P],
                                        AX_X, ALU.max, negate=True).then_inc(negm_ready, 1)

            def empty(i, p, b):
                j = blocks[b][0]
                for bank, n, kts, _ in plan.fills[b]:
                    if bank == 0:
                        dve.wait_ge(turned[0], F(0, i, p, n + 1) + 1)
                        nc.vector.tensor_copy(
                            pT[:, (j // QG + 1) % 2, kts[0]:kts[-1] + 1:2, j % QG * P:(j % QG + 1) * P],
                            ps[:, TURN_BANK, 0:len(kts) * P].rearrange("p (k n) -> p k n", n=P)).then_inc(emptied[0], 1)

            def meet_first(i, p, g):
                slot = (g + 1) % 2
                last = plan.last[g] if g >= 0 else -1
                dve.wait_ge(negm_ready, B(i, p, last + 1) if g >= 0 else B(i, p, 2))
                nc.vector.tensor_tensor(joint[:], negm[:, slot, :, 0], negm[:, slot, :, 1], ALU.min).then_inc(joint_ready, 1)
                dve.wait_ge(joint_ready, G(i, p, g) + 1)
                nc.vector.tensor_tensor(diff[:], joint[:].unsqueeze(2).to_broadcast([P, QG, 2]), negm[:, slot], ALU.subtract)\
                    .then_inc(diff_ready, 1)

            def meet_second(i, p, g):
                slot = (g + 1) % 2
                dve.wait_ge(alpha_ready, G(i, p, g) + 1)
                nc.vector.tensor_tensor(part[:], alpha[:], sums[:, slot], ALU.mult).then_inc(part_ready, 1)
                dve.wait_ge(part_ready, G(i, p, g) + 1)
                nc.vector.tensor_reduce(den[:], part[:], AX_X, ALU.add).then_inc(den_ready, 1)
                dve.wait_ge(den_ready, G(i, p, g) + 1)
                nc.vector.reciprocal(rden[:], den[:]).then_inc(rden_ready, 1)
                dve.wait_ge(rden_ready, G(i, p, g) + 1)
                nc.vector.tensor_tensor(wgt[:], alpha[:], rden[:].unsqueeze(2).to_broadcast([P, QG, 2]), ALU.mult)\
                    .then_inc(wgt_ready, 1)

            def add(i, p, g, half):
                dve.wait_ge(y_ready, G(i, p, g) * 2 + half + 1)
                dve.wait_ge(wgt_ready, G(i, p, g) + 1)
                dve.wait_ge(y_added, G(i, p, g) * 2 + half + 2)
                for jj in range(QG):
                    if causal and g == 0 and jj == 0 and half == 1:
                        continue
                    t = QG * (g % GROUPS) + jj
                    op = nc.vector.scalar_tensor_tensor(out=x[:, t, :], in0=ps[:, OUT_BANK, jj * P:(jj + 1) * P],
                                                        scalar=wgt[:, jj, half:half + 1], in1=x[:, t, :],
                                                        op0=ALU.mult, op1=ALU.add)
                op.then_inc(y_added, 1)

            def square_sums(i, p):
                dve.wait_ge(sq_ready, H(i, p, 1, 1))
                nc.vector.tensor_reduce(ss[:].rearrange("p (a t) -> p a t", a=2), sq[:], AX_X, ALU.add).then_inc(ss_ready, 1)

            def split(i, p, stepno):
                flat = rot[:].rearrange("p a t e -> p (a t) e")
                if stepno == 0:
                    dve.wait_ge(rinv_ready, H(i, p, 1, 1))
                    nc.vector.tensor_tensor(flat, flat, rinv[:].unsqueeze(2).to_broadcast([P, 2 * NT, HD]), ALU.mult)\
                        .then_inc(scaled, 1)
                if stepno == 1:
                    dve.wait_ge(scaled, H(i, p, 1, 1))
                    dve.wait_ge(made, H(i, p, FILLS, 8))
                    nc.vector.tensor_copy(halves[:, :, 0:HD], rot[:, 0])
                    nc.vector.tensor_copy(halves[:, :, 2 * HD:3 * HD], rot[:, 1])
                    nc.vector.tensor_copy(halves[:, :, 4 * HD:5 * HD], rot[:, 1]).then_inc(hi_ready, 1)
                if stepno == 2:
                    dve.wait_ge(hi_ready, H(i, p, 1, 1))
                    nc.vector.tensor_tensor(halves[:, :, HD:2 * HD], rot[:, 0], halves[:, :, 0:HD], ALU.subtract)
                    nc.vector.tensor_tensor(halves[:, :, 3 * HD:4 * HD], rot[:, 1], halves[:, :, 2 * HD:3 * HD], ALU.subtract)\
                        .then_inc(halves_ready, 1)

            dve.wait_ge(cleared, 1)
            nc.vector.memset(negm[:], 0.0).then_inc(emptied[0], 1)
            for n in range(2):
                nc.vector.memset(nought[:, 4 + n:5 + n], 0.0).then_inc(y_added, 1)
            if causal:
                square_sums(0, 0)
                for n in range(3):
                    split(0, 0, n)
            dve.wait_ge(emptied[0], 1)
            maximum(0, 0, 0)
            maximum(0, 0, 1)
            with dve.Fori(0, HEADS // 2) as i:
                for p in range(2):
                    nxt = (i, 1) if p == 0 else (i + 1, 0)
                    for k in range(NB):
                        for g, since in plan.due(k):
                            if since == 1:
                                meet_first(i, p, g)
                            if since == 2:
                                meet_second(i, p, g)
                            if since in (6, 7):
                                add(i, p, g, since - 6)
                        maximum(i, p, k + 2)
                        empty(i, p, k)
                        if causal and k == SUM_STEP:
                            square_sums(*nxt)
                        if causal and 0 <= k - TWIST_STEP < 3:
                            split(*nxt, k - TWIST_STEP)
            meet_first(HEADS // 2, 0, -1)
            meet_second(HEADS // 2, 0, -1)
            add(HEADS // 2, 0, -1, 0)
            add(HEADS // 2, 0, -1, 1)

        @block.scalar
        def _(act):
            def exps(i, p, b):
                slot = (p * NB + b) % 2
                j, s, kts = blocks[b % NB]
                g, jj = j // QG, j % QG
                act.wait_ge(negm_ready, B(i, p, b) + 1)
                width = len(kts) * P
                nc.scalar.activation(probs[:, slot, 0:width],
                                     ps[:, 2 * slot:2 * slot + 2, :].rearrange("p a n -> p (a n)")[:, 0:width],
                                     ACT.Exp, bias=negm[:, (g + 1) % 2, jj, s:s + 1],
                                     accum_out=sums[:, (g + 1) % 2, jj, s:s + 1]).then_inc(probs_ready, 1)

            def empty(i, p, b):
                j = blocks[b][0]
                for bank, n, kts, _ in plan.fills[b]:
                    if bank == 1:
                        act.wait_ge(turned[1], F(1, i, p, n + 1) + 1)
                        nc.scalar.activation(
                            pT[:, (j // QG + 1) % 2, kts[0]:kts[-1] + 1:2, j % QG * P:(j % QG + 1) * P],
                            ps[:, TURN_BANK + 1, 0:len(kts) * P].rearrange("p (k n) -> p k n", n=P),
                            ACT.Copy).then_inc(emptied[1], 1)

            def make_out(i, p, f):
                act.wait_ge(made, H(i, p, FILLS, f) + 1)
                if causal and f < 8:
                    bank = ps[:, MAKE_BANK, :].rearrange("p (t x) -> p t x", t=2)[:, :, 0:3 * HD]
                    op = nc.scalar.activation(raw[p][:, :, 2 * f:2 * f + 2, :],
                                              bank.rearrange("p t (a e) -> p a t e", a=3), ACT.Copy)
                elif causal:
                    what, half = (f - 8) % 3, (f - 8) // 3
                    dst = (q, kA, kB)[what][p]
                    op = nc.scalar.activation(dst[:, half * 1024:(half + 1) * 1024],
                                              ps[:, MAKE_BANK, :].bitcast(F16), ACT.Copy)
                else:
                    if f == 0:
                        act.wait_ge(bq_staged, H(i, p, 1, 1))
                    if not (isinstance(i, int) and i == 0 and p == 0 and f == 0):
                        act.wait_ge(q_ready, H(i, p, FILLS, f))
                    op = nc.scalar.activation(qf[:], ps[:, MAKE_BANK, :], ACT.Identity,
                                              bias=bq_h[p][:], scale=HD ** -0.5)
                op.then_inc(made_out, 1)

            def square(i, p):
                act.wait_ge(made_out, H(i, p, FILLS, 8) + 1)
                nc.scalar.activation(sq[:], raw[p][:, 0:2], ACT.Square).then_inc(sq_ready, 1)

            def alphas(i, p, g):
                act.wait_ge(diff_ready, G(i, p, g) + 1)
                act.wait_ge(probs_ready, (B(i, p, plan.last[g] + 1) if g >= 0 else B(i, p, 0)) + 1)
                nc.scalar.activation(alpha[:], diff[:], ACT.Exp).then_inc(alpha_ready, 1)

            def values_out(i, p, g):
                act.wait_ge(values_ready, G(i, p, g) + 1)
                nc.scalar.activation(o_sb[:], ps[:, OUT_BANK, :], ACT.Copy).then_inc(o_ready, 1)

            act.wait_ge(cleared, 1)
            for n, counted in enumerate((probs_ready, emptied[1], made_out)):
                nc.scalar.activation(nought[:, n + 1:n + 2], nought[:, 0:1], ACT.Copy).then_inc(counted, 1)
            for f in range(8 if causal else 4):
                make_out(0, 0, f)
            if causal:
                square(0, 0)
                for f in range(8, 14):
                    make_out(0, 0, f)
            act.wait_ge(probs_ready, 1)
            exps(0, 0, 0)
            with act.Fori(0, HEADS // 2) as i:
                for p in range(2):
                    nxt = (i, 1) if p == 0 else (i + 1, 0)
                    for k in range(NB):
                        act.wait_ge(turned[0], F(0, i, p, plan.before[k][0]) + 1)
                        act.wait_ge(turned[1], F(1, i, p, plan.before[k][1]) + 1)
                        exps(i, p, k + 1)
                        for g, since in plan.due(k):
                            if since == 1:
                                alphas(i, p, g)
                            if since == 5:
                                values_out(i, p, g)
                        empty(i, p, k)
                        if causal and 0 <= k - FIRST_PROJ < 8:
                            make_out(*nxt, k - FIRST_PROJ)
                        if causal and k == SQUARE_STEP:
                            square(*nxt)
                        if causal and 0 <= k - FIRST_TURN < 6:
                            make_out(*nxt, k - FIRST_TURN + 8)
                        if not causal and (k - FIRST_PROJ) % PROJ_GAP == 0 and 0 <= k - FIRST_PROJ < 4 * PROJ_GAP:
                            make_out(*nxt, (k - FIRST_PROJ) // PROJ_GAP)
            alphas(HEADS // 2, 0, -1)
            values_out(HEADS // 2, 0, -1)

        @block.gpsimd
        def _(pool):
            def stage_wo(i, p):
                pool.tensor_copy(wo_h[p][:], WoT[:, i * 2 + p, :]).then_inc(wo_staged, 1)

            def stage_wq(i, p):
                for a in range(2):
                    pool.tensor_copy(wq_h[p][:, a, :], make["WT"][:, i * 2 + p, :]).then_inc(wq_staged, 1)
                pool.tensor_copy(bq_h[p][:], make["bq"][:, i * 2 + p, :]).then_inc(bq_staged, 1)

            def rope(i, p):
                cosw, sinw = make["cosw"], make["sinw"]
                half = HD // 2
                pool.wait_ge(made_out, H(i, p, FILLS, 8) + 1)
                pool.tensor_tensor(rot[:], raw[p][:, 0:2], cosw[:], ALU.mult).then_inc(roped, 1)
                pool.wait_ge(ss_ready, H(i, p, 1, 1))
                pool.tensor_tensor(sq[:, :, :, 0:half], raw[p][:, 0:2, :, half:HD], sinw[:, :, :, 0:half], ALU.mult)\
                    .then_inc(roped, 1)
                pool.tensor_tensor(sq[:, :, :, half:HD], raw[p][:, 0:2, :, 0:half], sinw[:, :, :, half:HD], ALU.mult)\
                    .then_inc(roped, 1)
                pool.tensor_scalar(rms[:], ss[:], 1.0 / HD, RMS_EPS, ALU.mult, ALU.add).then_inc(rms_ready, 1)
                pool.wait_ge(rms_ready, H(i, p, 1, 1))
                pool.tensor_tensor(rinv[:], rms[:], minus_half[:].to_broadcast([P, 2 * NT]), ALU.pow).then_inc(roped, 1)
                pool.wait_ge(roped, H(i, p, 4, 4))
                pool.tensor_tensor(rot[:], rot[:], sq[:], ALU.add).then_inc(rinv_ready, 1)

            def split_q(i, p):
                for f in range(4):
                    cols = slice(f * 512, (f + 1) * 512)
                    pool.wait_ge(made_out, H(i, p, FILLS, f) + 2)
                    pool.tensor_tensor(q[p][:, cols], qf[:], const["ones"][:].to_broadcast([P, 512]), ALU.mult).then_inc(q_hi, 1)
                    pool.wait_ge(q_hi, H(i, p, FILLS, f + 1))
                    pool.tensor_tensor(q[p][HD:P, cols], qf[HD:P, :], q[p][HD:P, cols], ALU.subtract).then_inc(q_ready, 1)
                    pool.wait_ge(q_ready, H(i, p, FILLS, f + 1))

            pool.memset(pT[:, 0], 0.0)
            pool.memset(o_sb[:], 0.0)
            pool.memset(sums[:], 1.0)
            pool.memset(nought[:], 0.0)
            pool.memset(wo_h[1][:], 0.0).then_inc(wo_staged, 1)
            if causal:
                pool.memset(raw[1][:, 2], 0.0)
            pool.memset(wo_h[0][:, 0:1], 0.0).then_inc(cleared, 1)
            pool.wait_ge(cleared, 1)
            if causal:
                rope(0, 0)
            else:
                stage_wq(0, 0)
                split_q(0, 0)
            stage_wo(0, 0)
            with pool.Fori(0, HEADS // 2) as i:
                for p in range(2):
                    nxt = (i, 1) if p == 0 else (i + 1, 0)
                    if not causal:
                        pool.wait_ge(made, H(*nxt, FILLS, 0))
                        stage_wq(*nxt)
                    pool.wait_ge(y_ready, G(i, p, -1) * 2 + 2)
                    stage_wo(*nxt)
                    if causal:
                        pool.wait_ge(halves_ready, H(*nxt, 1, 0))
                        rope(*nxt)
                    else:
                        split_q(*nxt)


def load_stage(nc, ps, stage, const, x, x_in, loads):
    with ExitStack() as ctx:
        sem = Sems(nc, ctx, stage)
        loaded = sem("loaded")
        names = ("ident", "identb", "ident16")
        zeroed = {n: sem(f"zeroed_{n}") for n in names}
        made = {n: sem(f"made_{n}") for n in names}
        mask_zeroed, mask_made, half_made = sem("mask_zeroed"), sem("mask_made"), sem("half_made")
        block = ctx.enter_context(nc.Block())

        @block.sync
        def _(sp):
            sp.dma_start(x[:], x_in[0].rearrange("(t p) c -> p t c", p=P)).then_inc(loaded, 16)
            for dst, src in loads:
                sp.dma_start(dst, src).then_inc(loaded, 16)
            sp.wait_ge(loaded, 16 * (1 + len(loads)))

        @block.gpsimd
        def _(pool):
            for n in names:
                make_identity(pool, const[n], zeroed[n], made[n])
            pool.memset(const["mask"][:], 0.0).then_inc(mask_zeroed, 1)
            pool.wait_ge(mask_zeroed, 1)
            pool.affine_select(out=const["mask"][:], in_=const["mask"][:], compare_op=ALU.is_ge, fill=-1e30,
                               base=0, pattern=[[-1, P]], channel_multiplier=1).then_inc(mask_made, 1)
            pool.memset(const["ones"][:], 1.0)
            pool.memset(const["eps"][:], LN_EPS)
            pool.memset(const["minus_half"][:], -0.5).then_inc(half_made, 1)
            for n in names:
                pool.wait_ge(made[n], 1)
            pool.wait_ge(mask_made, 1)
            pool.wait_ge(half_made, 1)


def causal_weights_stage(nc, ps, stage, const, wqkv, wo2, tabs, normw, WT, WoT, cosw, sinw):
    NW = 3 * HEADS * HD // P
    with ExitStack() as ctx:
        sem = Sems(nc, ctx, stage)
        turned, emptied, padded, tabled = sem("turned"), sem("emptied"), sem("padded"), sem("tabled")
        block = ctx.enter_context(nc.Block())
        jobs = [("qkv", f) for f in range(NW // 4)] + [("o", f) for f in range(HEADS // 4)]

        @block.tensor
        def _(pe):
            for n, (what, f) in enumerate(jobs):
                if n >= 8:
                    pe.wait_ge(emptied, n - 7)
                for m in range(4):
                    src = wqkv[:, 4 * f + m, :] if what == "qkv" else wo2[:, 4 * f + m].rearrange("p a e -> p (a e)")
                    mm = nc.tensor.transpose(ps[:, n % 8, m * P:(m + 1) * P], src, const["ident"][:])
                mm.then_inc(turned, 1)

        @block.scalar
        def _(act):
            for n, (what, f) in enumerate(jobs):
                act.wait_ge(turned, n + 1)
                if what == "qkv":
                    dst = WT[:, f // 2, 8 * (f % 2):8 * (f % 2) + 8, :].rearrange("p h e -> p (h e)")
                else:
                    dst = WoT[:, 4 * f:4 * f + 4, :].rearrange("p h e -> p (h e)")
                nc.scalar.activation(dst, ps[:, n % 8, :], ACT.Copy).then_inc(emptied, 1)
            act.wait_ge(emptied, len(jobs))

        @block.gpsimd
        def _(pool):
            pool.memset(WT[:, :, HEADS, :], 0.0).then_inc(padded, 1)
            pool.memset(WoT[:, HEADS, :], 0.0).then_inc(padded, 1)
            pool.wait_ge(padded, 2)

        @block.vector
        def _(dve):
            half = HD // 2
            for a in range(2):
                scale = HD ** -0.5 if a == 0 else 1.0
                w = normw[:, a, :].unsqueeze(1)
                for dst, tab, cols, wcols in ((cosw, 0, slice(0, HD), slice(0, HD)),
                                              (sinw, 1, slice(0, half), slice(half, HD)),
                                              (sinw, 1, slice(half, HD), slice(0, half))):
                    nc.vector.scalar_tensor_tensor(
                        out=dst[:, a, :, cols], in0=tabs[:, tab, :, cols], scalar=scale,
                        in1=w[:, :, wcols].to_broadcast([P, NT, wcols.stop - wcols.start]),
                        op0=ALU.mult, op1=ALU.mult).then_inc(tabled, 1)
            dve.wait_ge(tabled, 6)


def store_stage(nc, stage, x, out):
    with ExitStack() as ctx:
        stored = Sems(nc, ctx, stage)("stored")
        block = ctx.enter_context(nc.Block())

        @block.sync
        def _(sp):
            sp.dma_start(out[0].rearrange("(t p) c -> p t c", p=P), x[:]).then_inc(stored, 16)
            sp.wait_ge(stored, 16)


LAYERS = 2
LH = 8
WIN = 64
INNER = LH * HD
HID = C * 4 * 2 // 3
HCH = [(c, min(P, HID - c)) for c in range(0, HID, P)]


def local_stage(nc, stage, ps, xf, const, ins, rows):
    LAG_S, LAG_O = 2, 3
    RQ, RV, RP = 3, 5, 3
    B_Q, B_K, B_V, B_QT, B_KT, B_S, B_X = 0, 1, 2, 3, 4, 5, 7

    with ExitStack() as ctx:
        sem = Sems(nc, ctx, stage)

        def sb(name, shape, dt):
            return ctx.enter_context(nc.sbuf_tensor(f"{stage}_{name}", shape, dt))

        wqkv = sb("wqkv", [P, 3 * INNER], F32)
        wo = sb("wo", [P, INNER // P, C], F32)
        w1 = sb("w1", [P, 2 * HID], F32)
        w2 = sb("w2", [P, len(HCH), C], F32)
        b1 = sb("b1", [P, 2, len(HCH)], F32)
        lng, lnb = sb("lng", [P, 1], F32), sb("lnb", [P, 1], F32)
        b2 = sb("b2", [P, C], F32)
        qks = sb("qks", [P, 2, HD], F32)
        tab = rows["xpos"]
        wtab = sb("wtab", [P, 4, NT, HD], F32)
        hT = sb("hT", [C, T + 1], F32)
        raw = [sb(f"raw{n}", [P, 2, LH, HD], F32) for n in range(2)]
        sq = [sb(f"sq{n}", [P, 2, LH, HD], F32) for n in range(2)]
        qk = [sb(f"qk{n}", [P, 2, LH, HD], F32) for n in range(RQ)]
        ss = [sb(f"ss{n}", [P, 2 * LH], F32) for n in range(2)]
        ssc = [sb(f"ssc{n}", [P, 2 * LH], F32) for n in range(2)]
        rinv = [sb(f"rinv{n}", [P, 2 * LH], F32) for n in range(2)]
        V = [sb(f"v{n}", [P, INNER], F32) for n in range(RV)]
        Vs = [sb(f"vs{n}", [P, INNER], F32) for n in range(RV)]
        qT = [sb(f"qT{n}", [P, LH // 2, P], F32) for n in range(2)]
        kT = [sb(f"kT{n}", [P, LH // 2, WIN + P], F32) for n in range(2)]
        probs = [sb(f"probs{n}", [P, LH, P], F32) for n in range(RP)]
        negm = [sb(f"negm{n}", [P, LH], F32) for n in range(2)]
        sums = [sb(f"sums{n}", [P, LH], F32) for n in range(2)]
        rsum = [sb(f"rsum{n}", [P, LH], F32) for n in range(2)]
        pT = [sb(f"pT{n}", [P, LH, P], F32) for n in range(2)]
        oT = [sb(f"oT{n}", [P, INNER // P, P], F32) for n in range(2)]
        mask = sb("mask", [P, 2, P], BF16)
        h = sb("h", [P, NT, C], F32)
        hn = [sb(f"hn{n}", [P, QG, C], F32) for n in range(2)]
        stats = sb("stats", [P, NT, 6], F32)
        mv = sb("mv", [P, NT, 2], F32)
        veps = sb("veps", [P, NT], F32)
        rstd = sb("rstd", [P, NT], F32)
        hnT = [sb(f"hnT{n}", [C, QG * P], F32) for n in range(2)]
        gl = [sb(f"gl{n}", [P, QG * P], F32) for n in range(2)]
        hh = [[sb(f"hh{n}_{c}", [P, QG * P], F32) for c in range(len(HCH))] for n in range(2)]

        cleared, masked = sem("cleared"), sem("masked")
        w_in = sem("w_in")
        f_in = sem("f_in")
        tabled = sem("tabled")
        xT_turned, xT_out = sem("xT_turned"), sem("xT_out")
        qk_ready, v_ready = sem("qk_ready"), sem("v_ready")
        raw_ready, sq_ready, v_out = sem("raw_ready"), sem("sq_ready"), sem("v_out")
        v_shifted = [sem(f"v_shifted{n}") for n in range(RV)]
        ss_ready, ssc_ready, rinv_ready = sem("ss_ready"), sem("ssc_ready"), sem("rinv_ready")
        cos_ready, sinA_ready, sinB_ready = sem("cos_ready"), sem("sinA_ready"), sem("sinB_ready")
        rot_ready, qk_scaled = sem("rot_ready"), sem("qk_scaled")
        qkT_turned, qT_out = sem("qkT_turned"), sem("qT_out")
        s_ready, negm_ready, probs_ready, rsum_ready, p_scaled = (sem(n) for n in ("s_ready", "negm_ready", "probs_ready", "rsum_ready", "p_scaled"))
        pT_turned, pT_outA, pT_outB = sem("pT_turned"), sem("pT_outA"), sem("pT_outB")
        o_ready, o_out, y_ready, y_added = sem("o_ready"), sem("o_out"), sem("y_ready"), sem("y_added")
        h_copied, h_shifted, b2_added = sem("h_copied"), sem("h_shifted"), sem("b2_added")
        stats_ready, mv_ready, veps_ready, rstd_ready, hn_ready = (sem(n) for n in ("stats_ready", "mv_ready", "veps_ready", "rstd_ready", "hn_ready"))
        hnT_turned, hnT_out = sem("hnT_turned"), sem("hnT_out")
        g_ready, g_out, a_ready, hh_ready = sem("g_ready"), sem("g_out"), sem("a_ready"), sem("hh_ready")
        f_ready, f_added = sem("f_ready"), sem("f_added")
        NCH = len(HCH)

        block = ctx.enter_context(nc.Block())

        def shifted(i, j):
            return i * (32 * len(range(j % RV, NT, RV))) + 32 * (j // RV + 1)

        def steps():
            return range(-1, NT + LAG_O)

        @block.sync
        def _(sp):
            with sp.Fori(0, LAYERS) as i:
                sp.wait_ge(cleared, i + 1)
                sp.dma_start(wqkv[:], ins["L0_ffn_wqkv"][bass.ds(i, 1)].rearrange("a p n -> (a p) n")).then_inc(w_in, 16)
                sp.dma_start(wo[:], ins["L0_ffn_wo"][bass.ds(i, 1)].rearrange("a (k p) n -> p (a k) n", p=P)).then_inc(w_in, 16)
                sp.dma_start(qks[:, 0, :], ins["L0_ffn_q_scale"][bass.ds(i, 1)].rearrange("a e -> (a e)").partition_broadcast(P)).then_inc(w_in, 16)
                sp.dma_start(qks[:, 1, :], ins["L0_ffn_k_scale"][bass.ds(i, 1)].rearrange("a e -> (a e)").partition_broadcast(P)).then_inc(w_in, 16)
                sp.dma_start(w1[:], ins["L0_ffn_w1"][bass.ds(i, 1)].rearrange("a p n -> (a p) n")).then_inc(f_in, 16)
                for n, (c, m) in enumerate(HCH):
                    sp.dma_start(w2[0:m, n, :], ins["L0_ffn_w2"][bass.ds(i, 1), c:c + m, :].rearrange("a p n -> (a p) n")).then_inc(f_in, 16)
                    for a in range(2):
                        sp.dma_start(b1[0:m, a, n:n + 1], ins["L0_ffn_b1"][bass.ds(i, 1), a * HID + c:a * HID + c + m].rearrange("a p -> p a")).then_inc(f_in, 16)
                sp.dma_start(lng[:], ins["L0_ffn_ln_g"][bass.ds(i, 1)].rearrange("a p -> p a")).then_inc(f_in, 16)
                sp.dma_start(lnb[:], ins["L0_ffn_ln_b"][bass.ds(i, 1)].rearrange("a p -> p a")).then_inc(f_in, 16)
                sp.dma_start(b2[:], ins["L0_ffn_b2"][bass.ds(i, 1)].rearrange("a e -> (a e)").partition_broadcast(P)).then_inc(f_in, 16)
                for j in range(NT):
                    sp.wait_ge(v_out, i * NT + j + 1)
                    if j >= RV:
                        sp.wait_ge(o_ready, i * NT + j - RV + 1)
                    sp.dma_start(Vs[j % RV][0:WIN, :], V[max(j - 1, 0) % RV][WIN:P, :]).then_inc(v_shifted[j % RV], 16)
                    sp.dma_start(Vs[j % RV][WIN:P, :], V[j % RV][0:WIN, :]).then_inc(v_shifted[j % RV], 16)
                sp.wait_ge(y_added, i * NT + NT)
                sp.dma_start(h[1:P, :, C // 2:C], xf[0:P - 1, :, C // 2:C]).then_inc(h_shifted, 16)
                sp.dma_start(h[0:1, 1:NT, C // 2:C], xf[P - 1:P, 0:NT - 1, C // 2:C]).then_inc(h_shifted, 16)
        F_IN = 16 * (1 + NCH * 3 + 3)

        @block.gpsimd
        def _(pool):
            setup = []

            def then(op):
                setup.append(op)
                op.then_inc(masked, 1)
                pool.wait_ge(masked, len(setup))

            then(pool.memset(mask[:], 0.0))
            then(pool.memset(hT[C // 2:C, 0:1], 0.0))
            then(pool.memset(h[0:1, 0, C // 2:C], 0.0))
            for n in range(2):
                for w in range(2):
                    part = mask[w * WIN:(w + 1) * WIN, n, :]
                    then(pool.affine_select(out=part, in_=part, compare_op=ALU.is_ge, fill=-1e30, base=WIN,
                                            pattern=[[-1, P]], channel_multiplier=1))
                    then(pool.affine_select(out=part, in_=part, compare_op=ALU.is_ge, fill=-1e30, base=0,
                                            pattern=[[1, P]], channel_multiplier=-1))
            pool.affine_select(out=mask[0:WIN, 0, :], in_=mask[0:WIN, 0, :], compare_op=ALU.is_ge, fill=-1e30,
                               base=-WIN, pattern=[[1, P]], channel_multiplier=0).then_inc(cleared, 1)
            pool.wait_ge(cleared, 1)
            with pool.Fori(0, LAYERS) as i:
                for tau in steps():
                    j = tau
                    if 0 <= j < NT:
                        half = HD // 2
                        w = wtab[:, :, j, :].unsqueeze(2)
                        pool.wait_ge(raw_ready, i * NT + j + 1)
                        pool.wait_ge(tabled, i * 6 + 6)
                        pool.wait_ge(ss_ready, i * NT + j + 1)
                        pool.tensor_tensor(sq[j % 2][:, :, :, half:HD], raw[j % 2][:, :, :, 0:half],
                                           w[:, 1:4:2, :, half:HD].to_broadcast([P, 2, LH, half]), ALU.mult).then_inc(sinB_ready, 1)
                        pool.wait_ge(ssc_ready, i * NT + j + 1)
                        pool.tensor_tensor(rinv[j % 2][:], ssc[j % 2][:], const["minus_half"][:].to_broadcast([P, 2 * LH]), ALU.pow)\
                            .then_inc(rinv_ready, 1)
                        pool.wait_ge(cos_ready, i * NT + j + 1)
                        pool.wait_ge(sinA_ready, i * NT + j + 1)
                        pool.wait_ge(sinB_ready, i * NT + j + 1)
                        pool.tensor_tensor(qk[j % RQ][:], qk[j % RQ][:], sq[j % 2][:], ALU.add).then_inc(rot_ready, 1)
                    j = tau - LAG_S
                    if 0 <= j < NT:
                        pool.wait_ge(rsum_ready, i * NT + j + 1)
                        pool.tensor_tensor(probs[j % RP][:], probs[j % RP][:], rsum[j % 2][:].unsqueeze(2).to_broadcast([P, LH, P]),
                                           ALU.mult).then_inc(p_scaled, 1)
                pool.wait_ge(y_added, i * NT + NT)
                pool.tensor_tensor(h[:, :, 0:C // 2], xf[:, :, 0:C // 2], const["ones"][:].unsqueeze(2).to_broadcast([P, NT, C // 2]), ALU.mult).then_inc(h_copied, 1)
                pool.wait_ge(f_in, i * F_IN + F_IN)
                pool.wait_ge(h_copied, i + 1)
                pool.wait_ge(h_shifted, i * 32 + 32)
                for g in range(GROUPS):
                    pool.wait_ge(mv_ready, i * NT + QG * g + QG)
                    cols = slice(QG * g, QG * g + QG)
                    pool.tensor_tensor(veps[:, cols], mv[:, cols, 1], const["eps"][:].to_broadcast([P, QG]), ALU.add).then_inc(veps_ready, 1)
                    pool.wait_ge(veps_ready, i * GROUPS + g + 1)
                    pool.tensor_tensor(rstd[:, cols], veps[:, cols], const["minus_half"][:].to_broadcast([P, QG]), ALU.pow)\
                        .then_inc(rstd_ready, 1)
                    if g == 0:
                        pool.tensor_tensor(xf[:, 1:NT], xf[:, 1:NT], b2[:].unsqueeze(1).to_broadcast([P, NT - 1, C]), ALU.add)\
                            .then_inc(b2_added, 1)
                pool.wait_ge(f_added, i * GROUPS + GROUPS)
                pool.tensor_tensor(veps[:, 0:1], rstd[:, 0:1], const["ones"][:], ALU.mult).then_inc(cleared, 1)

        @block.tensor
        def _(pe):
            pe.wait_ge(cleared, 1)
            with pe.Fori(0, LAYERS) as i:
                for tau in steps():
                    j = tau - LAG_S
                    if 0 <= j < NT:
                        pe.wait_ge(qk_scaled, i * NT + j + 1)
                        if j >= 1:
                            pe.wait_ge(qT_out, i * NT + j)
                        if j >= 2:
                            pe.wait_ge(y_added, i * NT + j - 1)
                        flat = qk[j % RQ][:].rearrange("p a (k b) e -> p (a k) (b e)", b=2)
                        for m in range(LH):
                            mm = nc.tensor.transpose(ps[:, B_QT + m // 4, m % 4 * P:(m % 4 + 1) * P], flat[:, m, :], const["ident"][:])
                        mm.then_inc(qkT_turned, 1)
                    j = tau - LAG_O
                    if 0 <= j < NT:
                        pe.wait_ge(p_scaled, i * NT + j + 1)
                        for m in range(LH):
                            mm = nc.tensor.transpose(ps[:, B_S + m // 4, m % 4 * P:(m % 4 + 1) * P], probs[j % RP][:, m, :], const["ident"][:])
                        mm.then_inc(pT_turned, 1)
                    j = tau + 1
                    if 0 <= j < NT:
                        if j == 0:
                            pe.wait_ge(cleared, i + 1)
                        else:
                            pe.wait_ge(xT_out, i * NT + j)
                        if tau - LAG_O - 1 >= 0:
                            pe.wait_ge(o_out, i * NT + tau - LAG_O)
                        nc.tensor.transpose(ps[:, B_X, 0:P], xf[:, j, :], const["ident"][:]).then_inc(xT_turned, 1)
                    j = tau
                    if 0 <= j < NT:
                        if j == 0:
                            pe.wait_ge(w_in, i * 64 + 64)
                        pe.wait_ge(xT_out, i * NT + j + 1)
                        if j > 0:
                            pe.wait_ge(raw_ready, i * NT + j)
                        ht = hT[:, j * P:(j + 1) * P]
                        nc.tensor.matmul(ps[:, B_Q, :], ht, wqkv[:, 0:INNER], start=True, stop=True)
                        nc.tensor.matmul(ps[:, B_K, :], ht, wqkv[:, INNER:2 * INNER], start=True, stop=True).then_inc(qk_ready, 1)
                        if j > 0:
                            pe.wait_ge(v_out, i * NT + j)
                        nc.tensor.matmul(ps[:, B_V, :], ht, wqkv[:, 2 * INNER:3 * INNER], start=True, stop=True).then_inc(v_ready, 1)
                    j = tau - LAG_O
                    if 0 <= j < NT:
                        pe.wait_ge(pT_outA, i * NT + j + 1)
                        pe.wait_ge(pT_outB, i * NT + j + 1)
                        pe.wait_ge(v_shifted[j % RV], shifted(i, j))
                        if tau + 1 < NT:
                            pe.wait_ge(xT_out, i * NT + tau + 2)
                        for pr in range(LH // 2):
                            for w in range(2):
                                for a in range(2):
                                    head = 2 * pr + a
                                    mm = nc.tensor.matmul(ps[a * HD:(a + 1) * HD, B_X, pr * P + w * WIN:pr * P + (w + 1) * WIN],
                                                          (Vs, V)[w][j % RV][:, head * HD:(head + 1) * HD],
                                                          pT[j % 2][:, a * 4 + pr, w * WIN:(w + 1) * WIN], start=True, stop=True)
                        mm.then_inc(o_ready, 1)
                    j = tau - LAG_S
                    if 0 <= j < NT:
                        pe.wait_ge(qT_out, i * NT + j + 1)
                        if tau - LAG_O >= 0:
                            pe.wait_ge(pT_outA, i * NT + tau - LAG_O + 1)
                            pe.wait_ge(pT_outB, i * NT + tau - LAG_O + 1)
                        if j >= 1:
                            pe.wait_ge(probs_ready, i * NT + j)
                        for a in range(2):
                            nc.tensor.matmul(ps[:, B_S + a, :], const["identb"][:],
                                             mask[:, min(j, 1), :].unsqueeze(1).to_broadcast([P, 4, P]),
                                             start=True, stop=False, skip_group_check=True)
                        for head in range(LH):
                            r = slice(head % 2 * HD, (head % 2 + 1) * HD)
                            for w in range(2):
                                mm = nc.tensor.matmul(ps[w * WIN:(w + 1) * WIN, B_S + head % 2, head // 2 * P:(head // 2 + 1) * P],
                                                 qT[j % 2][r, head // 2, w * WIN:(w + 1) * WIN],
                                                 kT[j % 2][r, head // 2, w * WIN:w * WIN + P],
                                                 start=False, stop=True, skip_group_check=True)
                        mm.then_inc(s_ready, 1)
                    j = tau - LAG_O
                    if 0 <= j < NT:
                        pe.wait_ge(o_out, i * NT + j + 1)
                        for k in range(INNER // P):
                            mm = nc.tensor.matmul(ps[:, B_QT, 0:C], oT[j % 2][:, k, :], wo[:, k, :], start=(k == 0), stop=(k == INNER // P - 1))
                        mm.then_inc(y_ready, 1)
                for g in range(GROUPS + 1):
                    if g < GROUPS:
                        pe.wait_ge(hn_ready, i * NT + QG * g + QG)
                        if g >= 1:
                            pe.wait_ge(hnT_out, i * GROUPS + g)
                        for m in range(QG):
                            mm = nc.tensor.transpose(ps[:, 0, m * P:(m + 1) * P], hn[g % 2][:, m, :], const["ident"][:])
                        mm.then_inc(hnT_turned, 1)
                    if g >= 1:
                        gg = g - 1
                        if gg >= 1:
                            pe.wait_ge(f_added, i * GROUPS + gg)
                        for m in range(QG):
                            for n, (c, w) in enumerate(HCH):
                                if m == 0:
                                    pe.wait_ge(hh_ready, i * (GROUPS * NCH) + gg * NCH + n + 1)
                                mm = nc.tensor.matmul(ps[:, 1, m * P:(m + 1) * P], hh[gg % 2][n][0:w, m * P:(m + 1) * P], w2[0:w, n, :],
                                                      start=(n == 0), stop=(n == NCH - 1))
                        mm.then_inc(f_ready, 1)
                    if g < GROUPS:
                        pe.wait_ge(hnT_out, i * GROUPS + g + 1)
                        for n, (c, w) in enumerate(HCH):
                            u = g * NCH + n
                            for what, ready, freed in ((1, g_ready, g_out), (0, a_ready, hh_ready)):
                                if u >= 2:
                                    pe.wait_ge(freed, i * (GROUPS * NCH) + u - 1)
                                nc.tensor.matmul(ps[0:w, 2 + 2 * what + u % 2, :], w1[:, what * HID + c:what * HID + c + w], hnT[g % 2][:],
                                                 start=True, stop=True).then_inc(ready, 1)

        @block.scalar
        def _(act):
            act.wait_ge(cleared, 1)
            with act.Fori(0, LAYERS) as i:
                for tau in steps():
                    j = tau - LAG_S
                    if 0 <= j < NT:
                        act.wait_ge(qkT_turned, i * NT + j + 1)
                        if j > 0:
                            nc.scalar.activation(kT[j % 2][:, :, 0:WIN], kT[(j - 1) % 2][:, :, P:P + WIN], ACT.Copy)
                        else:
                            nc.scalar.activation(kT[0][:, :, 0:WIN], ps[:, B_KT, :].rearrange("p (k n) -> p k n", n=P)[:, :, 0:WIN], ACT.Copy)
                        nc.scalar.activation(qT[j % 2][:], ps[:, B_QT, :].rearrange("p (k n) -> p k n", n=P), ACT.Copy)
                        nc.scalar.activation(kT[j % 2][:, :, WIN:WIN + P], ps[:, B_KT, :].rearrange("p (k n) -> p k n", n=P), ACT.Copy)\
                            .then_inc(qT_out, 1)
                    j = tau - LAG_O
                    if 0 <= j < NT:
                        act.wait_ge(pT_turned, i * NT + j + 1)
                        nc.scalar.activation(pT[j % 2][:, 0:4, :], ps[:, B_S, :].rearrange("p (k n) -> p k n", n=P), ACT.Copy).then_inc(pT_outA, 1)
                    j = tau + 1
                    if 0 <= j < NT:
                        act.wait_ge(xT_turned, i * NT + j + 1)
                        nc.scalar.activation(hT[0:C // 2, j * P:(j + 1) * P], ps[0:C // 2, B_X, 0:P], ACT.Copy)
                        nc.scalar.activation(hT[C // 2:C, j * P + 1:(j + 1) * P + 1], ps[C // 2:C, B_X, 0:P], ACT.Copy).then_inc(xT_out, 1)
                    j = tau
                    if 0 <= j < NT:
                        act.wait_ge(qk_ready, i * NT + j + 1)
                        if j >= 2:
                            act.wait_ge(rot_ready, i * NT + j - 1)
                        nc.scalar.activation(raw[j % 2][:], ps[:, B_Q:B_K + 1, :].rearrange("p a (k e) -> p a k e", e=HD), ACT.Copy).then_inc(raw_ready, 1)
                        act.wait_ge(raw_ready, i * NT + j + 1)
                        nc.scalar.activation(sq[j % 2][:], raw[j % 2][:], ACT.Square).then_inc(sq_ready, 1)
                    j = tau - LAG_O
                    if 0 <= j < NT:
                        act.wait_ge(o_ready, i * NT + j + 1)
                        nc.scalar.activation(oT[j % 2][:], ps[:, B_X, :].rearrange("p (k n) -> p k n", n=P), ACT.Copy).then_inc(o_out, 1)
                    j = tau - LAG_S
                    if 0 <= j < NT:
                        act.wait_ge(negm_ready, i * NT + j + 1)
                        for head in range(LH):
                            op = nc.scalar.activation(probs[j % RP][:, head, :], ps[:, B_S + head // 4, head % 4 * P:(head % 4 + 1) * P], ACT.Exp,
                                                      bias=negm[j % 2][:, head:head + 1], accum_out=sums[j % 2][:, head:head + 1])
                        op.then_inc(probs_ready, 1)
                act.wait_ge(f_in, i * F_IN + F_IN)
                for g in range(GROUPS):
                    act.wait_ge(hnT_turned, i * GROUPS + g + 1)
                    nc.scalar.activation(hnT[g % 2][:], ps[:, 0, :], ACT.Identity, bias=lnb[:], scale=lng[:]).then_inc(hnT_out, 1)
                    for n, (c, w) in enumerate(HCH):
                        u = g * NCH + n
                        act.wait_ge(g_ready, i * (GROUPS * NCH) + u + 1)
                        if u >= 2:
                            act.wait_ge(hh_ready, i * (GROUPS * NCH) + u - 1)
                        nc.scalar.activation(gl[u % 2][0:w, :], ps[0:w, 4 + u % 2, :], ACT.Gelu, bias=b1[0:w, 1, n:n + 1]).then_inc(g_out, 1)

        @block.vector
        def _(dve):
            half = HD // 2
            dve.wait_ge(cleared, 1)
            with dve.Fori(0, LAYERS) as i:
                dve.wait_ge(w_in, i * 64 + 64)
                for a in range(2):
                    w = qks[:, a, :].unsqueeze(1)
                    nc.vector.tensor_tensor(wtab[:, 2 * a], tab[:, 2 * a], w.to_broadcast([P, NT, HD]), ALU.mult).then_inc(tabled, 1)
                    nc.vector.tensor_tensor(wtab[:, 2 * a + 1, :, 0:half], tab[:, 2 * a + 1, :, 0:half],
                                            w[:, :, half:HD].to_broadcast([P, NT, half]), ALU.mult).then_inc(tabled, 1)
                    nc.vector.tensor_tensor(wtab[:, 2 * a + 1, :, half:HD], tab[:, 2 * a + 1, :, half:HD],
                                            w[:, :, 0:half].to_broadcast([P, NT, half]), ALU.mult).then_inc(tabled, 1)
                dve.wait_ge(tabled, i * 6 + 6)
                for tau in steps():
                    j = tau - LAG_O
                    if 0 <= j < NT:
                        dve.wait_ge(pT_turned, i * NT + j + 1)
                        nc.vector.tensor_copy(pT[j % 2][:, 4:8, :], ps[:, B_S + 1, :].rearrange("p (k n) -> p k n", n=P)).then_inc(pT_outB, 1)
                    j = tau
                    if 0 <= j < NT:
                        w = wtab[:, :, j, :].unsqueeze(2)
                        dve.wait_ge(raw_ready, i * NT + j + 1)
                        if j >= RQ:
                            dve.wait_ge(qkT_turned, i * NT + j - RQ + 1)
                        nc.vector.tensor_tensor(qk[j % RQ][:], raw[j % 2][:], w[:, 0:4:2].to_broadcast([P, 2, LH, HD]), ALU.mult).then_inc(cos_ready, 1)
                        dve.wait_ge(v_ready, i * NT + j + 1)
                        if j >= RV:
                            dve.wait_ge(o_ready, i * NT + j - RV + 1)
                            dve.wait_ge(v_shifted[(j - RV + 1) % RV], shifted(i, j - RV + 1))
                        nc.vector.tensor_copy(V[j % RV][:], ps[:, B_V, :]).then_inc(v_out, 1)
                        dve.wait_ge(sq_ready, i * NT + j + 1)
                        nc.vector.tensor_reduce(ss[j % 2][:].rearrange("p (a k) -> p a k", a=2), sq[j % 2][:], AX_X, ALU.add).then_inc(ss_ready, 1)
                        dve.wait_ge(ss_ready, i * NT + j + 1)
                        nc.vector.tensor_scalar(ssc[j % 2][:], ss[j % 2][:], 1e-24, 0.0, ALU.max, ALU.add).then_inc(ssc_ready, 1)
                        nc.vector.tensor_tensor(sq[j % 2][:, :, :, 0:half], raw[j % 2][:, :, :, half:HD],
                                                w[:, 1:4:2, :, 0:half].to_broadcast([P, 2, LH, half]), ALU.mult).then_inc(sinA_ready, 1)
                    j = tau - LAG_S
                    if 0 <= j < NT:
                        dve.wait_ge(s_ready, i * NT + j + 1)
                        nc.vector.tensor_reduce(negm[j % 2][:], ps[:, B_S:B_S + 2, :].rearrange("p a (k n) -> p (a k) n", n=P), AX_X, ALU.max,
                                                negate=True).then_inc(negm_ready, 1)
                    j = tau
                    if 0 <= j < NT:
                        dve.wait_ge(rot_ready, i * NT + j + 1)
                        dve.wait_ge(rinv_ready, i * NT + j + 1)
                        nc.vector.tensor_tensor(qk[j % RQ][:].rearrange("p a k e -> p (a k) e"), qk[j % RQ][:].rearrange("p a k e -> p (a k) e"),
                                                rinv[j % 2][:].unsqueeze(2).to_broadcast([P, 2 * LH, HD]), ALU.mult).then_inc(qk_scaled, 1)
                    j = tau - LAG_S
                    if 0 <= j < NT:
                        dve.wait_ge(probs_ready, i * NT + j + 1)
                        nc.vector.reciprocal(rsum[j % 2][:], sums[j % 2][:]).then_inc(rsum_ready, 1)
                    j = tau - LAG_O
                    if 0 <= j < NT:
                        dve.wait_ge(y_ready, i * NT + j + 1)
                        nc.vector.tensor_tensor(xf[:, j, :], ps[:, B_QT, 0:C], xf[:, j, :], ALU.add).then_inc(y_added, 1)
                dve.wait_ge(h_copied, i + 1)
                dve.wait_ge(h_shifted, i * 32 + 32)
                for t in range(NT):
                    nc.vector.bn_stats(stats[:, t, :], h[:, t, :]).then_inc(stats_ready, 1)
                dve.wait_ge(stats_ready, i * NT + NT)
                dve.wait_ge(f_in, i * F_IN + F_IN)
                nc.vector.tensor_tensor(xf[:, 0], xf[:, 0], b2[:], ALU.add).then_inc(b2_added, 1)
                for t in range(NT):
                    nc.vector.bn_aggr(mv[:, t, :], stats[:, t, :]).then_inc(mv_ready, 1)

                def normed(g):
                    dve.wait_ge(rstd_ready, i * GROUPS + g + 1)
                    dve.wait_ge(mv_ready, i * NT + NT)
                    if g >= 2:
                        dve.wait_ge(hnT_turned, i * GROUPS + g - 1)
                    for m in range(QG):
                        t = QG * g + m
                        nc.vector.tensor_scalar(hn[g % 2][:, m, :], h[:, t, :], mv[:, t, 0:1], rstd[:, t:t + 1], ALU.subtract, ALU.mult)\
                            .then_inc(hn_ready, 1)

                normed(0)
                for g in range(GROUPS):
                    if g + 1 < GROUPS:
                        normed(g + 1)
                    for n, (c, w) in enumerate(HCH):
                        u = g * NCH + n
                        dve.wait_ge(a_ready, i * (GROUPS * NCH) + u + 1)
                        dve.wait_ge(g_out, i * (GROUPS * NCH) + u + 1)
                        if g >= 2:
                            dve.wait_ge(f_ready, i * GROUPS + g - 1)
                        nc.vector.scalar_tensor_tensor(out=hh[g % 2][n][0:w, :], in0=ps[0:w, 2 + u % 2, :], scalar=b1[0:w, 0, n:n + 1],
                                                       in1=gl[u % 2][0:w, :], op0=ALU.add, op1=ALU.mult).then_inc(hh_ready, 1)
                    dve.wait_ge(f_ready, i * GROUPS + g + 1)
                    dve.wait_ge(b2_added, i * 2 + 2)
                    rows_ = xf[:, QG * g:QG * g + QG, :]
                    nc.vector.tensor_tensor(rows_, ps[:, 1, :].rearrange("p (t c) -> p t c", c=C), rows_, ALU.add).then_inc(f_added, 1)


def shared_weights_stage(nc, ps, stage, x, xnT, bo, wkd, bkd, wv, bv, bq, bqs, WqT, WoT2, kA, kB, V):
    with ExitStack() as ctx:
        sem = Sems(nc, ctx, stage)
        kf = [ctx.enter_context(nc.sbuf_tensor(f"{stage}_kf{n}", [P, 512], F32)) for n in range(2)]
        padded, k_ready, kf_ready, hi_ready, k_done = (sem(n) for n in ("padded", "k_ready", "kf_ready", "hi_ready", "k_done"))
        v_ready, v_done, scaled = sem("v_ready"), sem("v_done"), sem("scaled")
        block = ctx.enter_context(nc.Block())

        @block.tensor
        def _(pe):
            for f in range(4):
                nc.tensor.matmul(ps[:, f, :], wkd[:].rearrange("p a e -> p (a e)"), xnT[:, f * 512:(f + 1) * 512],
                                 start=True, stop=True).then_inc(k_ready, 1)
            for t in range(NT):
                mm = nc.tensor.matmul(ps[:, 4 + t // 8, t % 8 * HD:(t % 8 + 1) * HD], xnT[:, t * P:(t + 1) * P], wv[:],
                                      start=True, stop=True)
                if t % 8 == 7:
                    mm.then_inc(v_ready, 1)

        @block.scalar
        def _(act):
            nc.scalar.activation(bqs[:, 0:HEADS], bq[:], ACT.Copy, scale=HD ** -0.5).then_inc(scaled, 1)
            for f in range(4):
                act.wait_ge(k_ready, f + 1)
                if f >= 2:
                    act.wait_ge(k_done, f - 1)
                nc.scalar.activation(kf[f % 2][:], ps[:, f, :], ACT.Identity, bias=bkd[:]).then_inc(kf_ready, 1)
            act.wait_ge(scaled, 1)

        @block.vector
        def _(dve):
            for f in range(4):
                cols = slice(f * 512, (f + 1) * 512)
                dve.wait_ge(kf_ready, f + 1)
                nc.vector.tensor_copy(kA[:, cols], kf[f % 2][:]).then_inc(hi_ready, 1)
                dve.wait_ge(hi_ready, f + 1)
                nc.vector.tensor_tensor(kB[:, cols], kf[f % 2][:], kA[:, cols], ALU.subtract).then_inc(k_done, 1)
            for n in range(2):
                dve.wait_ge(v_ready, n + 1)
                nc.vector.tensor_tensor(V[:, 8 * n:8 * n + 8, :], ps[:, 4 + n, :].rearrange("p (t e) -> p t e", e=HD),
                                        bv[:].unsqueeze(1).to_broadcast([P, 8, HD]), ALU.add).then_inc(v_done, 1)
            dve.wait_ge(v_done, 2)
            dve.wait_ge(k_done, 4)

        @block.gpsimd
        def _(pool):
            pool.memset(WqT[:, HEADS, :], 0.0).then_inc(padded, 1)
            pool.memset(WoT2[:, HEADS, :], 0.0).then_inc(padded, 1)
            pool.memset(bqs[:, HEADS, :], 0.0).then_inc(padded, 1)
            pool.tensor_tensor(x[:], x[:], bo[:].unsqueeze(1).to_broadcast([P, NT, C]), ALU.add).then_inc(padded, 1)
            pool.wait_ge(padded, 4)


def add_stage(nc, stage, x, y):
    with ExitStack() as ctx:
        added = Sems(nc, ctx, stage)("added")
        block = ctx.enter_context(nc.Block())

        @block.vector
        def _(dve):
            nc.vector.tensor_tensor(x[:, 0:10], x[:, 0:10], y[:, 0:10], ALU.add).then_inc(added, 1)
            dve.wait_ge(added, 2)

        @block.gpsimd
        def _(pool):
            pool.tensor_tensor(x[:, 10:NT], x[:, 10:NT], y[:, 10:NT], ALU.add).then_inc(added, 1)
            pool.wait_ge(added, 2)


def load_only_stage(nc, stage, loads):
    with ExitStack() as ctx:
        loaded = Sems(nc, ctx, stage)("loaded")
        block = ctx.enter_context(nc.Block())

        @block.sync
        def _(sp):
            with nc.allow_non_contiguous_dma(reason="biases, a few KB"):
                for dst, src in loads:
                    sp.dma_start(dst, src).then_inc(loaded, 16)
            sp.wait_ge(loaded, 16 * len(loads))


EXPERTS = 8
FF = 512
FCH = FF // P


def experts_stage(nc, stage, ps, x, xnT, const, ins, out):
    HB = QG * P
    with ExitStack() as ctx:
        sem = Sems(nc, ctx, stage)

        def sb(name, shape, dt):
            return ctx.enter_context(nc.sbuf_tensor(f"{stage}_{name}", shape, dt))

        w1 = [sb(f"w1_{n}", [C, FF], F32) for n in range(2)]
        w2 = [sb(f"w2_{n}", [P, FCH, C], F32) for n in range(2)]
        b1 = [sb(f"b1_{n}", [P, FCH], F32) for n in range(2)]
        b2 = sb("b2", [EXPERTS, C], F32)
        rw = sb("rw", [C, EXPERTS], F32)
        rb = sb("rb", [P, EXPERTS], F32)
        logits = sb("logits", [P, NT, EXPERTS], F32)
        top = sb("top", [P, NT, 8], F32)
        topi = sb("topi", [P, NT, 8], U32)
        topf = sb("topf", [P, NT, 2], F32)
        gap = sb("gap", [P, NT], F32)
        egap = sb("egap", [P, NT], F32)
        esum = sb("esum", [P, NT], F32)
        g12 = sb("g12", [P, NT, 2], F32)
        iota = sb("iota", [P, EXPERTS], F32)
        hot = [sb(f"hot{n}", [P, NT, EXPERTS], F32) for n in range(2)]
        gates = sb("gates", [P, NT, EXPERTS], F32)
        gT = sb("gT", [EXPERTS, NT, P], F32)
        hh = [[sb(f"hh{n}_{c}", [P, HB], F32) for c in range(FCH)] for n in range(2)]

        r_in, w_in = sem("r_in"), [sem(f"w_in{n}") for n in range(2)]
        l_ready, l_done, top_ready, topi_ready = sem("l_ready"), sem("l_done"), sem("top_ready"), sem("topi_ready")
        topf_ready, gap_ready, egap_ready, esum_ready = sem("topf_ready"), sem("gap_ready"), sem("egap_ready"), sem("esum_ready")
        g12_ready, hot_ready, hot_weighted, gates_ready = sem("g12_ready"), sem("hot_ready"), sem("hot_weighted"), sem("gates_ready")
        iota_ready, gT_turned, gT_out, b_ready, b_added = (sem(n) for n in ("iota_ready", "gT_turned", "gT_out", "b_ready", "b_added"))
        h_ready = sem("h_ready")
        h_out = sem("h_out")
        y_ready = sem("y_ready")
        y_added = sem("y_added")
        stored = sem("stored")
        NH = GROUPS * FCH
        HBANKS, YBANKS = 4, 4

        block = ctx.enter_context(nc.Block())

        @block.sync
        def _(sp):
            sp.dma_start(rw[:], ins["L1_ffn_router_w"]).then_inc(r_in, 16)
            sp.dma_start(rb[:], ins["L1_ffn_router_b"].partition_broadcast(P)).then_inc(r_in, 16)
            sp.dma_start(b2[:], ins["L1_ffn_b2"]).then_inc(r_in, 16)

            def load(i, n):
                sp.dma_start(w1[n][:], ins["L1_ffn_w1"][bass.ds(i * 2 + n, 1)].rearrange("a p n -> (a p) n")).then_inc(w_in[n], 16)
                sp.dma_start(w2[n][:], ins["L1_ffn_w2"][bass.ds(i * 2 + n, 1)].rearrange("a (k p) n -> p (a k) n", p=P)).then_inc(w_in[n], 16)
                with nc.allow_non_contiguous_dma(reason="a bias, 2 KB"):
                    sp.dma_start(b1[n][:], ins["L1_ffn_b1"][bass.ds(i * 2 + n, 1)].rearrange("a (k p) -> p (a k)", p=P)).then_inc(w_in[n], 16)

            load(0, 0)
            load(0, 1)
            with sp.Fori(0, EXPERTS // 2 - 1) as i:
                for n in range(2):
                    sp.wait_ge(y_ready, i * (2 * GROUPS) + (n + 1) * GROUPS)
                    load(i + 1, n)
            for g in range(GROUPS):
                sp.wait_ge(y_added, (EXPERTS - 1) * GROUPS + g + 1 + YBANKS)
                sp.dma_start(out[0, g * HB:(g + 1) * HB, :].rearrange("(t p) c -> p t c", p=P), x[:, QG * g:QG * g + QG, :]).then_inc(stored, 16)
            sp.wait_ge(stored, 16 * GROUPS)

        @block.tensor
        def _(pe):
            pe.wait_ge(r_in, 48)
            for t in range(NT):
                mm = nc.tensor.matmul(ps[:, 0, t * EXPERTS:(t + 1) * EXPERTS], xnT[:, t * P:(t + 1) * P], rw[:], start=True, stop=True)
            mm.then_inc(l_ready, 1)
            pe.wait_ge(gates_ready, 1)
            for g in range(GROUPS):
                for m in range(QG):
                    mm = nc.tensor.transpose(ps[0:EXPERTS, 4 + g, m * P:(m + 1) * P], gates[:, QG * g + m, :], const["ident"][:])
                mm.then_inc(gT_turned, 1)
            for g in range(GROUPS):
                pe.wait_ge(gT_out, g + 1)
                for m in range(QG):
                    mm = nc.tensor.matmul(ps[:, 4 + g, m * P:(m + 1) * P], gT[:, QG * g + m, :], b2[:], start=True, stop=True)
                mm.then_inc(b_ready, 1)

            def hidden(i, n, g):
                for c in range(FCH):
                    u = n * NH + g * FCH + c
                    pe.wait_ge(h_out, i * (2 * NH) + (u + 1))
                    nc.tensor.matmul(ps[:, c, :], w1[n][:, c * P:(c + 1) * P], xnT[:, g * HB:(g + 1) * HB],
                                     start=True, stop=True).then_inc(h_ready, 1)

            def output(i, n, g):
                u = n * GROUPS + g
                pe.wait_ge(y_added, i * (2 * GROUPS) + (u + 1))
                pe.wait_ge(h_out, i * (2 * NH) + ((u + 1) * FCH + HBANKS))
                for m in range(QG):
                    for c in range(FCH):
                        mm = nc.tensor.matmul(ps[:, 4 + g, m * P:(m + 1) * P], hh[g % 2][c][:, m * P:(m + 1) * P], w2[n][:, c, :],
                                              start=(c == 0), stop=(c == FCH - 1))
                mm.then_inc(y_ready, 1)

            with pe.Fori(0, EXPERTS // 2) as i:
                pe.wait_ge(w_in[0], i * 48 + 48)
                hidden(i, 0, 0)
                for n in range(2):
                    for g in range(GROUPS):
                        if g + 1 < GROUPS:
                            hidden(i, n, g + 1)
                        elif n == 0:
                            pe.wait_ge(w_in[1], i * 48 + 48)
                            hidden(i, 1, 0)
                        output(i, n, g)

        @block.scalar
        def _(act):
            act.wait_ge(gap_ready, 1)
            nc.scalar.activation(egap[:], gap[:], ACT.Exp).then_inc(egap_ready, 1)
            for g in range(GROUPS):
                act.wait_ge(gT_turned, g + 1)
                nc.scalar.activation(gT[:, QG * g:QG * g + QG, :], ps[0:EXPERTS, 4 + g, :].rearrange("p (t n) -> p t n", n=P), ACT.Copy)\
                    .then_inc(gT_out, 1)
            for n in range(HBANKS):
                nc.scalar.activation(hh[0][0][:, n:n + 1], egap[:, n:n + 1], ACT.Copy).then_inc(h_out, 1)
            act.wait_ge(h_out, HBANKS)
            with act.Fori(0, EXPERTS // 2) as i:
                for n in range(2):
                    act.wait_ge(w_in[n], i * 48 + 48)
                    for g in range(GROUPS):
                        for c in range(FCH):
                            u = n * NH + g * FCH + c
                            act.wait_ge(h_ready, i * (2 * NH) + (u + 1))
                            nc.scalar.activation(hh[g % 2][c][:], ps[:, c, :], ACT.Gelu, bias=b1[n][:, c:c + 1]).then_inc(h_out, 1)

        @block.vector
        def _(dve):
            dve.wait_ge(l_ready, 1)
            dve.wait_ge(r_in, 48)
            nc.vector.tensor_tensor(logits[:], ps[:, 0, 0:NT * EXPERTS].rearrange("p (t e) -> p t e", e=EXPERTS),
                                    rb[:].unsqueeze(1).to_broadcast([P, NT, EXPERTS]), ALU.add).then_inc(l_done, 1)
            dve.wait_ge(l_done, 1)
            for t in range(NT):
                nc.vector.max(top[:, t, :], logits[:, t, :]).then_inc(top_ready, 1)
            for t in range(NT):
                dve.wait_ge(top_ready, t + 1)
                nc.vector.max_index(topi[:, t, :], top[:, t, :], logits[:, t, :]).then_inc(topi_ready, 1)
            dve.wait_ge(topi_ready, NT)
            nc.vector.tensor_copy(topf[:], topi[:, :, 0:2]).then_inc(topf_ready, 1)
            dve.wait_ge(top_ready, NT)
            nc.vector.tensor_tensor(gap[:], top[:, :, 1], top[:, :, 0], ALU.subtract).then_inc(gap_ready, 1)
            dve.wait_ge(egap_ready, 1)
            nc.vector.tensor_scalar(esum[:], egap[:], 1.0, 0.0, ALU.add, ALU.add).then_inc(esum_ready, 1)
            dve.wait_ge(esum_ready, 1)
            nc.vector.reciprocal(g12[:, :, 0], esum[:]).then_inc(g12_ready, 1)
            dve.wait_ge(g12_ready, 1)
            nc.vector.tensor_tensor(g12[:, :, 1], g12[:, :, 0], egap[:], ALU.mult).then_inc(g12_ready, 1)
            dve.wait_ge(topf_ready, 1)
            dve.wait_ge(iota_ready, EXPERTS)
            for n in range(2):
                nc.vector.tensor_tensor(hot[n][:], topf[:, :, n:n + 1].to_broadcast([P, NT, EXPERTS]),
                                        iota[:].unsqueeze(1).to_broadcast([P, NT, EXPERTS]), ALU.is_equal).then_inc(hot_ready, 1)
            dve.wait_ge(g12_ready, 2)
            for n in range(2):
                dve.wait_ge(hot_ready, n + 1)
                nc.vector.tensor_tensor(hot[n][:], hot[n][:], g12[:, :, n:n + 1].to_broadcast([P, NT, EXPERTS]), ALU.mult).then_inc(hot_weighted, 1)
            dve.wait_ge(hot_weighted, 2)
            nc.vector.tensor_tensor(gates[:], hot[0][:], hot[1][:], ALU.add).then_inc(gates_ready, 1)
            dve.wait_ge(gates_ready, 1)
            for g in range(GROUPS):
                dve.wait_ge(b_ready, g + 1)
                rows = x[:, QG * g:QG * g + QG, :]
                nc.vector.tensor_tensor(rows, ps[:, 4 + g, :].rearrange("p (t c) -> p t c", c=C), rows, ALU.add).then_inc(y_added, 1)
            dve.wait_ge(y_added, GROUPS)
            with dve.Fori(0, EXPERTS // 2) as i:
                for n in range(2):
                    for g in range(GROUPS):
                        u = n * GROUPS + g
                        dve.wait_ge(y_ready, i * (2 * GROUPS) + (u + 1))
                        dve.wait_ge(y_added, i * (2 * GROUPS) + (u + 1))
                        for m in range(QG):
                            t = QG * g + m
                            op = nc.vector.scalar_tensor_tensor(out=x[:, t, :], in0=ps[:, 4 + g, m * P:(m + 1) * P], scalar=gates[:, t, bass.ds(i * 2 + n, 1)],
                                                                in1=x[:, t, :], op0=ALU.mult, op1=ALU.add)
                        op.then_inc(y_added, 1)

        @block.gpsimd
        def _(pool):
            for e in range(EXPERTS):
                pool.memset(iota[:, e:e + 1], float(e)).then_inc(iota_ready, 1)
            pool.wait_ge(iota_ready, EXPERTS)


def build(nc, ins, out):
    with ExitStack() as ctx:
        def sb(name, shape, dt, c=ctx):
            return c.enter_context(nc.sbuf_tensor(name, shape, dt))

        ps = ctx.enter_context(nc.psum_tensor("ps", [P, 8, 512], F32))
        x = sb("x", [P, NT, C], F32)
        const = {"ident": sb("ident", [P, P], F32), "identb": sb("identb", [P, P], BF16),
                 "ident16": sb("ident16", [P, P], F16), "mask": sb("mask", [P, P], BF16),
                 "minus_half": sb("minus_half", [P, 1], F32), "ones": sb("ones", [P, 1], F32),
                 "eps": sb("eps", [P, 1], F32)}
        ident = const["ident"]

        with ExitStack() as c0:
            WT = sb("WT", [P, 3, HEADS + 1, HD], F32, c0)
            WoT = sb("WoT", [P, HEADS + 1, C], F32, c0)
            cosw = sb("cosw", [P, 2, NT, HD], F32, c0)
            sinw = sb("sinw", [P, 2, NT, HD], F32, c0)
            xnT = sb("xnT0", [C, T], F32, c0)
            with ExitStack() as c1:
                wqkv = sb("wqkv", [P, 3 * HEADS * HD // P, C], F32, c1)
                wo2 = sb("wo2", [C, HEADS, 2, HD], F32, c1)
                tabs = sb("tabs", [P, 2, NT, HD], F32, c1)
                normw = sb("normw", [P, 2, HD], F32, c1)
                wo_in = ins["L0_attn_wo"].rearrange("c (h e) -> c h e", e=HD)
                load_stage(nc, ps, "load0", const, x, ins["L0_attn_x"], [
                    (wqkv[:], ins["L0_attn_wqkv"].rearrange("(n p) c -> p n c", p=P)),
                    (wo2[:, :, 0, :], wo_in), (wo2[:, :, 1, :], wo_in),
                    (tabs[:], ins["rope_tab"].rearrange("a (t p) e -> p a t e", p=P)),
                    (normw[:, 0, :], ins["L0_attn_q_norm_w"].partition_broadcast(P)),
                    (normw[:, 1, :], ins["L0_attn_k_norm_w"].partition_broadcast(P))])
                causal_weights_stage(nc, ps, "cw", const, wqkv, wo2, tabs, normw, WT, WoT, cosw, sinw)
            with ExitStack() as c1:
                xn = sb("xn0", [P, NT, C], F32, c1)
                layernorm_stage(nc, ps, x, xn, xnT, ident, "ln0")
            attention_stage(nc, HeadPlan(True), "at0", ps, x, xnT, const,
                            {"WT": WT, "WoT": WoT, "cosw": cosw, "sinw": sinw})

        with ExitStack() as c0:
            xf = sb("xf", [P, NT, C], F32, c0)
            with ExitStack() as c1:
                xnT = sb("xnT1", [C, T], F32, c1)
                layernorm_stage(nc, ps, x, xf, xnT, ident, "ln1")
            xpos = sb("xpos", [P, 4, NT, HD], F32, c0)
            load_only_stage(nc, "load1", [(xpos[:], ins["xpos_tab"].rearrange("a (t p) e -> p a t e", p=P))])
            local_stage(nc, "loc", ps, xf, const, ins, {"xpos": xpos})
            add_stage(nc, "add", x, xf)

        with ExitStack() as c0:
            WqT = sb("WqT", [C, HEADS + 1, HD], F32, c0)
            WoT2 = sb("WoT2", [P, HEADS + 1, C], F32, c0)
            bqs = sb("bqs", [P, HEADS + 1, 1], F32, c0)
            kA, kB = sb("kA", [P, T], F16, c0), sb("kB", [P, T], F16, c0)
            V = sb("V", [P, NT, HD], F32, c0)
            xnT = sb("xnT2", [C, T], F32, c0)
            with ExitStack() as c1:
                xn = sb("xn2", [P, NT, C], F32, c1)
                layernorm_stage(nc, ps, x, xn, xnT, ident, "ln2")
            with ExitStack() as c1:
                wkd = sb("wkd", [C, 2, HD], F32, c1)
                wv = sb("wv", [C, HD], F32, c1)
                bkd = sb("bkd", [P, 1], F32, c1)
                bv = sb("bv", [P, HD], F32, c1)
                bq = sb("bq", [P, HEADS, 1], F32, c1)
                bo = sb("bo", [P, C], F32, c1)
                wo_in = ins["L1_attn_Wo"].rearrange("(h e) c -> e h c", e=HD)
                loads = [(WqT[:, 0:HEADS, :], ins["L1_attn_Wq"].rearrange("c (h e) -> c h e", e=HD)),
                         (wv[:], ins["L1_attn_Wv"]), (bv[:], ins["L1_attn_bv"].partition_broadcast(P)),
                         (bo[:], ins["L1_attn_bo"].partition_broadcast(P))]
                for a in range(2):
                    rows = slice(a * HD, (a + 1) * HD)
                    loads += [(wkd[:, a, :], ins["L1_attn_Wk"]), (WoT2[rows, 0:HEADS, :], wo_in),
                              (bkd[rows, :], ins["L1_attn_bk"].unsqueeze(1)),
                              (bq[rows, :, 0], ins["L1_attn_bq"].rearrange("(h e) -> e h", e=HD))]
                load_only_stage(nc, "load2", loads)
                shared_weights_stage(nc, ps, "kv", x, xnT, bo, wkd, bkd, wv, bv, bq, bqs, WqT, WoT2, kA, kB, V)
            attention_stage(nc, HeadPlan(False), "at1", ps, x, xnT, const,
                            {"WT": WqT, "WoT": WoT2, "bq": bqs, "kA": kA, "kB": kB, "V": V})

        with ExitStack() as c0:
            xnT = sb("xnT3", [C, T], F32, c0)
            with ExitStack() as c1:
                xn = sb("xn3", [P, NT, C], F32, c1)
                layernorm_stage(nc, ps, x, xn, xnT, ident, "ln3")
            experts_stage(nc, "moe", ps, x, xnT, const, ins, out)


def rope_table():
    f32 = np.float32
    inv = (f32(1.0) / np.power(f32(10000.0), np.arange(0, HD, 2, dtype=f32) / f32(HD))).astype(f32)
    angle = (np.arange(T, dtype=f32)[:, None] * inv).astype(f32)
    cos, sin = np.cos(angle).astype(f32), np.sin(angle).astype(f32)
    return np.stack([np.concatenate([cos, cos], 1), np.concatenate([-sin, sin], 1)])


def xpos_table():
    f32 = np.float32
    t = np.arange(T, dtype=f32)
    idx = np.arange(0, HD, 2, dtype=f32)
    inv = (f32(1.0) / np.power(f32(10000.0), idx / f32(HD))).astype(f32)
    angle = (t[:, None] * inv[None]).astype(f32)
    angle = np.concatenate([angle, angle], -1)
    base = ((idx + f32(0.4 * HD)) / f32(1.4 * HD)).astype(f32)
    power = ((t - T // 2) / f32(WIN // 2)).astype(f32)
    scale = np.power(base[None], power[:, None]).astype(f32)
    scale = np.concatenate([scale, scale], -1)
    cos, sin = np.cos(angle).astype(f32), np.sin(angle).astype(f32)
    sin[:, :HD // 2] *= -1
    return np.stack([cos * scale * f32(8), sin * scale * f32(8), cos / scale, sin / scale]).astype(f32)


INPUTS = (
    "L0_attn_x", "L0_attn_wqkv", "L0_attn_wo", "L0_attn_q_norm_w", "L0_attn_k_norm_w",
    "L0_ffn_wqkv", "L0_ffn_q_scale", "L0_ffn_k_scale", "L0_ffn_wo", "L0_ffn_ln_g", "L0_ffn_ln_b",
    "L0_ffn_w1", "L0_ffn_b1", "L0_ffn_w2", "L0_ffn_b2",
    "L1_attn_Wq", "L1_attn_bq", "L1_attn_Wk", "L1_attn_bk", "L1_attn_Wv", "L1_attn_bv", "L1_attn_Wo", "L1_attn_bo",
    "L1_ffn_router_w", "L1_ffn_router_b", "L1_ffn_w1", "L1_ffn_b1", "L1_ffn_w2", "L1_ffn_b2")


def kernel(**inputs):
    import concourse.bacc as bacc
    from concourse.bass_utils import run_bass_kernel_spmd

    arrays = {name: np.ascontiguousarray(inputs[name]) for name in INPUTS}
    arrays["rope_tab"] = rope_table()
    arrays["xpos_tab"] = xpos_table()
    nc = bacc.Bacc("TRN2", target_bir_lowering=False, num_devices=1)
    ins = {name: nc.dram_tensor(name, a.shape, mybir.dt.from_np(a.dtype), kind="ExternalInput").ap()
           for name, a in arrays.items()}
    out = nc.dram_tensor("out", (1, T, C), F32, kind="ExternalOutput").ap()
    build(nc, ins, out)
    result = run_bass_kernel_spmd(nc, [arrays], core_ids=[0])
    return result.results[0]["out"]
```

```python
from contextlib import ExitStack

import concourse.bass as bass
from concourse import mybir
import numpy as np

F32 = mybir.dt.float32
F16 = mybir.dt.float16
BF16 = mybir.dt.bfloat16
U32 = mybir.dt.uint32
ACT = mybir.ActivationFunctionType
ALU = mybir.AluOpType
AX_X = mybir.AxisListType.X

P = 128
T = 2048
NT = T // P
C = 128
HEADS = 16
HD = 64
QG = 4
GROUPS = NT // QG
CHUNK = 4
LN_EPS = 1e-5
RMS_EPS = 1e-6

M_UNIT = 64.0

M_BANK, M_BANKS = 0, 3
ST_BANK = 3
O_BANK = 5
OUT_BANK = 6
MAKE_BANK = 7


def make_identity(pool, tile, zeroed, done):
    pool.memset(tile[:], 0.0).then_inc(zeroed, 1)
    pool.wait_ge(zeroed, 1)
    pool.affine_select(out=tile[:], in_=tile[:], compare_op=ALU.not_equal, fill=1.0, base=0,
                       pattern=[[-1, P]], channel_multiplier=1).then_inc(done, 1)


class Sems:

    def __init__(self, nc, ctx, stage):
        self.nc, self.stage, self.held = nc, stage, []
        ctx.callback(self.free)

    def __call__(self, name):
        self.held.append(self.nc.alloc_semaphore(name=f"{self.stage}_{name}"))
        return self.held[-1]

    def free(self):
        self.nc.clear_and_free_semaphores(self.held)
        self.nc.all_engine_barrier()


def load_ahead(nc, block, loaded, loads):
    @block.sync
    def _(sp):
        with nc.allow_non_contiguous_dma(reason="some are biases, a few KB"):
            for dst, src in loads:
                sp.dma_start(dst, src).then_inc(loaded, 16)
        sp.wait_ge(loaded, 16 * len(loads))


def layernorm_stage(nc, ps, x, xn, xnT, ident, stage, loads=()):
    CH = 4
    with ExitStack() as ctx:
        sem = Sems(nc, ctx, stage)
        stats = ctx.enter_context(nc.sbuf_tensor(f"{stage}_stats", [P, NT, 6], F32))
        mv = ctx.enter_context(nc.sbuf_tensor(f"{stage}_mv", [P, NT, 2], F32))
        veps = ctx.enter_context(nc.sbuf_tensor(f"{stage}_veps", [P, NT], F32))
        rstd = ctx.enter_context(nc.sbuf_tensor(f"{stage}_rstd", [P, NT], F32))
        minus_half = ctx.enter_context(nc.sbuf_tensor(f"{stage}_mh", [P, 1], F32))
        stats_done, mv_done, veps_done = sem("stats_done"), sem("mv_done"), sem("veps_done")
        rstd_done, const_done, xn_done = sem("rstd_done"), sem("const_done"), sem("xn_done")
        turned, emptied = sem("turned"), sem("emptied")
        loaded = sem("loaded")
        block = ctx.enter_context(nc.Block())
        if loads:
            load_ahead(nc, block, loaded, loads)

        @block.vector
        def _(dve):
            for t in range(NT):
                nc.vector.bn_stats(stats[:, t, :], x[:, t, :]).then_inc(stats_done, 1)
            for t in range(NT):
                dve.wait_ge(stats_done, t + 1)
                nc.vector.bn_aggr(mv[:, t, :], stats[:, t, :]).then_inc(mv_done, 1)
            for t in range(NT):
                if t % CH == 0:
                    dve.wait_ge(rstd_done, t // CH + 1)
                    dve.wait_ge(mv_done, NT)
                nc.vector.tensor_scalar(xn[:, t, :], x[:, t, :], mv[:, t, 0:1], rstd[:, t:t + 1],
                                        ALU.subtract, ALU.mult).then_inc(xn_done, 1)

        @block.gpsimd
        def _(pool):
            pool.memset(minus_half[:], -0.5).then_inc(const_done, 1)
            pool.wait_ge(const_done, 1)
            for k in range(NT // CH):
                pool.wait_ge(mv_done, CH * k + CH)
                pool.tensor_scalar(veps[:, CH * k:CH * k + CH], mv[:, CH * k:CH * k + CH, 1], LN_EPS, 0.0,
                                   ALU.add, ALU.add).then_inc(veps_done, 1)
                pool.wait_ge(veps_done, k + 1)
                pool.tensor_tensor(rstd[:, CH * k:CH * k + CH], veps[:, CH * k:CH * k + CH],
                                   minus_half[:].to_broadcast([P, CH]), ALU.pow).then_inc(rstd_done, 1)

        @block.tensor
        def _(pe):
            for k in range(NT // CH):
                pe.wait_ge(xn_done, CH * k + CH)
                for i in range(CH):
                    mm = nc.tensor.transpose(ps[:, k, i * P:(i + 1) * P], xn[:, CH * k + i, :], ident[:])
                mm.then_inc(turned, 1)

        @block.scalar
        def _(act):
            for k in range(NT // CH):
                act.wait_ge(turned, k + 1)
                nc.scalar.activation(xnT[:, k * CH * P:(k + 1) * CH * P], ps[:, k, :], ACT.Copy)\
                    .then_inc(emptied, 1)
            act.wait_ge(emptied, NT // CH)


class HeadPlan:

    def __init__(self, causal):
        self.causal = causal
        self.steps = [(g, k) for g in range(GROUPS) for k in range(QG * (g + 1) if causal else NT)]
        self.n = n = len(self.steps)
        self.start = [self.steps.index((g, 0)) for g in range(GROUPS)] + [n]
        if causal:
            spans = [(2, 0, -2, 8), (3, 0, 8, 20), (0, 1, 26, 30), (1, 1, 30, 38), (2, 1, 38, 48)]
            fills = [(k, "qk", k) for k in range(4)] + [(9, "max", 2), (21, "max", 3), (31, "max", 0), (39, "max", 1)]
            fills += [(k, "turn", m) for m, k in enumerate((17, 19, 22, 25, 27, 29))] + [(33, "v", 0), (35, "v", 1)]
        else:
            spans = [(1, 0, -4, 12), (2, 0, 12, 28), (3, 0, 28, 44), (0, 1, 44, 60), (1, 1, 60, 76)]
            fills = [(k, "q", m) for m, k in enumerate((18, 21, 24, 27))]
            fills += [(13, "max", 1), (29, "max", 2), (45, "max", 3), (61, "max", 0)]
        self.chunks = []
        for g, ahead, a, b in spans:
            mine = [(m, c) for m in range(QG) for c in range(g + 1 if causal else NT // CHUNK)]
            for n_, (m, c) in enumerate(mine):
                step = a + n_ * (b - a) // len(mine)
                if 0 <= step < n:
                    self.chunks.append((step, g, ahead, m, c))
        self.key_chunks = [g + 1 if causal else NT // CHUNK for g in range(GROUPS)]
        self.fills = sorted(fills)
        self.sums = {"pool": [], "dve": []}
        self.taken = {}
        for g in range(GROUPS):
            kts = range(QG * (g + 1) if causal else NT)
            dve = [k for k in range(1, QG * g, 2)] if causal else [3, 6, 9, 12, 15]
            for who, mine in (("pool", [k for k in kts if k not in dve]), ("dve", dve)):
                for a, b in zip(mine, mine[1:]):
                    if a == mine[0]:
                        self.taken[self.start[g] + a] = (who, len(self.sums[who]))
                    self.taken[self.start[g] + b] = (who, len(self.sums[who]))
                    self.sums[who].append((self.start[g] + b, g, self.start[g] + a if a == mine[0] else None, self.start[g] + b))
        self.sums_before = {who: [sum(1 for x in l if x[1] < g) for g in range(GROUPS + 1)] for who, l in self.sums.items()}
        self.maxima_order = [g for _, what, g in self.fills if what == "max"]
        self.ghost_chunks = sum(1 for c in self.chunks if not c[2])
        self.ghost_maxima = sum(1 for g in self.maxima_order if not self.next_head(g))

    def next_head(self, g):
        return g in ((0, 1) if self.causal else (0,))

    def fill(self, what, m):
        return [(w, x) for _, w, x in self.fills].index((what, m))

    def first_tile(self, g, k):
        return max(0, (k - QG * g) // 2 * 2) if self.causal else 0

    def trail(self, k):
        found = [(g, k - self.start[g + 1]) for g in range(-1, GROUPS - 1)]
        return [(g, since) for g, since in found if 0 <= since <= TRAIL]


TRAIL = 7


def wait(eng, sem, value):
    if not isinstance(value, int) or value > 0:
        eng.wait_ge(sem, value)


def attention_stage(nc, plan, stage, ps, x, xnT, const, make, loads=()):
    causal = plan.causal
    NS, NM, NF = plan.n, len(plan.chunks), len(plan.fills)
    PAIRS = HEADS // 2
    RING = 8 if causal else 16
    NSUM = {who: len(plan.sums[who]) for who in plan.sums}
    ident, identb, ident16, mask = const["ident"], const["identb"], const["ident16"], const["mask"]
    WoD = make["WoD"]
    SQUARE_STEP, COS_STEP, SUM_STEP, ROT_STEP, SCALE_STEP, HI_STEP, LO_STEP = 4, 4, 6, 9, 11, 13, 15

    with ExitStack() as ctx:
        sem = Sems(nc, ctx, stage)

        def sb(name, shape, dt):
            return ctx.enter_context(nc.sbuf_tensor(f"{stage}_{name}", shape, dt))

        pT = [sb(f"pT{r}", [P, QG * P], F32) for r in range(RING)]
        pm = sb("pm", [P, GROUPS, QG, NT // CHUNK], F32)
        negm = sb("negm", [P, GROUPS, QG], F32)
        m2 = sb("m2", [P, GROUPS, QG, 2], F16)
        rden = sb("rden", [P, QG], F32)
        acc = {who: [sb(f"acc_{who}{n}", [P, QG * P], F32) for n in range(2)] for who in ("pool", "dve")}
        oT = [sb(f"oT{n}", [P, QG * P], F32) for n in range(2)]
        nought, spare = sb("nought", [P, 8], F32), sb("spare", [P, 8], F32)
        q_hl = [sb(f"q_hl{i}", [P, T], F16) for i in range(2)]
        q_hm = [sb(f"q_hm{i}", [P, T], F16) for i in range(2)]
        if causal:
            k_hh = [sb(f"k_hh{i}", [P, T], F16) for i in range(2)]
            k_lm = [sb(f"k_lm{i}", [P, T], F16) for i in range(2)]
            V = [sb(f"V{i}", [P, NT, HD], F32) for i in range(2)]
            raw = sb("raw", [P, 2, NT, HD], F32)
            sq = sb("sq", [P, 2, NT, HD], F32)
            rot = sb("rot", [P, 2, NT, HD], F32)
            sinp = sb("sinp", [P, 2, NT, HD], F32)
            ss = sb("ss", [P, 2 * NT], F32)
            rms = sb("rms", [P, 2 * NT], F32)
            rinv = sb("rinv", [P, 2 * NT], F32)
            halves = sb("halves", [P, NT, 5 * HD], F16)
        else:
            k_hh, k_lm, V = [make["k_hh"]] * 2, [make["k_lm"]] * 2, [make["V"]] * 2
            wq_h = [sb(f"wq_h{i}", [P, 2, HD], F32) for i in range(2)]
            bq_h = [sb(f"bq_h{i}", [P, 1], F32) for i in range(2)]
            qf = sb("qf", [P, 512], F32)

        filled, cleared = sem("filled"), sem("cleared")
        st_ready = sem("st_ready")
        probs_ready = sem("probs_ready")
        pv_done = sem("pv_done")
        m_ready, m_taken = sem("m_ready"), sem("m_taken")
        negm_ready, m_hi = sem("negm_ready"), sem("m_hi")
        m2_ready = sem("m2_ready")
        made, made_out = sem("made"), sem("made_out")
        added = {"pool": sem("added_pool"), "dve": sem("added_dve")}
        merged = sem("merged")
        oT_out = sem("oT_out")
        den_ready, rden_ready = sem("den_ready"), sem("rden_ready")
        y_ready, y_added = sem("y_ready"), sem("y_added")
        if causal:
            sq_ready, cos_ready, ss_ready, rms_ready = sem("sq_ready"), sem("cos_ready"), sem("ss_ready"), sem("rms_ready")
            sin_ready, rinv_ready = sem("sin_ready"), sem("rinv_ready")
            rot_ready, scaled, hi_ready, halves_ready = (sem(n) for n in ("rot_ready", "scaled", "hi_ready", "halves_ready"))
        else:
            wq_staged, q_ready = sem("wq_staged"), sem("q_ready")

        def N(i, p, per, c):
            return i * (2 * per) + ((p + 1) * per + c)

        def owner(i, p, g):
            return (i, p, g) if g >= 0 else (i, 0, GROUPS - 1) if p == 1 else (i - 1, 1, GROUPS - 1)

        def total(g):
            return acc["dve" if plan.sums_before["dve"][g + 1] > plan.sums_before["dve"][g] else "pool"][g % 2]

        def merges(g):
            return plan.sums_before["dve"][g + 1] > plan.sums_before["dve"][g]

        def add_probs(eng, namespace, who, i, p, k):
            for n, (step, g, a, b) in enumerate(plan.sums[who]):
                if step != k:
                    continue
                _, kt = plan.steps[b]
                cols = slice(plan.first_tile(g, kt) * P, QG * P)
                mine = acc[who][g % 2]
                if a is not None:
                    wait(eng, den_ready, N(i, p, GROUPS, g - 1))
                else:
                    wait(eng, added[who], N(i, p, NSUM[who], n))
                wait(eng, probs_ready, N(i, p, NS, b + 1))
                namespace.tensor_tensor(mine[:, cols], pT[a % RING][:, cols] if a is not None else mine[:, cols],
                                        pT[b % RING][:, cols], ALU.add).then_inc(added[who], 1)

        def after(i, p):
            return (i, 1) if p == 0 else (i + 1, 0)

        def at(i, p, s):
            return (i, p, s) if s < NS else (*after(i, p), s - NS)

        def fills_of(k):
            return [(n, what, m) for n, (step, what, m) in enumerate(plan.fills) if step == k]

        def operands_wait(i, p, whole):
            if causal:
                return made_out, N(i, p, NF, plan.fill("turn", 4 if whole else 1) + 1)
            return q_ready, N(i, p, 4, 4)

        loaded = sem("loaded")
        block = ctx.enter_context(nc.Block())
        if loads:
            load_ahead(nc, block, loaded, loads)

        @block.tensor
        def _(pe):
            def scores(i, p, s):
                g, kt = plan.steps[s]
                if kt == 0:
                    own = (i, p) if not plan.next_head(g) else ((i, 0) if p == 1 else (i - 1, 1))
                    wait(pe, made_out, N(*own, NF, plan.fill("max", g) + 1))
                bank = ps[:, ST_BANK + s % 2, :]
                first = plan.first_tile(g, kt)
                cols = slice((QG * g + first) * P, (QG * g + QG) * P)
                out = bank[:, first * P:QG * P]
                diagonal = causal and kt >= QG * g
                k = slice(kt * P, (kt + 1) * P)
                nc.tensor.matmul(out, k_hh[p][:, k], q_hl[p][:, cols], start=True, stop=False)
                mm = nc.tensor.matmul(out, k_lm[p][:, k], q_hm[p][:, cols], start=False, stop=not diagonal)
                if diagonal:
                    hidden = kt - QG * g - first
                    if hidden:
                        nc.tensor.matmul(bank[:, first * P:(first + 1) * P], const["mask_all"][:], identb[:], start=False, stop=False)
                    at = (first + hidden) * P
                    mm = nc.tensor.matmul(bank[:, at:at + P], mask[:], identb[:], start=False, stop=True)
                mm.then_inc(st_ready, 1)

            def for_maximum(i, p, n):
                _, g, ahead, m, c = plan.chunks[n]
                own = p if not ahead else 1 - p
                last = n - M_BANKS if n >= M_BANKS else max(c for c in range(NM) if c % M_BANKS == n) - NM
                wait(pe, m_taken, N(i, p, NM, last + 1))
                j = QG * g + m
                tiles = min(CHUNK, j + 1 - CHUNK * c) if causal else CHUNK
                diagonal = causal and c == g
                out = ps[:, M_BANK + n % M_BANKS, 0:tiles * P]
                mm = nc.tensor.matmul(out, q_hl[own][:, j * P:(j + 1) * P], k_hh[own][:, CHUNK * c * P:(CHUNK * c + tiles) * P],
                                      start=True, stop=not diagonal)
                if diagonal:
                    mm = nc.tensor.matmul(out[:, (tiles - 1) * P:tiles * P], identb[:], mask[:], start=False, stop=True)
                mm.then_inc(m_ready, 1)

            def values(i, p, s):
                g, kt = plan.steps[s]
                cols = slice(plan.first_tile(g, kt) * P, QG * P)
                for a in range(2):
                    mm = nc.tensor.matmul(ps[a * HD:(a + 1) * HD, O_BANK, cols], V[p][:, kt + a, :], pT[(s + a) % RING][:, cols],
                                          start=(kt == 0), stop=(s + 2 == plan.start[g + 1]))
                mm.then_inc(pv_done, 2)

            def trail(i, p, g, since):
                i, p, g = owner(i, p, g)
                u = N(i, p, GROUPS, g)
                if since == 4:
                    pe.wait_ge(merged, u + 1)
                    wait(pe, y_added, u)
                    for m in range(QG):
                        mm = nc.tensor.matmul(ps[:, OUT_BANK, m:m + 1], total(g)[:, m * P:(m + 1) * P], const["ones"][:],
                                              start=True, stop=True)
                    mm.then_inc(den_ready, 1)
                if since == 6:
                    pe.wait_ge(oT_out, u + 1)
                    pe.wait_ge(rden_ready, u + 1)
                    for m in range(QG):
                        mm = nc.tensor.matmul(ps[:, OUT_BANK, m * P:(m + 1) * P], oT[g % 2][:, m * P:(m + 1) * P], WoD[:, i * 2 + (p + 1), :],
                                              start=True, stop=True)
                    mm.then_inc(y_ready, 1)

            def fill(i, p, n, what, m):
                wait(pe, made_out, N(i, p, NF, n))
                bank = ps[:, MAKE_BANK, :]
                bank16 = bank.bitcast(F16)
                head = after(i, p)
                if what == "qk":
                    for a in range(4):
                        t = 4 * m + a
                        mm = nc.tensor.matmul(bank[:, a * P:(a + 1) * P], xnT[:, t * P:(t + 1) * P],
                                              make["WT"][:, 0:2, head[0] * 2 + head[1], :], start=True, stop=True)
                elif what == "v":
                    for a in range(8):
                        t = 8 * m + a
                        mm = nc.tensor.matmul(bank[:, a * HD:(a + 1) * HD], xnT[:, t * P:(t + 1) * P],
                                              make["WT"][:, 2, head[0] * 2 + head[1], :], start=True, stop=True)
                elif what == "q":
                    wait(pe, wq_staged, N(i, p, 3, 3))
                    mm = nc.tensor.matmul(bank, wq_h[head[1]][:].rearrange("p a e -> p (a e)"),
                                          xnT[:, m * 512:(m + 1) * 512], start=True, stop=True)
                elif what == "turn":
                    if m < 2:
                        wait(pe, halves_ready, N(i, p, 2, m + 1))
                    if m == 1:
                        wait(pe, hi_ready, N(i, p, 3, 3))
                    kind, half = m % 3, m // 3
                    off = (0, 3 * HD, 2 * HD)[kind]
                    for a in range(8):
                        mm = nc.tensor.transpose(bank16[:, a * P:(a + 1) * P], halves[:, 8 * half + a, off:off + P], ident16[:])
                else:
                    wait(pe, m2_ready, N(i, p, GROUPS, plan.maxima_order.index(m) + 1))
                    for a in range(QG):
                        mm = nc.tensor.transpose(bank16[HD:HD + 2, a * P:(a + 1) * P], m2[:, m, a, :], ident16[:])
                mm.then_inc(made, 1)

            def body_step(i, p, k, ghost=False):
                if not ghost or k + 2 >= NS:
                    wait(pe, probs_ready, N(i, p, NS, k + 1))
                    scores(*at(i, p, k + 2))
                for n, (step, _, ahead, _, _) in enumerate(plan.chunks):
                    if step == k and (ahead or not ghost):
                        if n == plan.ghost_chunks:
                            wait(pe, *operands_wait(i, p, not causal))
                        if causal and plan.chunks[n][1:5] == (2, 1, 0, 0):
                            wait(pe, *operands_wait(i, p, True))
                        for_maximum(i, p, n)
                for n, what, m in fills_of(k):
                    fill(i, p, n, what, m)
                if not ghost:
                    for g, since in plan.trail(k):
                        trail(i, p, g, since)
                    if k % 2 == 1:
                        if plan.steps[k][1] == 1:
                            wait(pe, oT_out, N(i, p, GROUPS, plan.steps[k][0]))
                        values(i, p, k - 1)

            pe.wait_ge(cleared, 1)
            for n, (counted, credit) in enumerate(((st_ready, NS), (pv_done, NS), (m_ready, plan.ghost_chunks),
                                                   (den_ready, GROUPS - 1), (y_ready, GROUPS - 1))):
                nc.tensor.transpose(ps[:, OUT_BANK, 0:P], ident[:], ident[:]).then_inc(counted, credit)
            for k in range(NS):
                body_step(-1, 1, k, ghost=True)
            with pe.Fori(0, PAIRS) as i:
                for p in range(2):
                    for k in range(NS):
                        body_step(i, p, k)
            for since in range(TRAIL + 1):
                trail(PAIRS, 0, -1, since)

        @block.vector
        def _(dve):
            def maximum(i, p, n):
                _, g, _, m, c = plan.chunks[n]
                j = QG * g + m
                tiles = min(CHUNK, j + 1 - CHUNK * c) if causal else CHUNK
                dve.wait_ge(m_ready, N(i, p, NM, n + 1))
                nc.vector.tensor_reduce(pm[:, g, m, c:c + 1], ps[:, M_BANK + n % M_BANKS, 0:tiles * P], AX_X, ALU.max).then_inc(m_taken, 1)

            def maxima(i, p, n, g):
                u = N(i, p, GROUPS, plan.maxima_order.index(g) + 1)
                dve.wait_ge(m_taken, N(i, p, NM, n + 1))
                nc.vector.tensor_reduce(negm[:, g], pm[:, g, :, 0:plan.key_chunks[g]], AX_X, ALU.max, negate=True).then_inc(negm_ready, 1)
                wait(dve, made, N(i, p, NF, plan.fill("max", g) + 1 - NF))
                dve.wait_ge(negm_ready, u)
                nc.vector.tensor_scalar(m2[:, g, :, 0], negm[:, g], 1 / M_UNIT, 0.0, ALU.mult, ALU.add).then_inc(m_hi, 1)
                dve.wait_ge(m_hi, u)
                nc.vector.scalar_tensor_tensor(out=m2[:, g, :, 1], in0=negm[:, g], scalar=1 / M_UNIT, in1=m2[:, g, :, 0],
                                               op0=ALU.mult, op1=ALU.subtract).then_inc(m2_ready, 1)

            def trail(i, p, g, since):
                i, p, g = owner(i, p, g)
                u = N(i, p, GROUPS, g)
                if since == 3:
                    dve.wait_ge(added["pool"], N(i, p, NSUM["pool"], plan.sums_before["pool"][g + 1]))
                    if merges(g):
                        wait(dve, added["dve"], N(i, p, NSUM["dve"], plan.sums_before["dve"][g + 1]))
                        nc.vector.tensor_tensor(acc["dve"][g % 2][:], acc["dve"][g % 2][:], acc["pool"][g % 2][:], ALU.add).then_inc(merged, 1)
                    else:
                        nc.vector.memset(spare[:, 0:1], 0.0).then_inc(merged, 1)
                if since == 5:
                    dve.wait_ge(den_ready, u + 1)
                    nc.vector.reciprocal(rden[:], ps[:, OUT_BANK, 0:QG]).then_inc(rden_ready, 1)
                if since == 7:
                    dve.wait_ge(y_ready, u + 1)
                    dve.wait_ge(rden_ready, u + 1)
                    for m in range(QG):
                        t = QG * g + m
                        op = nc.vector.scalar_tensor_tensor(out=x[:, t, :], in0=ps[:, OUT_BANK, m * P:(m + 1) * P], scalar=rden[:, m:m + 1],
                                                            in1=x[:, t, :], op0=ALU.mult, op1=ALU.add)
                    op.then_inc(y_added, 1)

            def rotate(i, p, k):
                last = N(i, p, 2, 0)
                for a in range(2):
                    cols = slice(a * NT, (a + 1) * NT)
                    if k == COS_STEP + a:
                        wait(dve, halves_ready, last)
                        wait(dve, made_out, N(i, p, NF, plan.fill("qk", 3) + 1))
                        nc.vector.tensor_tensor(rot[:, a], raw[:, a], make["cosw"][:, a], ALU.mult).then_inc(cos_ready, 1)
                    if k == SUM_STEP + a:
                        wait(dve, sq_ready, last + a + 1)
                        if a == 0:
                            wait(dve, rinv_ready, N(i, p, 1, 0))
                        nc.vector.tensor_reduce(ss[:, cols], sq[:, a], AX_X, ALU.add).then_inc(ss_ready, 1)
                        wait(dve, ss_ready, last + a + 1)
                        nc.vector.tensor_scalar(rms[:, cols], ss[:, cols], 1.0 / HD, RMS_EPS, ALU.mult, ALU.add).then_inc(rms_ready, 1)
                    if k == ROT_STEP + a:
                        wait(dve, sin_ready, last + 2)
                        wait(dve, cos_ready, last + a + 1)
                        nc.vector.tensor_tensor(rot[:, a], rot[:, a], sinp[:, a], ALU.add).then_inc(rot_ready, 1)
                    if k == SCALE_STEP + a:
                        wait(dve, rinv_ready, N(i, p, 1, 1))
                        wait(dve, rot_ready, last + a + 1)
                        nc.vector.tensor_tensor(rot[:, a], rot[:, a], rinv[:, cols].unsqueeze(2).to_broadcast([P, NT, HD]), ALU.mult)\
                            .then_inc(scaled, 1)
                    if k == LO_STEP + a:
                        wait(dve, hi_ready, N(i, p, 3, a + 1))
                        at = (HD, 2 * HD)[a]
                        nc.vector.tensor_tensor(halves[:, :, at:at + HD], rot[:, a], halves[:, :, (0, 3 * HD)[a]:(HD, 4 * HD)[a]], ALU.subtract)\
                            .then_inc(halves_ready, 1)

            def body_step(i, p, k, ghost=False):
                if not ghost:
                    for g, since in plan.trail(k):
                        trail(i, p, g, since)
                for n, (step, g, ahead, m, c) in enumerate(plan.chunks):
                    if step == k and (ahead or not ghost):
                        maximum(i, p, n)
                        if m == QG - 1 and c == plan.key_chunks[g] - 1:
                            maxima(i, p, n, g)
                if not ghost:
                    add_probs(dve, nc.vector, "dve", i, p, k)
                if causal:
                    rotate(i, p, k)

            dve.wait_ge(cleared, 1)
            nc.vector.memset(ps[:, O_BANK, :], 1.0)
            for n, (counted, credit) in enumerate(((m_taken, plan.ghost_chunks), (negm_ready, plan.ghost_maxima), (m_hi, plan.ghost_maxima),
                                                   (m2_ready, plan.ghost_maxima), (merged, GROUPS - 1), (rden_ready, GROUPS - 1),
                                                   (y_added, GROUPS - 1), (added["dve"], NSUM["dve"]))):
                nc.vector.memset(spare[:, n:n + 1], 0.0).then_inc(counted, credit)
            for k in range(NS):
                body_step(-1, 1, k, ghost=True)
            with dve.Fori(0, PAIRS) as i:
                for p in range(2):
                    for k in range(NS):
                        body_step(i, p, k)
            for since in range(TRAIL + 1):
                trail(PAIRS, 0, -1, since)

        @block.scalar
        def _(act):
            def exps(i, p, s):
                g, kt = plan.steps[s]
                first = plan.first_tile(g, kt)
                act.wait_ge(st_ready, N(i, p, NS, s + 1))
                wait(act, pv_done, N(i, p, NS, s + 1 - RING))
                old, back = (s - RING, 0) if s >= RING else (s - RING + NS, 1)
                who, n = plan.taken[old]
                wait(act, added[who], N(i, p, NSUM[who], n + 1 - back * NSUM[who]))
                nc.scalar.activation(pT[s % RING][:, first * P:QG * P], ps[:, ST_BANK + s % 2, first * P:QG * P], ACT.Exp)\
                    .then_inc(probs_ready, 1)

            def fill_out(i, p, n, what, m):
                act.wait_ge(made, N(i, p, NF, n + 1))
                bank = ps[:, MAKE_BANK, :]
                bank16 = bank.bitcast(F16)
                own = after(i, p)[1]
                if what == "qk":
                    if m == 0:
                        wait(act, cos_ready, N(i, p, 2, 0))
                        wait(act, sin_ready, N(i, p, 2, 0))
                    op = nc.scalar.activation(raw[:, :, 4 * m:4 * m + 4, :].rearrange("p a t e -> p t a e"),
                                              bank.rearrange("p (t a e) -> p t a e", a=2, e=HD), ACT.Copy)
                elif what == "v":
                    op = nc.scalar.activation(V[own][:, 8 * m:8 * m + 8, 0:HD], bank.rearrange("p (t e) -> p t e", e=HD), ACT.Copy)
                elif what == "q":
                    wait(act, q_ready, N(i, p, 4, m))
                    cols = slice(m * 512, (m + 1) * 512)
                    bias = bq_h[own]
                    nc.scalar.activation(q_hl[own][:, cols], bank, ACT.Identity, bias=bias[:], scale=HD ** -0.5)
                    op = nc.scalar.activation(qf[HD:P, :], bank[HD:P, :], ACT.Identity, bias=bias[HD:P], scale=HD ** -0.5)
                elif what == "turn":
                    kind, half = m % 3, m // 3
                    cols = slice(half * 1024, (half + 1) * 1024)
                    if kind == 0:
                        op = nc.scalar.activation(q_hl[own][:, cols], bank16, ACT.Copy)
                    elif kind == 1:
                        op = nc.scalar.activation(k_hh[own][:, cols], bank16, ACT.Copy)
                    else:
                        op = nc.scalar.activation(k_lm[own][0:HD, cols], bank16[0:HD], ACT.Copy)
                else:
                    dst = q_hm[own if plan.next_head(m) else p]
                    op = nc.scalar.activation(dst[HD:HD + 2, QG * m * P:QG * (m + 1) * P], bank16[HD:HD + 2, 0:QG * P], ACT.Copy)
                op.then_inc(made_out, 1)

            def trail(i, p, g, since):
                i, p, g = owner(i, p, g)
                u = N(i, p, GROUPS, g)
                if since == 0:
                    act.wait_ge(pv_done, N(i, p, NS, plan.start[g + 1]))
                    wait(act, y_ready, u - 1)
                    nc.scalar.activation(oT[g % 2][:], ps[:, O_BANK, :], ACT.Copy).then_inc(oT_out, 1)

            def body_step(i, p, k, ghost=False):
                if not ghost or k + 1 >= NS:
                    exps(*at(i, p, k + 1))
                for n, what, m in fills_of(k):
                    fill_out(i, p, n, what, m)
                for a in range(2 if causal else 0):
                    if k == HI_STEP + a:
                        last = N(i, p, 2, 0)
                        wait(act, made, N(i, p, NF, plan.fill("turn", 5) + 1 - NF))
                        wait(act, scaled, last + a + 1)
                        col = (0, 3 * HD)[a]
                        nc.scalar.activation(halves[:, :, col:col + HD], rot[:, a], ACT.Copy).then_inc(hi_ready, 1)
                    if k == SQUARE_STEP + a:
                        wait(act, ss_ready, N(i, p, 2, 0))
                        act.wait_ge(made_out, N(i, p, NF, plan.fill("qk", 3) + 1))
                        nc.scalar.activation(sq[:, a], raw[:, a], ACT.Square).then_inc(sq_ready, 1)
                if causal and k == HI_STEP + 2:
                    nc.scalar.activation(halves[:, :, 4 * HD:5 * HD], rot[:, 1], ACT.Copy).then_inc(hi_ready, 1)
                for n in range(2 if causal else 4):
                    place = plan.fill(*(("turn", 3 * n) if causal else ("q", n)))
                    if k == plan.fills[place][0] + 1:
                        own, width = after(i, p)[1], T // (2 if causal else 4)
                        cols = slice(n * width, (n + 1) * width)
                        act.wait_ge(made_out, N(i, p, NF, place + 1))
                        nc.scalar.activation(q_hm[own][0:HD, cols], q_hl[own][0:HD, cols], ACT.Copy)
                if not ghost:
                    for g, since in plan.trail(k):
                        trail(i, p, g, since)

            act.wait_ge(cleared, 1)
            for n, (counted, credit) in enumerate(((probs_ready, NS), (oT_out, GROUPS - 1))):
                nc.scalar.activation(nought[:, n + 1:n + 2], nought[:, 0:1], ACT.Copy).then_inc(counted, credit)
            for k in range(NS):
                body_step(-1, 1, k, ghost=True)
            with act.Fori(0, PAIRS) as i:
                for p in range(2):
                    for k in range(NS):
                        body_step(i, p, k)
            trail(PAIRS, 0, -1, 0)

        @block.gpsimd
        def _(pool):
            def rotate(i, p, k):
                half = HD // 2
                sinw = make["sinw"]
                if k == COS_STEP:
                    wait(pool, rot_ready, N(i, p, 2, 0))
                    pool.wait_ge(made_out, N(i, p, NF, plan.fill("qk", 3) + 1))
                    pool.tensor_tensor(sinp[:, :, :, 0:half], raw[:, :, :, half:HD], sinw[:, :, :, 0:half], ALU.mult).then_inc(sin_ready, 1)
                    pool.tensor_tensor(sinp[:, :, :, half:HD], raw[:, :, :, 0:half], sinw[:, :, :, half:HD], ALU.mult).then_inc(sin_ready, 1)
                if k == SUM_STEP + 2:
                    wait(pool, scaled, N(i, p, 2, 0))
                    pool.wait_ge(rms_ready, N(i, p, 2, 2))
                    pool.tensor_tensor(rinv[:], rms[:], const["minus_half"][:].to_broadcast([P, 2 * NT]), ALU.pow).then_inc(rinv_ready, 1)

            def stage_wq(i, p):
                head = after(i, p)
                own = head[1]
                wait(pool, made_out, N(i, p, NF, 0))
                for a in range(2):
                    pool.tensor_copy(wq_h[own][:, a, :], make["WT"][:, head[0] * 2 + own, :]).then_inc(wq_staged, 1)
                pool.tensor_copy(bq_h[own][:], make["bq"][:, head[0] * 2 + own, :]).then_inc(wq_staged, 1)

            def low_q(i, p, m):
                own = after(i, p)[1]
                cols = slice(m * 512, (m + 1) * 512)
                pool.wait_ge(made_out, N(i, p, NF, plan.fill("q", m) + 1))
                pool.tensor_tensor(q_hl[own][HD:P, cols], qf[HD:P, :], q_hl[own][HD:P, cols], ALU.subtract).then_inc(q_ready, 1)
                pool.wait_ge(q_ready, N(i, p, 4, m + 1))

            def body_step(i, p, k, ghost=False):
                if k == 0 and not causal:
                    stage_wq(i, p)
                if not ghost:
                    add_probs(pool, pool, "pool", i, p, k)
                for n, what, m in fills_of(k):
                    if what == "q":
                        if not ghost:
                            pool.wait_ge(added["pool"], N(i, p, NSUM["pool"], sum(1 for x in plan.sums["pool"] if x[0] <= k)))
                        low_q(i, p, m)
                if causal:
                    rotate(i, p, k)

            fillings = [(m2[:], 0.0), (nought[:], 0.0), (q_hm[0][HD:P, :], 0.0), (q_hm[1][HD:P, :], 0.0), (acc["dve"][1][:], 1.0),
                        (acc["pool"][1][:], 1.0)]
            if causal:
                for n in range(2):
                    fillings += [(k_lm[n][HD:P, :], 0.0), (k_lm[n][HD:HD + 2, :], M_UNIT)]
            for n, (part, value) in enumerate(fillings):
                pool.memset(part, value).then_inc(filled, 1)
                pool.wait_ge(filled, n + 1)
            pool.memset(nought[:, 6:7], 0.0).then_inc(cleared, 1)
            pool.memset(nought[:, 7:8], 0.0).then_inc(added["pool"], NSUM["pool"])
            for k in range(NS):
                body_step(-1, 1, k, ghost=True)
            with pool.Fori(0, PAIRS) as i:
                for p in range(2):
                    for k in range(NS):
                        body_step(i, p, k)


def load_stage(nc, ps, stage, const, x, x_in, loads):
    with ExitStack() as ctx:
        sem = Sems(nc, ctx, stage)
        loaded = sem("loaded")
        names = ("ident", "identb", "ident16")
        zeroed = {n: sem(f"zeroed_{n}") for n in names}
        made = {n: sem(f"made_{n}") for n in names}
        mask_zeroed, mask_made, half_made = sem("mask_zeroed"), sem("mask_made"), sem("half_made")
        block = ctx.enter_context(nc.Block())

        @block.sync
        def _(sp):
            sp.dma_start(x[:], x_in[0].rearrange("(t p) c -> p t c", p=P)).then_inc(loaded, 16)
            for dst, src in loads:
                sp.dma_start(dst, src).then_inc(loaded, 16)
            sp.wait_ge(loaded, 16 * (1 + len(loads)))

        @block.gpsimd
        def _(pool):
            for n in names:
                make_identity(pool, const[n], zeroed[n], made[n])
            pool.memset(const["mask"][:], 0.0).then_inc(mask_zeroed, 1)
            pool.wait_ge(mask_zeroed, 1)
            pool.affine_select(out=const["mask"][:], in_=const["mask"][:], compare_op=ALU.is_ge, fill=-1e30,
                               base=0, pattern=[[-1, P]], channel_multiplier=1).then_inc(mask_made, 1)
            pool.memset(const["mask_all"][:], -1e30)
            pool.memset(const["ones"][:], 1.0)
            pool.memset(const["eps"][:], LN_EPS)
            pool.memset(const["minus_half"][:], -0.5).then_inc(half_made, 1)
            for n in names:
                pool.wait_ge(made[n], 1)
            pool.wait_ge(mask_made, 1)
            pool.wait_ge(half_made, 1)


def causal_weights_stage(nc, ps, stage, const, wqkv, wo2, tabs, normw, WT, WoD, cosw, sinw):
    NW = 3 * HEADS * HD // P
    with ExitStack() as ctx:
        sem = Sems(nc, ctx, stage)
        turned, emptied, padded, tabled = sem("turned"), sem("emptied"), sem("padded"), sem("tabled")
        block = ctx.enter_context(nc.Block())
        jobs = [("qkv", f) for f in range(NW // 4)] + [("o", f) for f in range(HEADS // 4)]

        @block.tensor
        def _(pe):
            for n, (what, f) in enumerate(jobs):
                if n >= 8:
                    pe.wait_ge(emptied, n - 7)
                for m in range(4):
                    src = wqkv[:, 4 * f + m, :] if what == "qkv" else wo2[:, 4 * f + m].rearrange("p a e -> p (a e)")
                    mm = nc.tensor.transpose(ps[:, n % 8, m * P:(m + 1) * P], src, const["ident"][:])
                mm.then_inc(turned, 1)

        @block.scalar
        def _(act):
            for n, (what, f) in enumerate(jobs):
                act.wait_ge(turned, n + 1)
                if what == "qkv":
                    dst = WT[:, f // 2, 8 * (f % 2):8 * (f % 2) + 8, :].rearrange("p h e -> p (h e)")
                else:
                    dst = WoD[:, 1 + 4 * f:5 + 4 * f, :].rearrange("p h e -> p (h e)")
                nc.scalar.activation(dst, ps[:, n % 8, :], ACT.Copy).then_inc(emptied, 1)
            act.wait_ge(emptied, len(jobs))

        @block.gpsimd
        def _(pool):
            pool.memset(WT[:, :, HEADS, :], 0.0).then_inc(padded, 1)
            pool.memset(WoD[:, 0, :], 0.0).then_inc(padded, 1)
            pool.wait_ge(padded, 2)

        @block.vector
        def _(dve):
            half = HD // 2
            for a in range(2):
                scale = HD ** -0.5 if a == 0 else 1.0
                w = normw[:, a, :].unsqueeze(1)
                for dst, tab, cols, wcols in ((cosw, 0, slice(0, HD), slice(0, HD)),
                                              (sinw, 1, slice(0, half), slice(half, HD)),
                                              (sinw, 1, slice(half, HD), slice(0, half))):
                    nc.vector.scalar_tensor_tensor(
                        out=dst[:, a, :, cols], in0=tabs[:, tab, :, cols], scalar=scale,
                        in1=w[:, :, wcols].to_broadcast([P, NT, wcols.stop - wcols.start]),
                        op0=ALU.mult, op1=ALU.mult).then_inc(tabled, 1)
            dve.wait_ge(tabled, 6)


LAYERS = 2
LH = 8
WIN = 64
INNER = LH * HD
HID = C * 4 * 2 // 3
HCH = [(c, min(P, HID - c)) for c in range(0, HID, P)]


def local_stage(nc, stage, ps, xf, const, ins, rows, loads=()):
    LAG_S, LAG_O = 2, 4
    RQ, RV, RP = 3, 5, 3
    B_Q, B_K, B_V, B_QT, B_KT, B_S, B_X = 0, 1, 2, 3, 4, 5, 7

    with ExitStack() as ctx:
        sem = Sems(nc, ctx, stage)

        def sb(name, shape, dt):
            return ctx.enter_context(nc.sbuf_tensor(f"{stage}_{name}", shape, dt))

        wqkv = sb("wqkv", [P, 3 * INNER], F32)
        wo = sb("wo", [P, INNER // P, C], F32)
        w1 = sb("w1", [P, 2 * HID], F32)
        w2 = sb("w2", [P, len(HCH), C], F32)
        b1 = sb("b1", [P, 2, len(HCH)], F32)
        lng, lnb = sb("lng", [P, 1], F32), sb("lnb", [P, 1], F32)
        b2 = sb("b2", [P, C], F32)
        qks = sb("qks", [P, 2, HD], F32)
        tab = rows["xpos"]
        wtab = sb("wtab", [P, 4, NT, HD], F32)
        hT = sb("hT", [C, T + 1], F32)
        raw = [sb(f"raw{n}", [P, 2, LH, HD], F32) for n in range(2)]
        sq = [sb(f"sq{n}", [P, 2, LH, HD], F32) for n in range(2)]
        qk = [sb(f"qk{n}", [P, 2, LH, HD], F32) for n in range(RQ)]
        ss = [sb(f"ss{n}", [P, 2 * LH], F32) for n in range(2)]
        ssc = [sb(f"ssc{n}", [P, 2 * LH], F32) for n in range(2)]
        rinv = [sb(f"rinv{n}", [P, 2 * LH], F32) for n in range(2)]
        V = [sb(f"v{n}", [P, INNER], F32) for n in range(RV)]
        Vs = [sb(f"vs{n}", [P, INNER], F32) for n in range(RV)]
        qT = [sb(f"qT{n}", [P, LH // 2, P], F32) for n in range(2)]
        kT = [sb(f"kT{n}", [P, LH // 2, WIN + P], F32) for n in range(2)]
        probs = [sb(f"probs{n}", [P, LH, P], F32) for n in range(RP)]
        negm = [sb(f"negm{n}", [P, LH], F32) for n in range(2)]
        sums = [sb(f"sums{n}", [P, LH], F32) for n in range(2)]
        rsum = [sb(f"rsum{n}", [P, LH], F32) for n in range(2)]
        pT = [sb(f"pT{n}", [P, LH, P], F32) for n in range(2)]
        oT = [sb(f"oT{n}", [P, INNER // P, P], F32) for n in range(2)]
        mask = sb("mask", [P, 2, P], BF16)
        h = sb("h", [P, NT, C], F32)
        hn = [sb(f"hn{n}", [P, QG, C], F32) for n in range(2)]
        stats = sb("stats", [P, NT, 6], F32)
        mv = sb("mv", [P, NT, 2], F32)
        veps = sb("veps", [P, NT], F32)
        rstd = sb("rstd", [P, NT], F32)
        hnT = [sb(f"hnT{n}", [C, QG * P], F32) for n in range(2)]
        gl = [sb(f"gl{n}", [P, QG * P], F32) for n in range(2)]
        hh = [[sb(f"hh{n}_{c}", [P, QG * P], F32) for c in range(len(HCH))] for n in range(2)]

        cleared, masked = sem("cleared"), sem("masked")
        loaded = sem("loaded")
        w_in = sem("w_in")
        f_in = sem("f_in")
        tabled = sem("tabled")
        xT_turned, xT_out = sem("xT_turned"), sem("xT_out")
        qk_ready, v_ready = sem("qk_ready"), sem("v_ready")
        raw_ready, sq_ready, v_out = sem("raw_ready"), sem("sq_ready"), sem("v_out")
        v_shifted = [sem(f"v_shifted{n}") for n in range(RV)]
        ss_ready, ssc_ready, rinv_ready = sem("ss_ready"), sem("ssc_ready"), sem("rinv_ready")
        cos_ready, sinA_ready, sinB_ready = sem("cos_ready"), sem("sinA_ready"), sem("sinB_ready")
        rot_ready, qk_scaled = sem("rot_ready"), sem("qk_scaled")
        qkT_turned, qT_out = sem("qkT_turned"), sem("qT_out")
        s_ready, negm_ready, probs_ready, rsum_ready, p_scaled = (sem(n) for n in ("s_ready", "negm_ready", "probs_ready", "rsum_ready", "p_scaled"))
        pT_turned, pT_outA, pT_outB = sem("pT_turned"), sem("pT_outA"), sem("pT_outB")
        o_ready, o_out, y_ready, y_added = sem("o_ready"), sem("o_out"), sem("y_ready"), sem("y_added")
        h_copied, h_shifted, b2_added = sem("h_copied"), sem("h_shifted"), sem("b2_added")
        stats_ready, mv_ready, veps_ready, rstd_ready, hn_ready = (sem(n) for n in ("stats_ready", "mv_ready", "veps_ready", "rstd_ready", "hn_ready"))
        hnT_turned, hnT_out = sem("hnT_turned"), sem("hnT_out")
        g_ready, g_out, a_ready, hh_ready = sem("g_ready"), sem("g_out"), sem("a_ready"), sem("hh_ready")
        f_ready, f_added = sem("f_ready"), sem("f_added")
        NCH = len(HCH)

        block = ctx.enter_context(nc.Block())

        def shifted(i, j):
            return i * (32 * len(range(j % RV, NT, RV))) + 32 * (j // RV + 1)

        def steps():
            return range(-1, NT + LAG_O)

        @block.sync
        def _(sp):
            with nc.allow_non_contiguous_dma(reason="some are biases, a few KB"):
                for dst, src in loads:
                    sp.dma_start(dst, src).then_inc(loaded, 16)
            if loads:
                sp.wait_ge(loaded, 16 * len(loads))
            with sp.Fori(0, LAYERS) as i:
                sp.wait_ge(cleared, i + 1)
                sp.dma_start(wqkv[:], ins["L0_ffn_wqkv"][bass.ds(i, 1)].rearrange("a p n -> (a p) n")).then_inc(w_in, 16)
                sp.dma_start(wo[:], ins["L0_ffn_wo"][bass.ds(i, 1)].rearrange("a (k p) n -> p (a k) n", p=P)).then_inc(w_in, 16)
                sp.dma_start(qks[:, 0, :], ins["L0_ffn_q_scale"][bass.ds(i, 1)].rearrange("a e -> (a e)").partition_broadcast(P)).then_inc(w_in, 16)
                sp.dma_start(qks[:, 1, :], ins["L0_ffn_k_scale"][bass.ds(i, 1)].rearrange("a e -> (a e)").partition_broadcast(P)).then_inc(w_in, 16)
                sp.dma_start(w1[:], ins["L0_ffn_w1"][bass.ds(i, 1)].rearrange("a p n -> (a p) n")).then_inc(f_in, 16)
                for n, (c, m) in enumerate(HCH):
                    sp.dma_start(w2[0:m, n, :], ins["L0_ffn_w2"][bass.ds(i, 1), c:c + m, :].rearrange("a p n -> (a p) n")).then_inc(f_in, 16)
                    for a in range(2):
                        sp.dma_start(b1[0:m, a, n:n + 1], ins["L0_ffn_b1"][bass.ds(i, 1), a * HID + c:a * HID + c + m].rearrange("a p -> p a")).then_inc(f_in, 16)
                sp.dma_start(lng[:], ins["L0_ffn_ln_g"][bass.ds(i, 1)].rearrange("a p -> p a")).then_inc(f_in, 16)
                sp.dma_start(lnb[:], ins["L0_ffn_ln_b"][bass.ds(i, 1)].rearrange("a p -> p a")).then_inc(f_in, 16)
                sp.dma_start(b2[:], ins["L0_ffn_b2"][bass.ds(i, 1)].rearrange("a e -> (a e)").partition_broadcast(P)).then_inc(f_in, 16)
                for j in range(NT):
                    sp.wait_ge(v_out, i * NT + j + 1)
                    if j >= RV:
                        sp.wait_ge(o_ready, i * NT + j - RV + 1)
                    sp.dma_start(Vs[j % RV][0:WIN, :], V[max(j - 1, 0) % RV][WIN:P, :]).then_inc(v_shifted[j % RV], 16)
                    sp.dma_start(Vs[j % RV][WIN:P, :], V[j % RV][0:WIN, :]).then_inc(v_shifted[j % RV], 16)
                sp.wait_ge(y_added, i * NT + NT)
                sp.dma_start(h[1:P, :, C // 2:C], xf[0:P - 1, :, C // 2:C]).then_inc(h_shifted, 16)
                sp.dma_start(h[0:1, 1:NT, C // 2:C], xf[P - 1:P, 0:NT - 1, C // 2:C]).then_inc(h_shifted, 16)
        F_IN = 16 * (1 + NCH * 3 + 3)

        @block.gpsimd
        def _(pool):
            setup = []

            def then(op):
                setup.append(op)
                op.then_inc(masked, 1)
                pool.wait_ge(masked, len(setup))

            then(pool.memset(mask[:], 0.0))
            then(pool.memset(hT[C // 2:C, 0:1], 0.0))
            then(pool.memset(h[0:1, 0, C // 2:C], 0.0))
            for n in range(2):
                for w in range(2):
                    part = mask[w * WIN:(w + 1) * WIN, n, :]
                    then(pool.affine_select(out=part, in_=part, compare_op=ALU.is_ge, fill=-1e30, base=WIN,
                                            pattern=[[-1, P]], channel_multiplier=1))
                    then(pool.affine_select(out=part, in_=part, compare_op=ALU.is_ge, fill=-1e30, base=0,
                                            pattern=[[1, P]], channel_multiplier=-1))
            pool.affine_select(out=mask[0:WIN, 0, :], in_=mask[0:WIN, 0, :], compare_op=ALU.is_ge, fill=-1e30,
                               base=-WIN, pattern=[[1, P]], channel_multiplier=0).then_inc(cleared, 1)
            pool.wait_ge(cleared, 1)
            with pool.Fori(0, LAYERS) as i:
                for tau in steps():
                    j = tau - LAG_S - 1
                    if 0 <= j < NT:
                        pool.wait_ge(rsum_ready, i * NT + j + 1)
                        pool.tensor_tensor(probs[j % RP][:], probs[j % RP][:], rsum[j % 2][:].unsqueeze(2).to_broadcast([P, LH, P]),
                                           ALU.mult).then_inc(p_scaled, 1)
                    j = tau
                    if 0 <= j < NT:
                        half = HD // 2
                        w = wtab[:, :, j, :].unsqueeze(2)
                        pool.wait_ge(raw_ready, i * NT + j + 1)
                        pool.wait_ge(tabled, i * 6 + 6)
                        pool.wait_ge(ss_ready, i * NT + j + 1)
                        pool.tensor_tensor(sq[j % 2][:, :, :, half:HD], raw[j % 2][:, :, :, 0:half],
                                           w[:, 1:4:2, :, half:HD].to_broadcast([P, 2, LH, half]), ALU.mult).then_inc(sinB_ready, 1)
                        pool.wait_ge(ssc_ready, i * NT + j + 1)
                        pool.tensor_tensor(rinv[j % 2][:], ssc[j % 2][:], const["minus_half"][:].to_broadcast([P, 2 * LH]), ALU.pow)\
                            .then_inc(rinv_ready, 1)
                pool.wait_ge(y_added, i * NT + NT)
                pool.tensor_tensor(h[:, :, 0:C // 2], xf[:, :, 0:C // 2], const["ones"][:].unsqueeze(2).to_broadcast([P, NT, C // 2]), ALU.mult).then_inc(h_copied, 1)
                pool.wait_ge(f_in, i * F_IN + F_IN)
                pool.wait_ge(h_copied, i + 1)
                pool.wait_ge(h_shifted, i * 32 + 32)
                for g in range(GROUPS):
                    pool.wait_ge(mv_ready, i * NT + QG * g + QG)
                    cols = slice(QG * g, QG * g + QG)
                    pool.tensor_tensor(veps[:, cols], mv[:, cols, 1], const["eps"][:].to_broadcast([P, QG]), ALU.add).then_inc(veps_ready, 1)
                    pool.wait_ge(veps_ready, i * GROUPS + g + 1)
                    pool.tensor_tensor(rstd[:, cols], veps[:, cols], const["minus_half"][:].to_broadcast([P, QG]), ALU.pow)\
                        .then_inc(rstd_ready, 1)
                    if g == 0:
                        pool.tensor_tensor(xf[:, 1:NT], xf[:, 1:NT], b2[:].unsqueeze(1).to_broadcast([P, NT - 1, C]), ALU.add)\
                            .then_inc(b2_added, 1)
                pool.wait_ge(f_added, i * GROUPS + GROUPS)
                pool.tensor_tensor(veps[:, 0:1], rstd[:, 0:1], const["ones"][:], ALU.mult).then_inc(cleared, 1)

        @block.tensor
        def _(pe):
            pe.wait_ge(cleared, 1)
            with pe.Fori(0, LAYERS) as i:
                for tau in steps():
                    j = tau - LAG_S
                    if 0 <= j < NT:
                        pe.wait_ge(qk_scaled, i * NT + j + 1)
                        if j >= 1:
                            pe.wait_ge(qT_out, i * NT + j)
                        if j >= LAG_O - LAG_S + 1:
                            pe.wait_ge(y_added, i * NT + j - (LAG_O - LAG_S))
                        flat = qk[j % RQ][:].rearrange("p a (k b) e -> p (a k) (b e)", b=2)
                        for m in range(LH):
                            mm = nc.tensor.transpose(ps[:, B_QT + m // 4, m % 4 * P:(m % 4 + 1) * P], flat[:, m, :], const["ident"][:])
                        mm.then_inc(qkT_turned, 1)
                    j = tau
                    if 0 <= j < NT:
                        if j == 0:
                            pe.wait_ge(w_in, i * 64 + 64)
                        pe.wait_ge(xT_out, i * NT + j + 1)
                        if j > 0:
                            pe.wait_ge(raw_ready, i * NT + j)
                        ht = hT[:, j * P:(j + 1) * P]
                        nc.tensor.matmul(ps[:, B_Q, :], ht, wqkv[:, 0:INNER], start=True, stop=True)
                        nc.tensor.matmul(ps[:, B_K, :], ht, wqkv[:, INNER:2 * INNER], start=True, stop=True).then_inc(qk_ready, 1)
                    j = tau - LAG_O
                    if 0 <= j < NT:
                        pe.wait_ge(p_scaled, i * NT + j + 1)
                        if tau - 1 - LAG_S < NT:
                            pe.wait_ge(probs_ready, i * NT + tau - LAG_S)
                        for m in range(LH):
                            mm = nc.tensor.transpose(ps[:, B_S + m // 4, m % 4 * P:(m % 4 + 1) * P], probs[j % RP][:, m, :], const["ident"][:])
                        mm.then_inc(pT_turned, 1)
                    j = tau
                    if 0 <= j < NT:
                        ht = hT[:, j * P:(j + 1) * P]
                        if j > 0:
                            pe.wait_ge(v_out, i * NT + j)
                        nc.tensor.matmul(ps[:, B_V, :], ht, wqkv[:, 2 * INNER:3 * INNER], start=True, stop=True).then_inc(v_ready, 1)
                    j = tau - LAG_O
                    if 0 <= j < NT:
                        pe.wait_ge(pT_outA, i * NT + j + 1)
                        pe.wait_ge(pT_outB, i * NT + j + 1)
                        pe.wait_ge(v_shifted[j % RV], shifted(i, j))
                        if tau < NT:
                            pe.wait_ge(xT_out, i * NT + tau + 1)
                        for pr in range(LH // 2):
                            for w in range(2):
                                for a in range(2):
                                    head = 2 * pr + a
                                    mm = nc.tensor.matmul(ps[a * HD:(a + 1) * HD, B_X, pr * P + w * WIN:pr * P + (w + 1) * WIN],
                                                          (Vs, V)[w][j % RV][:, head * HD:(head + 1) * HD],
                                                          pT[j % 2][:, a * 4 + pr, w * WIN:(w + 1) * WIN], start=True, stop=True)
                        mm.then_inc(o_ready, 1)
                    j = tau - LAG_S
                    if 0 <= j < NT:
                        pe.wait_ge(qT_out, i * NT + j + 1)
                        if tau - LAG_O >= 0:
                            pe.wait_ge(pT_outA, i * NT + tau - LAG_O + 1)
                            pe.wait_ge(pT_outB, i * NT + tau - LAG_O + 1)
                        if j >= 1:
                            pe.wait_ge(probs_ready, i * NT + j)
                        for a in range(2):
                            nc.tensor.matmul(ps[:, B_S + a, :], const["identb"][:],
                                             mask[:, min(j, 1), :].unsqueeze(1).to_broadcast([P, 4, P]),
                                             start=True, stop=False, skip_group_check=True)
                        for head in range(LH):
                            r = slice(head % 2 * HD, (head % 2 + 1) * HD)
                            for w in range(2):
                                mm = nc.tensor.matmul(ps[w * WIN:(w + 1) * WIN, B_S + head % 2, head // 2 * P:(head // 2 + 1) * P],
                                                 qT[j % 2][r, head // 2, w * WIN:(w + 1) * WIN],
                                                 kT[j % 2][r, head // 2, w * WIN:w * WIN + P],
                                                 start=False, stop=True, skip_group_check=True)
                        mm.then_inc(s_ready, 1)
                    j = tau + 1
                    if 0 <= j < NT:
                        if j == 0:
                            pe.wait_ge(cleared, i + 1)
                        if tau - LAG_O >= 0:
                            pe.wait_ge(o_out, i * NT + tau - LAG_O + 1)
                        elif j > 0:
                            pe.wait_ge(xT_out, i * NT + j)
                        nc.tensor.transpose(ps[:, B_X, 0:P], xf[:, j, :], const["ident"][:]).then_inc(xT_turned, 1)
                    j = tau - LAG_O
                    if 0 <= j < NT:
                        pe.wait_ge(o_out, i * NT + j + 1)
                        for k in range(INNER // P):
                            mm = nc.tensor.matmul(ps[:, B_QT, 0:C], oT[j % 2][:, k, :], wo[:, k, :], start=(k == 0), stop=(k == INNER // P - 1))
                        mm.then_inc(y_ready, 1)
                for g in range(GROUPS + 1):
                    if g < GROUPS:
                        pe.wait_ge(hn_ready, i * NT + QG * g + QG)
                        if g >= 1:
                            pe.wait_ge(hnT_out, i * GROUPS + g)
                        for m in range(QG):
                            mm = nc.tensor.transpose(ps[:, 0, m * P:(m + 1) * P], hn[g % 2][:, m, :], const["ident"][:])
                        mm.then_inc(hnT_turned, 1)
                    if g >= 1:
                        gg = g - 1
                        if gg >= 1:
                            pe.wait_ge(f_added, i * GROUPS + gg)
                        for m in range(QG):
                            for n, (c, w) in enumerate(HCH):
                                if m == 0:
                                    pe.wait_ge(hh_ready, i * (GROUPS * NCH) + gg * NCH + n + 1)
                                mm = nc.tensor.matmul(ps[:, 1, m * P:(m + 1) * P], hh[gg % 2][n][0:w, m * P:(m + 1) * P], w2[0:w, n, :],
                                                      start=(n == 0), stop=(n == NCH - 1))
                        mm.then_inc(f_ready, 1)
                    if g < GROUPS:
                        pe.wait_ge(hnT_out, i * GROUPS + g + 1)
                        for n, (c, w) in enumerate(HCH):
                            u = g * NCH + n
                            for what, ready, freed in ((1, g_ready, g_out), (0, a_ready, hh_ready)):
                                if u >= 2:
                                    pe.wait_ge(freed, i * (GROUPS * NCH) + u - 1)
                                nc.tensor.matmul(ps[0:w, 2 + 2 * what + u % 2, :], w1[:, what * HID + c:what * HID + c + w], hnT[g % 2][:],
                                                 start=True, stop=True).then_inc(ready, 1)

        @block.scalar
        def _(act):
            act.wait_ge(cleared, 1)
            with act.Fori(0, LAYERS) as i:
                for tau in steps():
                    j = tau - LAG_S
                    if 0 <= j < NT:
                        act.wait_ge(qkT_turned, i * NT + j + 1)
                        if j > 0:
                            nc.scalar.activation(kT[j % 2][:, :, 0:WIN], kT[(j - 1) % 2][:, :, P:P + WIN], ACT.Copy)
                        else:
                            nc.scalar.activation(kT[0][:, :, 0:WIN], ps[:, B_KT, :].rearrange("p (k n) -> p k n", n=P)[:, :, 0:WIN], ACT.Copy)
                        nc.scalar.activation(qT[j % 2][:], ps[:, B_QT, :].rearrange("p (k n) -> p k n", n=P), ACT.Copy)
                        nc.scalar.activation(kT[j % 2][:, :, WIN:WIN + P], ps[:, B_KT, :].rearrange("p (k n) -> p k n", n=P), ACT.Copy)\
                            .then_inc(qT_out, 1)
                    j = tau - LAG_O
                    if 0 <= j < NT:
                        act.wait_ge(pT_turned, i * NT + j + 1)
                        nc.scalar.activation(pT[j % 2][:, 0:4, :], ps[:, B_S, :].rearrange("p (k n) -> p k n", n=P), ACT.Copy).then_inc(pT_outA, 1)
                    j = tau
                    if 0 <= j < NT:
                        act.wait_ge(qk_ready, i * NT + j + 1)
                        if j >= 2:
                            act.wait_ge(rot_ready, i * NT + j - 1)
                        nc.scalar.activation(raw[j % 2][:], ps[:, B_Q:B_K + 1, :].rearrange("p a (k e) -> p a k e", e=HD), ACT.Copy).then_inc(raw_ready, 1)
                    j = tau
                    if 0 <= j < NT:
                        act.wait_ge(raw_ready, i * NT + j + 1)
                        nc.scalar.activation(sq[j % 2][:], raw[j % 2][:], ACT.Square).then_inc(sq_ready, 1)
                    j = tau - LAG_O
                    if 0 <= j < NT:
                        act.wait_ge(o_ready, i * NT + j + 1)
                        nc.scalar.activation(oT[j % 2][:], ps[:, B_X, :].rearrange("p (k n) -> p k n", n=P), ACT.Copy).then_inc(o_out, 1)
                    j = tau + 1
                    if 0 <= j < NT:
                        act.wait_ge(xT_turned, i * NT + j + 1)
                        nc.scalar.activation(hT[0:C // 2, j * P:(j + 1) * P], ps[0:C // 2, B_X, 0:P], ACT.Copy)
                        nc.scalar.activation(hT[C // 2:C, j * P + 1:(j + 1) * P + 1], ps[C // 2:C, B_X, 0:P], ACT.Copy).then_inc(xT_out, 1)
                    j = tau - LAG_S
                    if 0 <= j < NT:
                        act.wait_ge(negm_ready, i * NT + j + 1)
                        for head in range(LH):
                            op = nc.scalar.activation(probs[j % RP][:, head, :], ps[:, B_S + head // 4, head % 4 * P:(head % 4 + 1) * P], ACT.Exp,
                                                      bias=negm[j % 2][:, head:head + 1], accum_out=sums[j % 2][:, head:head + 1])
                        op.then_inc(probs_ready, 1)
                act.wait_ge(f_in, i * F_IN + F_IN)
                for g in range(GROUPS):
                    act.wait_ge(hnT_turned, i * GROUPS + g + 1)
                    nc.scalar.activation(hnT[g % 2][:], ps[:, 0, :], ACT.Identity, bias=lnb[:], scale=lng[:]).then_inc(hnT_out, 1)
                    for n, (c, w) in enumerate(HCH):
                        u = g * NCH + n
                        act.wait_ge(g_ready, i * (GROUPS * NCH) + u + 1)
                        if u >= 2:
                            act.wait_ge(hh_ready, i * (GROUPS * NCH) + u - 1)
                        nc.scalar.activation(gl[u % 2][0:w, :], ps[0:w, 4 + u % 2, :], ACT.Gelu, bias=b1[0:w, 1, n:n + 1]).then_inc(g_out, 1)

        @block.vector
        def _(dve):
            half = HD // 2
            dve.wait_ge(cleared, 1)
            with dve.Fori(0, LAYERS) as i:
                dve.wait_ge(w_in, i * 64 + 64)
                for a in range(2):
                    w = qks[:, a, :].unsqueeze(1)
                    nc.vector.tensor_tensor(wtab[:, 2 * a], tab[:, 2 * a], w.to_broadcast([P, NT, HD]), ALU.mult).then_inc(tabled, 1)
                    nc.vector.tensor_tensor(wtab[:, 2 * a + 1, :, 0:half], tab[:, 2 * a + 1, :, 0:half],
                                            w[:, :, half:HD].to_broadcast([P, NT, half]), ALU.mult).then_inc(tabled, 1)
                    nc.vector.tensor_tensor(wtab[:, 2 * a + 1, :, half:HD], tab[:, 2 * a + 1, :, half:HD],
                                            w[:, :, 0:half].to_broadcast([P, NT, half]), ALU.mult).then_inc(tabled, 1)
                dve.wait_ge(tabled, i * 6 + 6)
                for tau in steps():
                    j = tau - 1
                    if 0 <= j < NT:
                        for ready in (cos_ready, sinA_ready, sinB_ready):
                            dve.wait_ge(ready, i * NT + j + 1)
                        nc.vector.tensor_tensor(qk[j % RQ][:], qk[j % RQ][:], sq[j % 2][:], ALU.add).then_inc(rot_ready, 1)
                        dve.wait_ge(rot_ready, i * NT + j + 1)
                        dve.wait_ge(rinv_ready, i * NT + j + 1)
                        nc.vector.tensor_tensor(qk[j % RQ][:].rearrange("p a k e -> p (a k) e"), qk[j % RQ][:].rearrange("p a k e -> p (a k) e"),
                                                rinv[j % 2][:].unsqueeze(2).to_broadcast([P, 2 * LH, HD]), ALU.mult).then_inc(qk_scaled, 1)
                    j = tau - LAG_S - 1
                    if 0 <= j < NT:
                        dve.wait_ge(probs_ready, i * NT + j + 1)
                        nc.vector.reciprocal(rsum[j % 2][:], sums[j % 2][:]).then_inc(rsum_ready, 1)
                    j = tau - LAG_O
                    if 0 <= j < NT:
                        dve.wait_ge(pT_turned, i * NT + j + 1)
                        nc.vector.tensor_copy(pT[j % 2][:, 4:8, :], ps[:, B_S + 1, :].rearrange("p (k n) -> p k n", n=P)).then_inc(pT_outB, 1)
                    j = tau
                    if 0 <= j < NT:
                        w = wtab[:, :, j, :].unsqueeze(2)
                        dve.wait_ge(raw_ready, i * NT + j + 1)
                        if j >= RQ:
                            dve.wait_ge(qkT_turned, i * NT + j - RQ + 1)
                        nc.vector.tensor_tensor(qk[j % RQ][:], raw[j % 2][:], w[:, 0:4:2].to_broadcast([P, 2, LH, HD]), ALU.mult).then_inc(cos_ready, 1)
                    j = tau
                    if 0 <= j < NT:
                        dve.wait_ge(sq_ready, i * NT + j + 1)
                        nc.vector.tensor_reduce(ss[j % 2][:].rearrange("p (a k) -> p a k", a=2), sq[j % 2][:], AX_X, ALU.add).then_inc(ss_ready, 1)
                        dve.wait_ge(v_ready, i * NT + j + 1)
                        if j >= RV:
                            dve.wait_ge(o_ready, i * NT + j - RV + 1)
                            dve.wait_ge(v_shifted[(j - RV + 1) % RV], shifted(i, j - RV + 1))
                        nc.vector.tensor_copy(V[j % RV][:], ps[:, B_V, :]).then_inc(v_out, 1)
                        dve.wait_ge(ss_ready, i * NT + j + 1)
                        nc.vector.tensor_scalar(ssc[j % 2][:], ss[j % 2][:], 1e-24, 0.0, ALU.max, ALU.add).then_inc(ssc_ready, 1)
                        nc.vector.tensor_tensor(sq[j % 2][:, :, :, 0:half], raw[j % 2][:, :, :, half:HD],
                                                w[:, 1:4:2, :, 0:half].to_broadcast([P, 2, LH, half]), ALU.mult).then_inc(sinA_ready, 1)
                    j = tau - LAG_S
                    if 0 <= j < NT:
                        dve.wait_ge(s_ready, i * NT + j + 1)
                        nc.vector.tensor_reduce(negm[j % 2][:], ps[:, B_S:B_S + 2, :].rearrange("p a (k n) -> p (a k) n", n=P), AX_X, ALU.max,
                                                negate=True).then_inc(negm_ready, 1)
                    j = tau - LAG_O
                    if 0 <= j < NT:
                        dve.wait_ge(y_ready, i * NT + j + 1)
                        nc.vector.tensor_tensor(xf[:, j, :], ps[:, B_QT, 0:C], xf[:, j, :], ALU.add).then_inc(y_added, 1)
                dve.wait_ge(h_copied, i + 1)
                dve.wait_ge(h_shifted, i * 32 + 32)
                for t in range(NT):
                    nc.vector.bn_stats(stats[:, t, :], h[:, t, :]).then_inc(stats_ready, 1)
                dve.wait_ge(stats_ready, i * NT + NT)
                dve.wait_ge(f_in, i * F_IN + F_IN)
                nc.vector.tensor_tensor(xf[:, 0], xf[:, 0], b2[:], ALU.add).then_inc(b2_added, 1)
                for t in range(NT):
                    nc.vector.bn_aggr(mv[:, t, :], stats[:, t, :]).then_inc(mv_ready, 1)

                def normed(g):
                    dve.wait_ge(rstd_ready, i * GROUPS + g + 1)
                    dve.wait_ge(mv_ready, i * NT + NT)
                    if g >= 2:
                        dve.wait_ge(hnT_turned, i * GROUPS + g - 1)
                    for m in range(QG):
                        t = QG * g + m
                        nc.vector.tensor_scalar(hn[g % 2][:, m, :], h[:, t, :], mv[:, t, 0:1], rstd[:, t:t + 1], ALU.subtract, ALU.mult)\
                            .then_inc(hn_ready, 1)

                normed(0)
                for g in range(GROUPS):
                    if g + 1 < GROUPS:
                        normed(g + 1)
                    for n, (c, w) in enumerate(HCH):
                        u = g * NCH + n
                        dve.wait_ge(a_ready, i * (GROUPS * NCH) + u + 1)
                        dve.wait_ge(g_out, i * (GROUPS * NCH) + u + 1)
                        if g >= 2:
                            dve.wait_ge(f_ready, i * GROUPS + g - 1)
                        nc.vector.scalar_tensor_tensor(out=hh[g % 2][n][0:w, :], in0=ps[0:w, 2 + u % 2, :], scalar=b1[0:w, 0, n:n + 1],
                                                       in1=gl[u % 2][0:w, :], op0=ALU.add, op1=ALU.mult).then_inc(hh_ready, 1)
                    dve.wait_ge(f_ready, i * GROUPS + g + 1)
                    dve.wait_ge(b2_added, i * 2 + 2)
                    rows_ = xf[:, QG * g:QG * g + QG, :]
                    nc.vector.tensor_tensor(rows_, ps[:, 1, :].rearrange("p (t c) -> p t c", c=C), rows_, ALU.add).then_inc(f_added, 1)


def shared_weights_stage(nc, ps, stage, x, xnT, bo, wkd, bkd, wv, bv, bq, bqs, WqT, WoD, k_hh, k_lm, V):
    with ExitStack() as ctx:
        sem = Sems(nc, ctx, stage)
        kf = [ctx.enter_context(nc.sbuf_tensor(f"{stage}_kf{n}", [P, 512], F32)) for n in range(2)]
        padded, k_ready, kf_ready, hi_ready, k_done = (sem(n) for n in ("padded", "k_ready", "kf_ready", "hi_ready", "k_done"))
        v_ready, v_done, scaled = sem("v_ready"), sem("v_done"), sem("scaled")
        block = ctx.enter_context(nc.Block())

        @block.tensor
        def _(pe):
            for f in range(4):
                nc.tensor.matmul(ps[:, f, :], wkd[:].rearrange("p a e -> p (a e)"), xnT[:, f * 512:(f + 1) * 512],
                                 start=True, stop=True).then_inc(k_ready, 1)
            for t in range(NT):
                mm = nc.tensor.matmul(ps[:, 4 + t // 8, t % 8 * HD:(t % 8 + 1) * HD], xnT[:, t * P:(t + 1) * P], wv[:],
                                      start=True, stop=True)
                if t % 8 == 7:
                    mm.then_inc(v_ready, 1)

        @block.scalar
        def _(act):
            nc.scalar.activation(bqs[:, 0:HEADS], bq[:], ACT.Copy, scale=HD ** -0.5).then_inc(scaled, 1)
            for f in range(4):
                act.wait_ge(k_ready, f + 1)
                if f >= 2:
                    act.wait_ge(k_done, f - 1)
                nc.scalar.activation(kf[f % 2][:], ps[:, f, :], ACT.Identity, bias=bkd[:]).then_inc(kf_ready, 1)
            act.wait_ge(scaled, 1)

        @block.vector
        def _(dve):
            for f in range(4):
                cols = slice(f * 512, (f + 1) * 512)
                dve.wait_ge(kf_ready, f + 1)
                nc.vector.tensor_copy(k_hh[:, cols], kf[f % 2][:]).then_inc(hi_ready, 1)
                dve.wait_ge(hi_ready, f + 1)
                nc.vector.tensor_tensor(k_lm[0:HD, cols], kf[f % 2][0:HD], k_hh[0:HD, cols], ALU.subtract).then_inc(k_done, 1)
            for n in range(2):
                dve.wait_ge(v_ready, n + 1)
                nc.vector.tensor_tensor(V[:, 8 * n:8 * n + 8, :], ps[:, 4 + n, :].rearrange("p (t e) -> p t e", e=HD),
                                        bv[:].unsqueeze(1).to_broadcast([P, 8, HD]), ALU.add).then_inc(v_done, 1)
            dve.wait_ge(v_done, 2)
            dve.wait_ge(k_done, 4)

        @block.gpsimd
        def _(pool):
            fillings = [(WqT[:, HEADS, :], 0.0), (WoD[:, 0, :], 0.0), (bqs[:, HEADS, :], 0.0),
                        (k_lm[HD:P, :], 0.0), (k_lm[HD:HD + 2, :], M_UNIT)]
            for n, (part, value) in enumerate(fillings):
                pool.memset(part, value).then_inc(padded, 1)
                pool.wait_ge(padded, n + 1)
            pool.tensor_tensor(x[:], x[:], bo[:].unsqueeze(1).to_broadcast([P, NT, C]), ALU.add).then_inc(padded, 1)
            pool.wait_ge(padded, len(fillings) + 1)


def add_stage(nc, stage, x, y):
    with ExitStack() as ctx:
        added = Sems(nc, ctx, stage)("added")
        block = ctx.enter_context(nc.Block())

        @block.vector
        def _(dve):
            nc.vector.tensor_tensor(x[:, 0:10], x[:, 0:10], y[:, 0:10], ALU.add).then_inc(added, 1)
            dve.wait_ge(added, 2)

        @block.gpsimd
        def _(pool):
            pool.tensor_tensor(x[:, 10:NT], x[:, 10:NT], y[:, 10:NT], ALU.add).then_inc(added, 1)
            pool.wait_ge(added, 2)


EXPERTS = 8
FF = 512
FCH = FF // P
W_UNIT = 64.0


def experts_stage(nc, stage, ps, x, xnT, const, ins, out):
    HB = QG * P
    with ExitStack() as ctx:
        sem = Sems(nc, ctx, stage)

        def sb(name, shape, dt):
            return ctx.enter_context(nc.sbuf_tensor(f"{stage}_{name}", shape, dt))

        w1 = [sb(f"w1_{n}", [C, FF], F32) for n in range(2)]
        w2 = [sb(f"w2_{n}", [P, FCH, C], F32) for n in range(2)]
        w1_hl = [[sb(f"w1_{a}{n}", [C, FF], F16) for a in "hl"] for n in range(2)]
        w2_hl = [[sb(f"w2_{a}{n}", [P, FCH, C], F16) for a in "hl"] for n in range(2)]
        x_hl = [sb(f"x_{a}", [C, T], F16) for a in "hl"]
        unit = sb("unit", [P, 1], F32)
        b1 = [sb(f"b1_{n}", [P, FCH], F32) for n in range(2)]
        b2 = sb("b2", [EXPERTS, C], F32)
        rw = sb("rw", [C, EXPERTS], F32)
        rb = sb("rb", [P, EXPERTS], F32)
        logits = sb("logits", [P, NT, EXPERTS], F32)
        top = sb("top", [P, NT, 8], F32)
        topi = sb("topi", [P, NT, 8], U32)
        topf = sb("topf", [P, NT, 2], F32)
        gap = sb("gap", [P, NT], F32)
        egap = sb("egap", [P, NT], F32)
        esum = sb("esum", [P, NT], F32)
        g12 = sb("g12", [P, NT, 2], F32)
        iota = sb("iota", [P, EXPERTS], F32)
        hot = [sb(f"hot{n}", [P, NT, EXPERTS], F32) for n in range(2)]
        gates = sb("gates", [P, NT, EXPERTS], F32)
        gates_u = sb("gates_u", [P, NT, EXPERTS], F32)
        gT = sb("gT", [EXPERTS, NT, P], F32)
        hf = [sb(f"hf{n}", [P, HB], F32) for n in range(4)]
        hh = [[[sb(f"h{a}{n}_{c}", [P, HB], F16) for a in "hl"] for c in range(FCH)] for n in range(2)]

        r_in, w_in = sem("r_in"), [sem(f"w_in{n}") for n in range(2)]
        l_ready, l_done, top_ready, topi_ready = sem("l_ready"), sem("l_done"), sem("top_ready"), sem("topi_ready")
        topf_ready, gap_ready, egap_ready, esum_ready = sem("topf_ready"), sem("gap_ready"), sem("egap_ready"), sem("esum_ready")
        g12_ready, hot_ready, hot_weighted, gates_ready = sem("g12_ready"), sem("hot_ready"), sem("hot_weighted"), sem("gates_ready")
        iota_ready, gT_turned, gT_out, b_ready, b_added = (sem(n) for n in ("iota_ready", "gT_turned", "gT_out", "b_ready", "b_added"))
        h_ready = sem("h_ready")
        h_out = sem("h_out")
        h_low = sem("h_low")
        x_hi, x_split, unit_ready, gates_u_ready = sem("x_hi"), sem("x_split"), sem("unit_ready"), sem("gates_u_ready")
        w_scaled, w_hi, w_split = sem("w_scaled"), sem("w_hi"), sem("w_split")
        y_ready = sem("y_ready")
        y_added = sem("y_added")
        stored = sem("stored")
        NH = GROUPS * FCH
        HBANKS, YBANKS = 4, 4

        block = ctx.enter_context(nc.Block())

        @block.sync
        def _(sp):
            sp.dma_start(rw[:], ins["L1_ffn_router_w"]).then_inc(r_in, 16)
            sp.dma_start(rb[:], ins["L1_ffn_router_b"].partition_broadcast(P)).then_inc(r_in, 16)
            sp.dma_start(b2[:], ins["L1_ffn_b2"]).then_inc(r_in, 16)

            def load(i, n):
                sp.dma_start(w1[n][:], ins["L1_ffn_w1"][bass.ds(i * 2 + n, 1)].rearrange("a p n -> (a p) n")).then_inc(w_in[n], 16)
                sp.dma_start(w2[n][:], ins["L1_ffn_w2"][bass.ds(i * 2 + n, 1)].rearrange("a (k p) n -> p (a k) n", p=P)).then_inc(w_in[n], 16)
                with nc.allow_non_contiguous_dma(reason="a bias, 2 KB"):
                    sp.dma_start(b1[n][:], ins["L1_ffn_b1"][bass.ds(i * 2 + n, 1)].rearrange("a (k p) -> p (a k)", p=P)).then_inc(w_in[n], 16)

            load(0, 0)
            load(0, 1)
            with sp.Fori(0, EXPERTS // 2 - 1) as i:
                for n in range(2):
                    sp.wait_ge(h_out, i * (2 * NH) + ((n + 1) * NH + HBANKS))
                    load(i + 1, n)
            for g in range(GROUPS):
                sp.wait_ge(y_added, (EXPERTS - 1) * GROUPS + g + 1 + YBANKS)
                sp.dma_start(out[0, g * HB:(g + 1) * HB, :].rearrange("(t p) c -> p t c", p=P), x[:, QG * g:QG * g + QG, :]).then_inc(stored, 16)
            sp.wait_ge(stored, 16 * GROUPS)

        @block.tensor
        def _(pe):
            pe.wait_ge(r_in, 48)
            for t in range(NT):
                mm = nc.tensor.matmul(ps[:, 0, t * EXPERTS:(t + 1) * EXPERTS], xnT[:, t * P:(t + 1) * P], rw[:], start=True, stop=True)
            mm.then_inc(l_ready, 1)
            pe.wait_ge(gates_ready, 1)
            for g in range(GROUPS):
                for m in range(QG):
                    mm = nc.tensor.transpose(ps[0:EXPERTS, 4 + g, m * P:(m + 1) * P], gates[:, QG * g + m, :], const["ident"][:])
                mm.then_inc(gT_turned, 1)
            for g in range(GROUPS):
                pe.wait_ge(gT_out, g + 1)
                for m in range(QG):
                    mm = nc.tensor.matmul(ps[:, 4 + g, m * P:(m + 1) * P], gT[:, QG * g + m, :], b2[:], start=True, stop=True)
                mm.then_inc(b_ready, 1)

            def hidden(i, n, g):
                for c in range(FCH):
                    u = n * NH + g * FCH + c
                    pe.wait_ge(h_out, i * (2 * NH) + (u + 1))
                    cols, tokens = slice(c * P, (c + 1) * P), slice(g * HB, (g + 1) * HB)
                    (w_h, w_l), (x_h, x_l) = w1_hl[n], x_hl
                    nc.tensor.matmul(ps[:, c, :], w_h[:, cols], x_h[:, tokens], start=True, stop=False)
                    nc.tensor.matmul(ps[:, c, :], w_h[:, cols], x_l[:, tokens], start=False, stop=False)
                    nc.tensor.matmul(ps[:, c, :], w_l[:, cols], x_h[:, tokens], start=False, stop=True).then_inc(h_ready, 1)

            def output(i, n, g):
                u = n * GROUPS + g
                pe.wait_ge(y_added, i * (2 * GROUPS) + (u + 1))
                pe.wait_ge(h_low, i * (2 * NH) + ((u + 1) * FCH + HBANKS))
                for m in range(QG):
                    for c in range(FCH):
                        out_ = ps[:, 4 + g, m * P:(m + 1) * P]
                        (h_h, h_l), (w_h, w_l), cols = hh[g % 2][c], w2_hl[n], slice(m * P, (m + 1) * P)
                        nc.tensor.matmul(out_, h_h[:, cols], w_h[:, c, :], start=(c == 0), stop=False)
                        nc.tensor.matmul(out_, h_h[:, cols], w_l[:, c, :], start=False, stop=False)
                        mm = nc.tensor.matmul(out_, h_l[:, cols], w_h[:, c, :], start=False, stop=(c == FCH - 1))
                mm.then_inc(y_ready, 1)

            pe.wait_ge(x_split, 4)
            with pe.Fori(0, EXPERTS // 2) as i:
                pe.wait_ge(w_split, i * 4 + 2)
                hidden(i, 0, 0)
                for n in range(2):
                    for g in range(GROUPS):
                        if g + 1 < GROUPS:
                            hidden(i, n, g + 1)
                        elif n == 0:
                            pe.wait_ge(w_split, i * 4 + 4)
                            hidden(i, 1, 0)
                        output(i, n, g)

        @block.scalar
        def _(act):
            for g in range(GROUPS):
                cols = slice(g * HB, (g + 1) * HB)
                nc.scalar.activation(x_hl[0][:, cols], xnT[:, cols], ACT.Copy).then_inc(x_hi, 1)
            act.wait_ge(gap_ready, 1)
            nc.scalar.activation(egap[:], gap[:], ACT.Exp).then_inc(egap_ready, 1)
            for g in range(GROUPS):
                act.wait_ge(gT_turned, g + 1)
                nc.scalar.activation(gT[:, QG * g:QG * g + QG, :], ps[0:EXPERTS, 4 + g, :].rearrange("p (t n) -> p t n", n=P), ACT.Copy)\
                    .then_inc(gT_out, 1)
            for n in range(HBANKS):
                nc.scalar.activation(hf[n][:, 0:1], egap[:, n:n + 1], ACT.Copy).then_inc(h_out, 1)
            act.wait_ge(h_out, HBANKS)
            with act.Fori(0, EXPERTS // 2) as i:
                for n in range(2):
                    act.wait_ge(w_in[n], i * 48 + 48)
                    for g in range(GROUPS):
                        for c in range(FCH):
                            u = n * NH + g * FCH + c
                            act.wait_ge(h_ready, i * (2 * NH) + (u + 1))
                            act.wait_ge(h_low, i * (2 * NH) + (u + 1))
                            nc.scalar.activation(hf[c][:], ps[:, c, :], ACT.Gelu, bias=b1[n][:, c:c + 1], scale=1 / W_UNIT)
                            nc.scalar.activation(hh[g % 2][c][0][:], ps[:, c, :], ACT.Gelu, bias=b1[n][:, c:c + 1], scale=1 / W_UNIT)\
                                .then_inc(h_out, 1)

        @block.vector
        def _(dve):
            dve.wait_ge(l_ready, 1)
            dve.wait_ge(r_in, 48)
            nc.vector.tensor_tensor(logits[:], ps[:, 0, 0:NT * EXPERTS].rearrange("p (t e) -> p t e", e=EXPERTS),
                                    rb[:].unsqueeze(1).to_broadcast([P, NT, EXPERTS]), ALU.add).then_inc(l_done, 1)
            dve.wait_ge(l_done, 1)
            for t in range(NT):
                nc.vector.max(top[:, t, :], logits[:, t, :]).then_inc(top_ready, 1)
            for t in range(NT):
                dve.wait_ge(top_ready, t + 1)
                nc.vector.max_index(topi[:, t, :], top[:, t, :], logits[:, t, :]).then_inc(topi_ready, 1)
            dve.wait_ge(topi_ready, NT)
            nc.vector.tensor_copy(topf[:], topi[:, :, 0:2]).then_inc(topf_ready, 1)
            dve.wait_ge(top_ready, NT)
            nc.vector.tensor_tensor(gap[:], top[:, :, 1], top[:, :, 0], ALU.subtract).then_inc(gap_ready, 1)
            dve.wait_ge(egap_ready, 1)
            nc.vector.tensor_scalar(esum[:], egap[:], 1.0, 0.0, ALU.add, ALU.add).then_inc(esum_ready, 1)
            dve.wait_ge(esum_ready, 1)
            nc.vector.reciprocal(g12[:, :, 0], esum[:]).then_inc(g12_ready, 1)
            dve.wait_ge(g12_ready, 1)
            nc.vector.tensor_tensor(g12[:, :, 1], g12[:, :, 0], egap[:], ALU.mult).then_inc(g12_ready, 1)
            dve.wait_ge(topf_ready, 1)
            dve.wait_ge(iota_ready, EXPERTS)
            for n in range(2):
                nc.vector.tensor_tensor(hot[n][:], topf[:, :, n:n + 1].to_broadcast([P, NT, EXPERTS]),
                                        iota[:].unsqueeze(1).to_broadcast([P, NT, EXPERTS]), ALU.is_equal).then_inc(hot_ready, 1)
            dve.wait_ge(g12_ready, 2)
            for n in range(2):
                dve.wait_ge(hot_ready, n + 1)
                nc.vector.tensor_tensor(hot[n][:], hot[n][:], g12[:, :, n:n + 1].to_broadcast([P, NT, EXPERTS]), ALU.mult).then_inc(hot_weighted, 1)
            dve.wait_ge(hot_weighted, 2)
            nc.vector.tensor_tensor(gates[:], hot[0][:], hot[1][:], ALU.add).then_inc(gates_ready, 1)
            dve.wait_ge(gates_ready, 1)
            nc.vector.tensor_scalar(gates_u[:], gates[:], 1 / W_UNIT, 0.0, ALU.mult, ALU.add).then_inc(gates_u_ready, 1)
            for g in range(GROUPS):
                dve.wait_ge(b_ready, g + 1)
                rows = x[:, QG * g:QG * g + QG, :]
                nc.vector.tensor_tensor(rows, ps[:, 4 + g, :].rearrange("p (t c) -> p t c", c=C), rows, ALU.add).then_inc(y_added, 1)
            dve.wait_ge(y_added, GROUPS)
            dve.wait_ge(gates_u_ready, 1)
            for n in range(HBANKS):
                nc.vector.memset(hot[0][:, n, 0:1], 0.0).then_inc(h_low, 1)

            def low(i, n, g):
                for c in range(FCH):
                    u = n * NH + g * FCH + c
                    dve.wait_ge(h_out, i * (2 * NH) + (u + 1 + HBANKS))
                    h_h, h_l = hh[g % 2][c]
                    nc.vector.tensor_tensor(h_l[:], hf[c][:], h_h[:], ALU.subtract).then_inc(h_low, 1)

            def add(i, n, g):
                u = n * GROUPS + g
                dve.wait_ge(y_ready, i * (2 * GROUPS) + (u + 1))
                dve.wait_ge(y_added, i * (2 * GROUPS) + (u + 1))
                for m in range(QG):
                    t = QG * g + m
                    op = nc.vector.scalar_tensor_tensor(out=x[:, t, :], in0=ps[:, 4 + g, m * P:(m + 1) * P],
                                                        scalar=gates_u[:, t, bass.ds(i * 2 + n, 1)],
                                                        in1=x[:, t, :], op0=ALU.mult, op1=ALU.add)
                op.then_inc(y_added, 1)

            with dve.Fori(0, EXPERTS // 2) as i:
                low(i, 0, 0)
                for n in range(2):
                    for g in range(GROUPS):
                        if g + 1 < GROUPS:
                            low(i, n, g + 1)
                        elif n == 0:
                            low(i, 1, 0)
                        add(i, n, g)

        @block.gpsimd
        def _(pool):
            for e in range(EXPERTS):
                pool.memset(iota[:, e:e + 1], float(e)).then_inc(iota_ready, 1)
            pool.wait_ge(iota_ready, EXPERTS)
            pool.memset(unit[:], W_UNIT).then_inc(unit_ready, 1)
            for g in range(GROUPS):
                cols = slice(g * HB, (g + 1) * HB)
                pool.wait_ge(x_hi, g + 1)
                pool.tensor_tensor(x_hl[1][:, cols], xnT[:, cols], x_hl[0][:, cols], ALU.subtract).then_inc(x_split, 1)
            pool.wait_ge(unit_ready, 1)

            def split(i, n):
                pool.wait_ge(w_in[n], i * 48 + 48)
                for f, (w, (w_h, w_l)) in enumerate(((w1[n][:], w1_hl[n]), (w2[n][:].rearrange("p k c -> p (k c)"), w2_hl[n]))):
                    if f == 1:
                        w_h, w_l = (t[:].rearrange("p k c -> p (k c)") for t in (w_h, w_l))
                    else:
                        w_h, w_l = w_h[:], w_l[:]
                    pool.tensor_tensor(w, w, unit[:].to_broadcast([P, FF]), ALU.mult).then_inc(w_scaled, 1)
                    pool.wait_ge(w_scaled, i * 4 + (2 * n + f + 1))
                    pool.tensor_tensor(w_h, w, const["ones"][:].to_broadcast([P, FF]), ALU.mult).then_inc(w_hi, 1)
                    pool.wait_ge(w_hi, i * 4 + (2 * n + f + 1))
                    pool.tensor_tensor(w_l, w, w_h, ALU.subtract).then_inc(w_split, 1)

            split(0, 0)
            split(0, 1)
            with pool.Fori(0, EXPERTS // 2 - 1) as i:
                for n in range(2):
                    pool.wait_ge(y_ready, i * (2 * GROUPS) + (n + 1) * GROUPS)
                    split(i + 1, n)


def build(nc, ins, out):
    with ExitStack() as ctx:
        def sb(name, shape, dt, c=ctx):
            return c.enter_context(nc.sbuf_tensor(name, shape, dt))

        ps = ctx.enter_context(nc.psum_tensor("ps", [P, 8, 512], F32))
        x = sb("x", [P, NT, C], F32)
        const = {"ident": sb("ident", [P, P], F32), "identb": sb("identb", [P, P], BF16),
                 "ident16": sb("ident16", [P, P], F16), "mask": sb("mask", [P, P], BF16),
                 "minus_half": sb("minus_half", [P, 1], F32), "ones": sb("ones", [P, 1], F32),
                 "eps": sb("eps", [P, 1], F32), "mask_all": sb("mask_all", [P, P], BF16)}
        ident = const["ident"]

        with ExitStack() as layers:
            WqT = sb("WqT", [C, HEADS + 1, HD], F32, layers)
            WoD1 = sb("WoD1", [P, 1 + HEADS, C], F32, layers)
            wkd = sb("wkd", [C, 2, HD], F32, layers)
            wv = sb("wv", [C, HD], F32, layers)
            bkd = sb("bkd", [P, 1], F32, layers)
            bv = sb("bv", [P, HD], F32, layers)
            bq = sb("bq", [P, HEADS, 1], F32, layers)
            bo = sb("bo", [P, C], F32, layers)
            loads1 = [(WqT[:, 0:HEADS, :], ins["L1_attn_Wq"].rearrange("c (h e) -> c h e", e=HD)),
                      (wv[:], ins["L1_attn_Wv"]), (bv[:], ins["L1_attn_bv"].partition_broadcast(P)),
                      (bo[:], ins["L1_attn_bo"].partition_broadcast(P))]
            for a in range(2):
                rows = slice(a * HD, (a + 1) * HD)
                loads1 += [(wkd[:, a, :], ins["L1_attn_Wk"]),
                           (WoD1[rows, 1:, :], ins["L1_attn_Wo"].rearrange("(h e) c -> e h c", e=HD)),
                           (bkd[rows, :], ins["L1_attn_bk"].unsqueeze(1)),
                           (bq[rows, :, 0], ins["L1_attn_bq"].rearrange("(h e) -> e h", e=HD))]

            with ExitStack() as layer0:
                xpos = sb("xpos", [P, 4, NT, HD], F32, layer0)

                with ExitStack() as c0:
                    WT = sb("WT", [P, 3, HEADS + 1, HD], F32, c0)
                    WoD = sb("WoD0", [P, 1 + HEADS, C], F32, c0)
                    cosw = sb("cosw", [P, 2, NT, HD], F32, c0)
                    sinw = sb("sinw", [P, 2, NT, HD], F32, c0)
                    xnT = sb("xnT0", [C, T], F32, c0)
                    with ExitStack() as c1:
                        wqkv = sb("wqkv", [P, 3 * HEADS * HD // P, C], F32, c1)
                        wo2 = sb("wo2", [C, HEADS, 2, HD], F32, c1)
                        tabs = sb("tabs", [P, 2, NT, HD], F32, c1)
                        normw = sb("normw", [P, 2, HD], F32, c1)
                        xn = sb("xn0", [P, NT, C], F32, c1)
                        wo_in = ins["L0_attn_wo"].rearrange("c (h e) -> c h e", e=HD)
                        load_stage(nc, ps, "load0", const, x, ins["L0_attn_x"], [])
                        layernorm_stage(nc, ps, x, xn, xnT, ident, "ln0", loads=[
                            (wqkv[:], ins["L0_attn_wqkv"].rearrange("(n p) c -> p n c", p=P)),
                            (wo2[:, :, 0, :], wo_in), (wo2[:, :, 1, :], wo_in),
                            (tabs[:], ins["rope_tab"].rearrange("a (t p) e -> p a t e", p=P)),
                            (normw[:, 0, :], ins["L0_attn_q_norm_w"].partition_broadcast(P)),
                            (normw[:, 1, :], ins["L0_attn_k_norm_w"].partition_broadcast(P))])
                        causal_weights_stage(nc, ps, "cw", const, wqkv, wo2, tabs, normw, WT, WoD, cosw, sinw)
                    attention_stage(nc, HeadPlan(True), "at0", ps, x, xnT, const,
                                    {"WT": WT, "WoD": WoD, "cosw": cosw, "sinw": sinw},
                                    loads=[(xpos[:], ins["xpos_tab"].rearrange("a (t p) e -> p a t e", p=P))])

                with ExitStack() as c0:
                    xf = sb("xf", [P, NT, C], F32, c0)
                    with ExitStack() as c1:
                        xnT = sb("xnT1", [C, T], F32, c1)
                        layernorm_stage(nc, ps, x, xf, xnT, ident, "ln1")
                    local_stage(nc, "loc", ps, xf, const, ins, {"xpos": xpos}, loads=loads1)
                    add_stage(nc, "add", x, xf)

            with ExitStack() as c0:
                bqs = sb("bqs", [P, HEADS + 1, 1], F32, c0)
                k_hh, k_lm = sb("k_hh", [P, T], F16, c0), sb("k_lm", [P, T], F16, c0)
                V = sb("V", [P, NT, HD], F32, c0)
                xnT = sb("xnT2", [C, T], F32, c0)
                with ExitStack() as c1:
                    xn = sb("xn2", [P, NT, C], F32, c1)
                    layernorm_stage(nc, ps, x, xn, xnT, ident, "ln2")
                shared_weights_stage(nc, ps, "kv", x, xnT, bo, wkd, bkd, wv, bv, bq, bqs, WqT, WoD1, k_hh, k_lm, V)
                attention_stage(nc, HeadPlan(False), "at1", ps, x, xnT, const,
                                {"WT": WqT, "WoD": WoD1, "bq": bqs, "k_hh": k_hh, "k_lm": k_lm, "V": V})

        with ExitStack() as c0:
            xnT = sb("xnT3", [C, T], F32, c0)
            with ExitStack() as c1:
                xn = sb("xn3", [P, NT, C], F32, c1)
                layernorm_stage(nc, ps, x, xn, xnT, ident, "ln3")
            experts_stage(nc, "moe", ps, x, xnT, const, ins, out)


def rope_table():
    f32 = np.float32
    inv = (f32(1.0) / np.power(f32(10000.0), np.arange(0, HD, 2, dtype=f32) / f32(HD))).astype(f32)
    angle = (np.arange(T, dtype=f32)[:, None] * inv).astype(f32)
    cos, sin = np.cos(angle).astype(f32), np.sin(angle).astype(f32)
    return np.stack([np.concatenate([cos, cos], 1), np.concatenate([-sin, sin], 1)])


def xpos_table():
    f32 = np.float32
    t = np.arange(T, dtype=f32)
    idx = np.arange(0, HD, 2, dtype=f32)
    inv = (f32(1.0) / np.power(f32(10000.0), idx / f32(HD))).astype(f32)
    angle = (t[:, None] * inv[None]).astype(f32)
    angle = np.concatenate([angle, angle], -1)
    base = ((idx + f32(0.4 * HD)) / f32(1.4 * HD)).astype(f32)
    power = ((t - T // 2) / f32(WIN // 2)).astype(f32)
    scale = np.power(base[None], power[:, None]).astype(f32)
    scale = np.concatenate([scale, scale], -1)
    cos, sin = np.cos(angle).astype(f32), np.sin(angle).astype(f32)
    sin[:, :HD // 2] *= -1
    return np.stack([cos * scale * f32(8), sin * scale * f32(8), cos / scale, sin / scale]).astype(f32)


INPUTS = (
    "L0_attn_x", "L0_attn_wqkv", "L0_attn_wo", "L0_attn_q_norm_w", "L0_attn_k_norm_w",
    "L0_ffn_wqkv", "L0_ffn_q_scale", "L0_ffn_k_scale", "L0_ffn_wo", "L0_ffn_ln_g", "L0_ffn_ln_b",
    "L0_ffn_w1", "L0_ffn_b1", "L0_ffn_w2", "L0_ffn_b2",
    "L1_attn_Wq", "L1_attn_bq", "L1_attn_Wk", "L1_attn_bk", "L1_attn_Wv", "L1_attn_bv", "L1_attn_Wo", "L1_attn_bo",
    "L1_ffn_router_w", "L1_ffn_router_b", "L1_ffn_w1", "L1_ffn_b1", "L1_ffn_w2", "L1_ffn_b2")


def kernel(**inputs):
    import concourse.bacc as bacc
    from concourse.bass_utils import run_bass_kernel_spmd

    arrays = {name: np.ascontiguousarray(inputs[name]) for name in INPUTS}
    arrays["rope_tab"] = rope_table()
    arrays["xpos_tab"] = xpos_table()
    nc = bacc.Bacc("TRN2", target_bir_lowering=False, num_devices=1)
    ins = {name: nc.dram_tensor(name, a.shape, mybir.dt.from_np(a.dtype), kind="ExternalInput").ap()
           for name, a in arrays.items()}
    out = nc.dram_tensor("out", (1, T, C), F32, kind="ExternalOutput").ap()
    build(nc, ins, out)
    result = run_bass_kernel_spmd(nc, [arrays], core_ids=[0])
    return result.results[0]["out"]
```
